# Optimizing a Trainium2 kernel written in Bass

```python
import numpy as np
import jax
import jax.numpy as jnp

def _softmax(x, axis=-1):
    return jax.nn.softmax(x, axis=axis)

def _gelu(x):
    return jax.nn.gelu(x, approximate=True)

def _silu(x):
    return jax.nn.silu(x)

def _sigmoid(x):
    return jax.nn.sigmoid(x)

def _layernorm(x, axis=-1, eps=1e-05):
    m = jnp.mean(x, axis=axis, keepdims=True)
    v = jnp.var(x, axis=axis, keepdims=True)
    return (x - m) / jnp.sqrt(v + eps)

def _scatter_add(tgt, idx, src, axis=0):
    return tgt.at[idx].add(src)

def _segment_sum(src, seg, n):
    return jax.ops.segment_sum(src, seg, n)
kernel_name = 'mk_xattn_ffn_d4_seqx_r8_8d4ef2'

def setup_inputs(seed: int=0):
    np.random.seed(seed)
    _w = jnp.asarray

    def _rec_inputs():
        import jax
        import jax.numpy as jnp
        _rk = jax.random.key(seed)
        x = -0.0003929 + 0.9999 * jax.random.normal(jax.random.fold_in(_rk, 1), (8, 256, 128), jnp.float32)
        _lenS = 256 - jax.random.randint(jax.random.fold_in(_rk, 7), (8,), 0, max(1, 256 // 4) + 1, jnp.int32)
        _lenS2 = 256 - jax.random.randint(jax.random.fold_in(_rk, 8), (8,), 0, max(1, 256 // 4) + 1, jnp.int32)
        _ctx_1024P = jax.random.normal(jax.random.fold_in(_rk, 11), (8, 16, 128), jnp.float32)
        _ctx_1024c = jax.random.dirichlet(jax.random.fold_in(_rk, 511), 0.3 * jnp.ones((16,), jnp.float32), (8, 256))
        _ctx_1024t = jnp.einsum('bsk,bkd->bsd', _ctx_1024c, _ctx_1024P)
        _ctx_1024t = _ctx_1024t * jax.lax.rsqrt(jnp.mean(jnp.square(_ctx_1024t)) + 1e-12) * 0.953939
        ctx_1024 = 2.81802e-05 + 1.00001 * (_ctx_1024t + 0.3 * jax.random.normal(jax.random.fold_in(_rk, 611), (8, 256, 128), jnp.float32))
        _validS = jnp.arange(256)[None, :] < _lenS[:, None]
        _validS2 = jnp.arange(256)[None, :] < _lenS2[:, None]
        _causal = jnp.tril(jnp.ones((256, 256), dtype=bool))
        mask_BxS2_bf1 = jnp.ones((8, 256), dtype=bool)
        return (x, ctx_1024, _lenS2, mask_BxS2_bf1)
    x, ctx_1024, _lenS2, mask_BxS2_bf1 = _rec_inputs()

    def _L0_xattn_setup():
        import jax, jax.numpy as jnp
        import numpy as np
        import math
        D_MODEL = 128
        N_HEADS = 16
        C = 1
        B, L = (8, 256)

        def _glorot(key, fan):
            lim = np.sqrt(6.0 / (fan + fan)).astype(np.float32)
            return jax.random.uniform(key, (fan, fan), jnp.float32, -lim, lim)
        key = jax.random.key(seed)
        ks = jax.random.split(key, 7)
        queries = jax.random.normal(ks[0], (B, L, D_MODEL), jnp.float32)
        keys = jax.random.normal(ks[1], (B, L, D_MODEL), jnp.float32)
        values = jax.random.normal(ks[2], (B, L, D_MODEL), jnp.float32)
        wq = _glorot(ks[3], D_MODEL)
        wk = _glorot(ks[4], D_MODEL)
        wv = _glorot(ks[5], D_MODEL)
        wo = _glorot(ks[6], D_MODEL)
        return {'queries': queries, 'keys': keys, 'values': values, 'wq': wq, 'wk': wk, 'wv': wv, 'wo': wo}
    _L0_xattn_all = _L0_xattn_setup()
    _L0_xattn_in = {k: v for k, v in _L0_xattn_all.items() if k in ('wq', 'wk', 'wv', 'wo')}
    del _L0_xattn_all

    def _L0_ffn_setup():
        import jax, jax.numpy as jnp
        import numpy as np
        HIDDEN = 128
        INNER = 512

        def _weight_quant(w):
            scale = 1.0 / jnp.clip(jnp.mean(jnp.abs(w)), 1e-05)
            wq = jnp.clip(jnp.round(w * scale), -1.0, 1.0) / scale
            return w + jax.lax.stop_gradient(wq - w)

        def _act_quant(x):
            scale = 127.0 / jnp.clip(jnp.max(jnp.abs(x), axis=-1, keepdims=True), 1e-05)
            xq = jnp.clip(jnp.round(x * scale), -128.0, 127.0) / scale
            return x + jax.lax.stop_gradient(xq - x)

        def _bitlinear(x, w):
            return jnp.einsum('bsi,oi->bso', _act_quant(x), _weight_quant(w))
        key = jax.random.key(seed)
        k0, k1, k2, k3 = jax.random.split(key, 4)
        x = jax.random.normal(k0, (4, 256, HIDDEN), dtype=jnp.float32)
        w_gate = jax.random.normal(k1, (INNER, HIDDEN), dtype=jnp.float32) / np.sqrt(HIDDEN)
        w_up = jax.random.normal(k2, (INNER, HIDDEN), dtype=jnp.float32) / np.sqrt(HIDDEN)
        w_down = jax.random.normal(k3, (HIDDEN, INNER), dtype=jnp.float32) / np.sqrt(INNER)
        return {'x': x, 'w_gate': w_gate, 'w_up': w_up, 'w_down': w_down}
    _L0_ffn_all = _L0_ffn_setup()
    _L0_ffn_in = {k: v for k, v in _L0_ffn_all.items() if k in ('w_gate', 'w_up', 'w_down')}
    del _L0_ffn_all

    def _L1_xattn_setup():
        import jax, jax.numpy as jnp
        import numpy as np
        import math
        B, S, DM, H, DK, DV = (2, 256, 128, 16, 64, 64)
        NEG = -1000000.0
        key = jax.random.key(seed)
        ks = jax.random.split(key, 12)
        inp = {'queries': jax.random.normal(ks[0], (B, S, DM), jnp.float32), 'keys': jax.random.normal(ks[1], (B, S, DM), jnp.float32), 'values': jax.random.normal(ks[2], (B, S, DM), jnp.float32), 'WQ': jax.random.normal(ks[3], (H, DM, DK), jnp.float32) / math.sqrt(DM), 'bQ': jax.random.normal(ks[4], (H, DK), jnp.float32) * 0.02, 'WK': jax.random.normal(ks[5], (H, DM, DK), jnp.float32) / math.sqrt(DM), 'bK': jax.random.normal(ks[6], (H, DK), jnp.float32) * 0.02, 'WV': jax.random.normal(ks[7], (H, DM, DV), jnp.float32) / math.sqrt(DM), 'bV': jax.random.normal(ks[8], (H, DV), jnp.float32) * 0.02, 'WO': jax.random.normal(ks[9], (H * DV, DM), jnp.float32) / math.sqrt(H * DV), 'bO': jax.random.normal(ks[10], (DM,), jnp.float32) * 0.02, 'source_seq_len': jax.random.randint(ks[11], (B,), 1, S + 1).astype(jnp.int64)}
        return inp
    _L1_xattn_all = _L1_xattn_setup()
    _L1_xattn_in = {k: v for k, v in _L1_xattn_all.items() if k in ('WQ', 'bQ', 'WK', 'bK', 'WV', 'bV', 'WO', 'bO')}
    del _L1_xattn_all

    def _L1_ffn_setup():
        import jax, jax.numpy as jnp
        import numpy as np
        B, S, D = (2, 512, 128)
        H = 512
        E = 8
        K = 4
        key = jax.random.key(seed)
        kx, kr, ku, kd = jax.random.split(key, 4)
        x = jax.random.normal(kx, (B, S, D), dtype=jnp.float32)
        router_w = jax.random.normal(kr, (D, E), dtype=jnp.float32) / np.sqrt(D)
        up_w = jax.random.normal(ku, (E, D, H), dtype=jnp.float32) / np.sqrt(D)
        down_w = jax.random.normal(kd, (E, H, D), dtype=jnp.float32) / np.sqrt(H)
        return {'x': x, 'router_w': router_w, 'up_w': up_w, 'down_w': down_w}
    _L1_ffn_all = _L1_ffn_setup()
    _L1_ffn_in = {k: v for k, v in _L1_ffn_all.items() if k in ('router_w', 'up_w', 'down_w')}
    del _L1_ffn_all

    def _L2_xattn_setup():
        import jax, jax.numpy as jnp
        import numpy as np
        B, NT, NM, C, H, FF = (8, 128, 256, 128, 8, 512)

        def _ln(x, g, b):
            m = x.mean(-1, keepdims=True)
            v = jnp.mean((x - m) ** 2, axis=-1, keepdims=True)
            return (x - m) / jnp.sqrt(v + 1e-05) * g + b
        key = jax.random.key(seed)
        ks = jax.random.split(key, 8)
        w = lambda k, shape, s=0.02: jax.random.normal(k, shape, dtype=jnp.float32) * s
        return {'tgt': jax.random.normal(ks[0], (B, NT, C), dtype=jnp.float32), 'memory': jax.random.normal(ks[1], (B, NM, C), dtype=jnp.float32), 'qkv_w': w(ks[2], (3 * C, C)), 'qkv_b': jnp.zeros((3 * C,), jnp.float32), 'sa_out_w': w(ks[3], (C, C)), 'sa_out_b': jnp.zeros((C,), jnp.float32), 'in_proj_w': w(ks[4], (3 * C, C)), 'in_proj_b': jnp.zeros((3 * C,), jnp.float32), 'mha_out_w': w(ks[5], (C, C)), 'mha_out_b': jnp.zeros((C,), jnp.float32), 'lin1_w': w(ks[6], (FF, C)), 'lin1_b': jnp.zeros((FF,), jnp.float32), 'lin2_w': w(ks[7], (C, FF)), 'lin2_b': jnp.zeros((C,), jnp.float32), 'ln1_g': jnp.ones((C,), jnp.float32), 'ln1_b': jnp.zeros((C,), jnp.float32), 'ln2_g': jnp.ones((C,), jnp.float32), 'ln2_b': jnp.zeros((C,), jnp.float32), 'ln3_g': jnp.ones((C,), jnp.float32), 'ln3_b': jnp.zeros((C,), jnp.float32)}
    _L2_xattn_all = _L2_xattn_setup()
    _L2_xattn_in = {k: v for k, v in _L2_xattn_all.items() if k in ('qkv_w', 'qkv_b', 'sa_out_w', 'sa_out_b', 'in_proj_w', 'in_proj_b', 'mha_out_w', 'mha_out_b', 'lin1_w', 'lin1_b', 'lin2_w', 'lin2_b', 'ln1_g', 'ln1_b', 'ln2_g', 'ln2_b', 'ln3_g', 'ln3_b')}
    del _L2_xattn_all

    def _L2_ffn_setup():
        import jax, jax.numpy as jnp
        import numpy as np
        B, N, D = (4, 256, 128)
        SPARSITY = 0.01
        key = jax.random.key(seed)
        k1, k2, k3 = jax.random.split(key, 3)
        x = jax.random.normal(k1, (B, N, D), dtype=jnp.float32)
        spatial = jax.random.normal(k2, (D, D), dtype=jnp.float32) * 0.02
        freq = jnp.fft.fft(spatial, axis=-1)
        k = int(D * SPARSITY)
        mag = jnp.abs(freq)
        kth = jax.lax.top_k(mag, k)[0][:, -1:]
        w_sparse = jnp.where(mag >= kth, freq, 0.0 + 0j)
        bias = jax.random.normal(k3, (D,), dtype=jnp.float32) * 0.01
        return {'x': x, 'w_freq_real': jnp.real(w_sparse).astype(jnp.float32), 'w_freq_imag': jnp.imag(w_sparse).astype(jnp.float32), 'bias': bias}
    _L2_ffn_all = _L2_ffn_setup()
    _L2_ffn_in = {k: v for k, v in _L2_ffn_all.items() if k in ('w_freq_real', 'w_freq_imag', 'bias')}
    del _L2_ffn_all

    def _L3_xattn_setup():
        import jax, jax.numpy as jnp
        import numpy as np
        D_MODEL = 128
        N_HEADS = 16
        HEAD_DIM = D_MODEL // N_HEADS
        key = jax.random.key(seed)
        ks = jax.random.split(key, 11)
        B, Q, K = (4, 256, 256)
        s = 1.0 / np.sqrt(D_MODEL)
        inp = {'q': jax.random.normal(ks[0], (B, Q, D_MODEL), jnp.float32), 'k': jax.random.normal(ks[1], (B, K, D_MODEL), jnp.float32), 'v': jax.random.normal(ks[2], (B, K, D_MODEL), jnp.float32), 'kv_mask': jnp.ones((B, K), dtype=bool), 'Wq': jax.random.normal(ks[3], (D_MODEL, D_MODEL), jnp.float32) * s, 'bq': jnp.zeros((D_MODEL,), jnp.float32), 'Wk': jax.random.normal(ks[4], (D_MODEL, D_MODEL), jnp.float32) * s, 'bk': jnp.zeros((D_MODEL,), jnp.float32), 'Wv': jax.random.normal(ks[5], (D_MODEL, D_MODEL), jnp.float32) * s, 'bv': jnp.zeros((D_MODEL,), jnp.float32), 'Wo': jax.random.normal(ks[6], (D_MODEL, D_MODEL), jnp.float32) * s, 'bo': jnp.zeros((D_MODEL,), jnp.float32)}
        return inp
    _L3_xattn_all = _L3_xattn_setup()
    _L3_xattn_in = {k: v for k, v in _L3_xattn_all.items() if k in ('Wq', 'bq', 'Wk', 'bk', 'Wv', 'bv', 'Wo', 'bo')}
    del _L3_xattn_all

    def _L3_ffn_setup():
        import jax, jax.numpy as jnp
        import numpy as np
        B, T, C = (2, 128, 128)
        H = 512
        E_R, E_S, K = (8, 2, 2)

        def _rmsnorm(x, g):
            eps = jnp.finfo(x.dtype).eps
            return x * jax.lax.rsqrt(jnp.mean(x * x, axis=-1, keepdims=True) + eps) * g

        def _experts_mlp(x, g, W1, b1, W2, b2):
            xn = _rmsnorm(x, g)
            h = jnp.einsum('btc,ech->bteh', xn, W1) + b1
            h = jax.nn.gelu(h, approximate=False)
            return jnp.einsum('bteh,ehc->btec', h, W2) + b2
        key = jax.random.key(seed)
        ks = jax.random.split(key, 12)
        s = 0.02
        return {'u': jax.random.normal(ks[0], (B, T, C), dtype=jnp.float32), 'g_shared': jnp.ones((C,), jnp.float32), 'W1_s': jax.random.normal(ks[1], (E_S, C, H), jnp.float32) * s, 'b1_s': jax.random.normal(ks[2], (E_S, H), jnp.float32) * s, 'W2_s': jax.random.normal(ks[3], (E_S, H, C), jnp.float32) * s, 'b2_s': jax.random.normal(ks[4], (E_S, C), jnp.float32) * s, 'g_routed': jnp.ones((C,), jnp.float32), 'W1_r': jax.random.normal(ks[5], (E_R, C, H), jnp.float32) * s, 'b1_r': jax.random.normal(ks[6], (E_R, H), jnp.float32) * s, 'W2_r': jax.random.normal(ks[7], (E_R, H, C), jnp.float32) * s, 'b2_r': jax.random.normal(ks[8], (E_R, C), jnp.float32) * s, 'centroids': jax.random.normal(ks[9], (C, E_R), jnp.float32) * s}
    _L3_ffn_all = _L3_ffn_setup()
    _L3_ffn_in = {k: v for k, v in _L3_ffn_all.items() if k in ('g_shared', 'W1_s', 'b1_s', 'W2_s', 'b2_s', 'g_routed', 'W1_r', 'b1_r', 'W2_r', 'b2_r', 'centroids')}
    del _L3_ffn_all
    return {'x': x, 'ctx_1024': ctx_1024, '_lenS2': _lenS2, 'mask_BxS2_bf1': mask_BxS2_bf1, 'L0_xattn_wq': _L0_xattn_in['wq'], 'L0_xattn_wk': _L0_xattn_in['wk'], 'L0_xattn_wv': _L0_xattn_in['wv'], 'L0_xattn_wo': _L0_xattn_in['wo'], 'L0_ffn_w_gate': _L0_ffn_in['w_gate'], 'L0_ffn_w_up': _L0_ffn_in['w_up'], 'L0_ffn_w_down': _L0_ffn_in['w_down'], 'L1_xattn_WQ': _L1_xattn_in['WQ'], 'L1_xattn_bQ': _L1_xattn_in['bQ'], 'L1_xattn_WK': _L1_xattn_in['WK'], 'L1_xattn_bK': _L1_xattn_in['bK'], 'L1_xattn_WV': _L1_xattn_in['WV'], 'L1_xattn_bV': _L1_xattn_in['bV'], 'L1_xattn_WO': _L1_xattn_in['WO'], 'L1_xattn_bO': _L1_xattn_in['bO'], 'L1_ffn_router_w': _L1_ffn_in['router_w'], 'L1_ffn_up_w': _L1_ffn_in['up_w'], 'L1_ffn_down_w': _L1_ffn_in['down_w'], 'L2_xattn_qkv_w': _L2_xattn_in['qkv_w'], 'L2_xattn_qkv_b': _L2_xattn_in['qkv_b'], 'L2_xattn_sa_out_w': _L2_xattn_in['sa_out_w'], 'L2_xattn_sa_out_b': _L2_xattn_in['sa_out_b'], 'L2_xattn_in_proj_w': _L2_xattn_in['in_proj_w'], 'L2_xattn_in_proj_b': _L2_xattn_in['in_proj_b'], 'L2_xattn_mha_out_w': _L2_xattn_in['mha_out_w'], 'L2_xattn_mha_out_b': _L2_xattn_in['mha_out_b'], 'L2_xattn_lin1_w': _L2_xattn_in['lin1_w'], 'L2_xattn_lin1_b': _L2_xattn_in['lin1_b'], 'L2_xattn_lin2_w': _L2_xattn_in['lin2_w'], 'L2_xattn_lin2_b': _L2_xattn_in['lin2_b'], 'L2_xattn_ln1_g': _L2_xattn_in['ln1_g'], 'L2_xattn_ln1_b': _L2_xattn_in['ln1_b'], 'L2_xattn_ln2_g': _L2_xattn_in['ln2_g'], 'L2_xattn_ln2_b': _L2_xattn_in['ln2_b'], 'L2_xattn_ln3_g': _L2_xattn_in['ln3_g'], 'L2_xattn_ln3_b': _L2_xattn_in['ln3_b'], 'L2_ffn_w_freq_real': _L2_ffn_in['w_freq_real'], 'L2_ffn_w_freq_imag': _L2_ffn_in['w_freq_imag'], 'L2_ffn_bias': _L2_ffn_in['bias'], 'L3_xattn_Wq': _L3_xattn_in['Wq'], 'L3_xattn_bq': _L3_xattn_in['bq'], 'L3_xattn_Wk': _L3_xattn_in['Wk'], 'L3_xattn_bk': _L3_xattn_in['bk'], 'L3_xattn_Wv': _L3_xattn_in['Wv'], 'L3_xattn_bv': _L3_xattn_in['bv'], 'L3_xattn_Wo': _L3_xattn_in['Wo'], 'L3_xattn_bo': _L3_xattn_in['bo'], 'L3_ffn_g_shared': _L3_ffn_in['g_shared'], 'L3_ffn_W1_s': _L3_ffn_in['W1_s'], 'L3_ffn_b1_s': _L3_ffn_in['b1_s'], 'L3_ffn_W2_s': _L3_ffn_in['W2_s'], 'L3_ffn_b2_s': _L3_ffn_in['b2_s'], 'L3_ffn_g_routed': _L3_ffn_in['g_routed'], 'L3_ffn_W1_r': _L3_ffn_in['W1_r'], 'L3_ffn_b1_r': _L3_ffn_in['b1_r'], 'L3_ffn_W2_r': _L3_ffn_in['W2_r'], 'L3_ffn_b2_r': _L3_ffn_in['b2_r'], 'L3_ffn_centroids': _L3_ffn_in['centroids']}

def reference(x, ctx_1024, _lenS2, mask_BxS2_bf1, L0_xattn_wq, L0_xattn_wk, L0_xattn_wv, L0_xattn_wo, L0_ffn_w_gate, L0_ffn_w_up, L0_ffn_w_down, L1_xattn_WQ, L1_xattn_bQ, L1_xattn_WK, L1_xattn_bK, L1_xattn_WV, L1_xattn_bV, L1_xattn_WO, L1_xattn_bO, L1_ffn_router_w, L1_ffn_up_w, L1_ffn_down_w, L2_xattn_qkv_w, L2_xattn_qkv_b, L2_xattn_sa_out_w, L2_xattn_sa_out_b, L2_xattn_in_proj_w, L2_xattn_in_proj_b, L2_xattn_mha_out_w, L2_xattn_mha_out_b, L2_xattn_lin1_w, L2_xattn_lin1_b, L2_xattn_lin2_w, L2_xattn_lin2_b, L2_xattn_ln1_g, L2_xattn_ln1_b, L2_xattn_ln2_g, L2_xattn_ln2_b, L2_xattn_ln3_g, L2_xattn_ln3_b, L2_ffn_w_freq_real, L2_ffn_w_freq_imag, L2_ffn_bias, L3_xattn_Wq, L3_xattn_bq, L3_xattn_Wk, L3_xattn_bk, L3_xattn_Wv, L3_xattn_bv, L3_xattn_Wo, L3_xattn_bo, L3_ffn_g_shared, L3_ffn_W1_s, L3_ffn_b1_s, L3_ffn_W2_s, L3_ffn_b2_s, L3_ffn_g_routed, L3_ffn_W1_r, L3_ffn_b1_r, L3_ffn_W2_r, L3_ffn_b2_r, L3_ffn_centroids):
    import jax
    import jax.numpy as jnp

    def _L0_xattn_ref(queries, keys, values, wq, wk, wv, wo):
        import jax, jax.numpy as jnp
        import numpy as np
        import math
        D_MODEL = 128
        N_HEADS = 16
        C = 1
        B, L = (8, 256)

        def _glorot(key, fan):
            lim = np.sqrt(6.0 / (fan + fan)).astype(np.float32)
            return jax.random.uniform(key, (fan, fan), jnp.float32, -lim, lim)
        Bv, Lv, _ = queries.shape
        H = N_HEADS
        Dh = D_MODEL // N_HEADS
        Q = (queries @ wq).reshape(Bv, Lv, H, Dh).transpose(0, 2, 3, 1)
        K = (keys @ wk).reshape(Bv, Lv, H, Dh).transpose(0, 2, 3, 1)
        V = (values @ wv).reshape(Bv, Lv, H, Dh).transpose(0, 2, 3, 1)
        corr = jnp.fft.irfft(jnp.fft.rfft(Q, axis=-1) * jnp.conj(jnp.fft.rfft(K, axis=-1)), n=Lv, axis=-1)
        k_top = int(math.floor(C * math.log(Lv)))
        top_vals, top_idx = jax.lax.top_k(corr, k_top)
        w = jax.nn.softmax(top_vals, axis=-1)
        t = jnp.arange(Dh)
        out = jnp.zeros_like(V)
        for i in range(k_top):
            gather_idx = (t[None, None, :] - top_idx[..., i]) % Dh
            rolled = jnp.take_along_axis(V, gather_idx[..., None], axis=2)
            out = out + w[..., i, None] * rolled
        out = out.transpose(0, 2, 1, 3).reshape(Bv, Lv, D_MODEL)
        return out @ wo

    def _L0_ffn_ref(x, w_gate, w_up, w_down):
        import jax, jax.numpy as jnp
        import numpy as np
        HIDDEN = 128
        INNER = 512

        def _weight_quant(w):
            scale = 1.0 / jnp.clip(jnp.mean(jnp.abs(w)), 1e-05)
            wq = jnp.clip(jnp.round(w * scale), -1.0, 1.0) / scale
            return w + jax.lax.stop_gradient(wq - w)

        def _act_quant(x):
            scale = 127.0 / jnp.clip(jnp.max(jnp.abs(x), axis=-1, keepdims=True), 1e-05)
            xq = jnp.clip(jnp.round(x * scale), -128.0, 127.0) / scale
            return x + jax.lax.stop_gradient(xq - x)

        def _bitlinear(x, w):
            return jnp.einsum('bsi,oi->bso', _act_quant(x), _weight_quant(w))
        gate = jax.nn.silu(_bitlinear(x, w_gate))
        up = _bitlinear(x, w_up)
        return _bitlinear(gate * up, w_down)

    def _L1_xattn_ref(queries, keys, values, WQ, bQ, WK, bK, WV, bV, WO, bO, source_seq_len):
        import jax, jax.numpy as jnp
        import numpy as np
        import math
        B, S, DM, H, DK, DV = (2, 256, 128, 16, 64, 64)
        NEG = -1000000.0
        Bq, Sq, _ = queries.shape
        Sk = keys.shape[1]
        Q = jnp.einsum('bsd,hdk->bhsk', queries, WQ) + bQ[None, :, None, :]
        K = jnp.einsum('btd,hdk->bhtk', keys, WK) + bK[None, :, None, :]
        V = jnp.einsum('btd,hdv->bhtv', values, WV) + bV[None, :, None, :]
        scores = jnp.einsum('bhsk,bhtk->bhst', Q, K) / math.sqrt(Q.shape[-1])
        causal_ok = jnp.arange(Sk)[None, :] <= jnp.arange(Sq)[:, None]
        pad_ok = jnp.arange(Sk)[None, :] < source_seq_len[:, None]
        allowed = causal_ok[None, None, :, :] & pad_ok[:, None, None, :]
        attn = jax.nn.softmax(jnp.where(allowed, scores, NEG), axis=-1)
        heads = jnp.einsum('bhst,bhtv->bhsv', attn, V)
        concat = heads.transpose(0, 2, 1, 3).reshape(Bq, Sq, -1)
        return concat @ WO + bO

    def _L1_ffn_ref(x, router_w, up_w, down_w):
        import jax, jax.numpy as jnp
        import numpy as np
        B, S, D = (2, 512, 128)
        H = 512
        E = 8
        K = 4
        router_logits = jnp.einsum('bsd,de->bse', x, router_w)
        routing_weights = jax.nn.softmax(router_logits, axis=-1)
        topk_weights, topk_indices = jax.lax.top_k(routing_weights, K)
        topk_weights = topk_weights / jnp.sum(topk_weights, axis=-1, keepdims=True)
        h = jnp.einsum('bsd,edh->bseh', x, up_w)
        h = jax.nn.gelu(h)
        expert_outputs = jnp.einsum('bseh,ehd->bsed', h, down_w)
        gathered = jnp.take_along_axis(expert_outputs, topk_indices[:, :, :, None], axis=2)
        output = jnp.sum(topk_weights[:, :, :, None] * gathered, axis=2)
        return output

    def _L2_xattn_ref(tgt, memory, qkv_w, qkv_b, sa_out_w, sa_out_b, in_proj_w, in_proj_b, mha_out_w, mha_out_b, lin1_w, lin1_b, lin2_w, lin2_b, ln1_g, ln1_b, ln2_g, ln2_b, ln3_g, ln3_b):
        import jax, jax.numpy as jnp
        import numpy as np
        B, NT, NM, C, H, FF = (8, 128, 256, 128, 8, 512)

        def _ln(x, g, b):
            m = x.mean(-1, keepdims=True)
            v = jnp.mean((x - m) ** 2, axis=-1, keepdims=True)
            return (x - m) / jnp.sqrt(v + 1e-05) * g + b
        Bx, N, Cx = tgt.shape
        qkv = tgt @ qkv_w.T + qkv_b
        q, k, v = jnp.split(qkv, 3, axis=-1)
        scores = jnp.einsum('bnc,bmc->bnm', q, k) * jnp.sqrt(jnp.float32(Cx))
        diag = jnp.eye(N, dtype=bool)
        scores = jnp.where(diag[None, :, :], scores, -jnp.inf)
        attn = jax.nn.softmax(scores, axis=-1)
        sa = jnp.einsum('bnm,bmc->bnc', attn, v) @ sa_out_w.T + sa_out_b
        x = _ln(tgt + sa, ln1_g, ln1_b)
        d = Cx // H
        wq, wk, wv = jnp.split(in_proj_w, 3, axis=0)
        bq, bk, bv = jnp.split(in_proj_b, 3, axis=0)
        qh = (x @ wq.T + bq).reshape(Bx, N, H, d).transpose(0, 2, 1, 3)
        kh = (memory @ wk.T + bk).reshape(Bx, -1, H, d).transpose(0, 2, 1, 3)
        vh = (memory @ wv.T + bv).reshape(Bx, -1, H, d).transpose(0, 2, 1, 3)
        a = jax.nn.softmax(jnp.einsum('bhnd,bhmd->bhnm', qh, kh) / jnp.sqrt(jnp.float32(d)), axis=-1)
        ca = jnp.einsum('bhnm,bhmd->bhnd', a, vh).transpose(0, 2, 1, 3).reshape(Bx, N, Cx)
        ca = ca @ mha_out_w.T + mha_out_b
        x = _ln(x + ca, ln2_g, ln2_b)
        ff = jax.nn.relu(x @ lin1_w.T + lin1_b) @ lin2_w.T + lin2_b
        return _ln(x + ff, ln3_g, ln3_b)

    def _L2_ffn_ref(x, w_freq_real, w_freq_imag, bias):
        import jax, jax.numpy as jnp
        import numpy as np
        B, N, D = (4, 256, 128)
        SPARSITY = 0.01
        w = jax.lax.complex(w_freq_real, w_freq_imag)
        x_freq = jnp.fft.fft(x, axis=-1)
        y_freq = jnp.einsum('bnd,do->bno', x_freq, w)
        y = jnp.real(jnp.fft.ifft(y_freq, axis=-1))
        return y + bias

    def _L3_xattn_ref(q, k, v, kv_mask, Wq, bq, Wk, bk, Wv, bv, Wo, bo):
        import jax, jax.numpy as jnp
        import numpy as np
        D_MODEL = 128
        N_HEADS = 16
        HEAD_DIM = D_MODEL // N_HEADS
        B, Qlen, _ = q.shape
        Klen = k.shape[1]
        qh = (q @ Wq.T + bq).reshape(B, Qlen, N_HEADS, HEAD_DIM).transpose(0, 2, 1, 3)
        kh = (k @ Wk.T + bk).reshape(B, Klen, N_HEADS, HEAD_DIM).transpose(0, 2, 1, 3)
        vh = (v @ Wv.T + bv).reshape(B, Klen, N_HEADS, HEAD_DIM).transpose(0, 2, 1, 3)
        score = jnp.einsum('bhqd,bhkd->bhqk', qh, kh) / np.sqrt(HEAD_DIM).astype(np.float32)
        score = jnp.where(kv_mask[:, None, None, :], score, jnp.float32(-10000.0))
        attn = jax.nn.softmax(score, axis=-1)
        out = jnp.einsum('bhqk,bhkd->bhqd', attn, vh)
        out = out.transpose(0, 2, 1, 3).reshape(B, Qlen, D_MODEL)
        return out @ Wo.T + bo

    def _L3_ffn_ref(u, g_shared, W1_s, b1_s, W2_s, b2_s, g_routed, W1_r, b1_r, W2_r, b2_r, centroids):
        import jax, jax.numpy as jnp
        import numpy as np
        B, T, C = (2, 128, 128)
        H = 512
        E_R, E_S, K = (8, 2, 2)

        def _rmsnorm(x, g):
            eps = jnp.finfo(x.dtype).eps
            return x * jax.lax.rsqrt(jnp.mean(x * x, axis=-1, keepdims=True) + eps) * g

        def _experts_mlp(x, g, W1, b1, W2, b2):
            xn = _rmsnorm(x, g)
            h = jnp.einsum('btc,ech->bteh', xn, W1) + b1
            h = jax.nn.gelu(h, approximate=False)
            return jnp.einsum('bteh,ehc->btec', h, W2) + b2
        h_s = _experts_mlp(u, g_shared, W1_s, b1_s, W2_s, b2_s).sum(axis=-2)
        scores = jax.nn.sigmoid(u @ centroids)
        gpk, i_topk = jax.lax.top_k(scores, K)
        gk = gpk / scores.sum(axis=-1, keepdims=True)
        routed_all = _experts_mlp(u, g_routed, W1_r, b1_r, W2_r, b2_r)
        routed_topk = jnp.take_along_axis(routed_all, i_topk[..., None], axis=2)
        h_r = (gk[..., None] * routed_topk).sum(axis=-2)
        return u + h_s + h_r
    x = x + _L0_xattn_ref(_layernorm(x, axis=-1), ctx_1024, ctx_1024, L0_xattn_wq, L0_xattn_wk, L0_xattn_wv, L0_xattn_wo)
    x = x + _L0_ffn_ref(_layernorm(x, axis=-1), L0_ffn_w_gate, L0_ffn_w_up, L0_ffn_w_down)
    x = x + _L1_xattn_ref(_layernorm(x, axis=-1), ctx_1024, ctx_1024, L1_xattn_WQ, L1_xattn_bQ, L1_xattn_WK, L1_xattn_bK, L1_xattn_WV, L1_xattn_bV, L1_xattn_WO, L1_xattn_bO, _lenS2)
    x = x + _L1_ffn_ref(_layernorm(x, axis=-1), L1_ffn_router_w, L1_ffn_up_w, L1_ffn_down_w)
    x = x + _L2_xattn_ref(_layernorm(x, axis=-1), ctx_1024, L2_xattn_qkv_w, L2_xattn_qkv_b, L2_xattn_sa_out_w, L2_xattn_sa_out_b, L2_xattn_in_proj_w, L2_xattn_in_proj_b, L2_xattn_mha_out_w, L2_xattn_mha_out_b, L2_xattn_lin1_w, L2_xattn_lin1_b, L2_xattn_lin2_w, L2_xattn_lin2_b, L2_xattn_ln1_g, L2_xattn_ln1_b, L2_xattn_ln2_g, L2_xattn_ln2_b, L2_xattn_ln3_g, L2_xattn_ln3_b)
    x = x + _L2_ffn_ref(_layernorm(x, axis=-1), L2_ffn_w_freq_real, L2_ffn_w_freq_imag, L2_ffn_bias)
    x = x + _L3_xattn_ref(_layernorm(x, axis=-1), ctx_1024, ctx_1024, mask_BxS2_bf1, L3_xattn_Wq, L3_xattn_bq, L3_xattn_Wk, L3_xattn_bk, L3_xattn_Wv, L3_xattn_bv, L3_xattn_Wo, L3_xattn_bo)
    x = x + _L3_ffn_ref(_layernorm(x, axis=-1), L3_ffn_g_shared, L3_ffn_W1_s, L3_ffn_b1_s, L3_ffn_W2_s, L3_ffn_b2_s, L3_ffn_g_routed, L3_ffn_W1_r, L3_ffn_b1_r, L3_ffn_W2_r, L3_ffn_b2_r, L3_ffn_centroids)
    return x

_drawn_inputs = setup_inputs


def setup_inputs(seed=0):
    import zlib

    import numpy as np

    out = dict(_drawn_inputs(seed))
    spreads = {'L2_xattn_qkv_b': (0.0, 0.8),
     'L2_xattn_sa_out_b': (0.0, 0.1),
     'L2_xattn_in_proj_b': (0.0, 0.8),
     'L2_xattn_mha_out_b': (0.0, 0.1),
     'L2_xattn_lin1_b': (0.0, 0.698),
     'L2_xattn_lin2_b': (0.0, 0.1),
     'L2_xattn_ln1_g': (1.0, 0.2),
     'L2_xattn_ln1_b': (0.0, 0.1),
     'L2_xattn_ln2_g': (1.0, 0.2),
     'L2_xattn_ln2_b': (0.0, 0.1),
     'L2_xattn_ln3_g': (1.0, 0.2),
     'L2_xattn_ln3_b': (0.0, 0.1),
     'L3_xattn_bq': (0.0, 0.8),
     'L3_xattn_bk': (0.0, 2.0),
     'L3_xattn_bv': (0.0, 0.1),
     'L3_xattn_bo': (0.0, 0.1),
     'L3_ffn_g_shared': (1.0, 0.6),
     'L3_ffn_g_routed': (1.0, 0.6)}
    factors = {'L1_xattn_bQ': 8.0,
     'L1_xattn_bK': 64.0,
     'L1_xattn_bV': 3.389,
     'L1_xattn_bO': 3.051,
     'L2_xattn_qkv_w': 2.747,
     'L2_xattn_in_proj_w': 5.625,
     'L2_xattn_mha_out_w': 4.118,
     'L2_ffn_bias': 8.0,
     'L3_ffn_b1_s': 29.03,
     'L3_ffn_b2_s': 7.437,
     'L3_ffn_W1_r': 8.0,
     'L3_ffn_b1_r': 8.0,
     'L3_ffn_W2_r': 8.0,
     'L3_ffn_b2_r': 37.766,
     'L3_ffn_centroids': 8.0}
    for name, (base, spread) in spreads.items():
        noise = np.random.default_rng([zlib.crc32(name.encode()), seed]).standard_normal(out[name].shape)
        drawn = base * np.exp(spread * noise) if base else spread * noise
        out[name] = jnp.asarray(drawn.astype(out[name].dtype))
    for name, factor in factors.items():
        out[name] = (out[name] * factor).astype(out[name].dtype)
    return out
```

```python
from contextlib import ExitStack

import concourse.bass as bass
import numpy as np
from concourse import mybir

F32, BF16 = mybir.dt.float32, mybir.dt.bfloat16
I32, U32, U8 = mybir.dt.int32, mybir.dt.uint32, mybir.dt.uint8
ACT, ALU, AX = mybir.ActivationFunctionType, mybir.AluOpType, mybir.AxisListType

P = 128
B, L = 8, 256
T2 = L // P
NT = B * T2
EPS = 1e-5
EPS_RMS = float(np.finfo(np.float32).eps)
ROUND = float(3 << 22)
NEG = -1e30


class Order:

    def __init__(self, k, eng, name, turn=0, turns=1, per=None):
        self.k, self.eng, self.name, self.turns, self.per = k, eng, name, turns, per
        self.count = 0
        self.start = k.ordered[name] + (turn * per if turns > 1 else 0)

    def mark(self, ins):
        self.count += 1
        return ins.then_inc(self.k.order[self.name], 1)

    def settle(self):
        self.eng.wait_ge(self.k.order[self.name], self.start + self.count)

    def settle_apart(self):
        self.settle()
        self.k.carry(self.eng)

    def close(self):
        assert self.turns == 1 or self.count == self.per, (self.name, self.count)
        self.k.ordered[self.name] += self.turns * self.count


class Kit:

    def __init__(self, nc, ctx, dram, out):
        self.nc, self.ctx, self.d, self.out = nc, ctx, dram, out
        self.order = {e: ctx.enter_context(nc.semaphore(f"{e}_order")) for e in ("dve", "act", "pool")}
        self.ordered = dict.fromkeys(self.order, 0)
        self.bank = [self.psum(f"bank{n}") for n in range(8)]
        self.x = self.sb("x_stream", [P, NT, P])
        self.tick, self.ticks = self.sb("tick", [1, 256]), 0
        self.stats, self.rstd, self.normed = self.sem("norm_stats"), self.sem("norm_rstd"), 0
        self.rest, self.layer2, self.layer1, self.layer0 = ExitStack(), ExitStack(), ExitStack(), ExitStack()
        self.w = {}

    def sb(self, name, shape, dt=F32, ctx=None):
        return (ctx or self.ctx).enter_context(self.nc.sbuf_tensor(name, shape, dt))

    def norms(self, count):
        self.normed += count
        return self.stats, self.rstd, self.normed - count

    def carry(self, eng):
        self.ticks += 1
        own = self.tick[:, self.ticks - 1:self.ticks]
        if eng is self.nc.gpsimd:
            eng.tensor_tensor(own, self.w["eps"][0:1, 0:1], self.w["eps"][0:1, 0:1], ALU.add)
        else:
            eng.memset(own, 0.0)

    def psum(self, name):
        return self.ctx.enter_context(self.nc.psum_tensor(name, [P, 512], F32))

    def sem(self, name):
        return self.ctx.enter_context(self.nc.semaphore(name))


def flat(ap):
    return ap.rearrange("p a b -> p (a b)")


def stage_setup(k):
    nc = k.nc
    loaded = k.sem("setup_loaded")
    first = ["dft", "idft", "head_block", "iota8", "rolled_base", "not_first",
             "q0_wq", "q0_wk", "q0_wv", "q0_wo", "spread_rows", "fourier_cos", "fourier_sin", "fourier_nsin",
             "L2_ffn_w_freq_real", "L2_ffn_w_freq_imag", "L2_saT", "L2_sa_v", "L2_sa_vb"]
    later = ["ident", "ident_bf", "L2_bias", "L2_vecs", "L2_lin1T", "L2_lin1b", "L2_lin2T",
             "L2_wq", "L2_wk", "L2_wv", "L2_wo", "L2_bq", "L2_bk", "L2_bv", "L2_bo",
             "L3_wq", "L3_wk", "L3_wv", "L3_wo", "L3_bq", "L3_bk", "L3_bv", "L3_bo",
             "L3_centroids", "L3_g", "L3_b1", "L3_b2", "prefix"]
    second = ["L1_WQ", "L1_WK", "L1_WV", "L1_WO", "L1_bQ", "L1_bK", "L1_bV", "L1_bO", "L1_router",
              "causal", "iota_k", "head_pick"]
    w = k.w
    small = first + second + later
    for n in later:
        w[n] = k.sb("w_" + n, list(k.d[n].shape), k.d[n].dtype)
    n_small = 16 * (4 + len(small))
    w["fourier"] = k.sb("fourier", [P, P])
    w["minus_half"] = k.sb("minus_half", [P, 8])
    w["eps"], w["eps_rms"] = k.sb("eps", [P, 8]), k.sb("eps_rms", [P, 8])
    w["sa"] = k.sb("sa", [P, P])
    w["sa_bias"] = k.sb("sa_bias", [P, P])
    w["mask"] = k.sb("mask", [P, B * L])
    w["lens"] = k.sb("lens", [P, B])
    for n in second:
        w[n] = k.sb("w_" + n, list(k.d[n].shape), k.d[n].dtype, k.layer1)
    for n in ("up_w", "down_w"):
        w[n] = k.sb(n, [P, 8, 512], F32, k.layer1)
    for n in first:
        w[n] = k.sb("w_" + n, list(k.d[n].shape), k.d[n].dtype, k.layer0)
    for n in ("gate", "up", "down"):
        w["tern_" + n] = k.sb("tern_" + n, [P, 512], BF16, k.layer0)
        w["scale_" + n] = k.sb("scale_" + n, [P, 1], F32, k.layer0)
    with ExitStack() as local:
        raw = k.sb("raw_ternary", [P, 3, 512], ctx=local)
        ratio = k.sb("ternary_ratio", [P, 3, 512], ctx=local)
        rowsum = k.sb("ternary_rowsum", [P, 3], ctx=local)
        inv = k.sb("ternary_inv", [P, 3], ctx=local)
        ones = k.sb("ones128", [P, P], ctx=local)
        spec = k.sb("fourier_ab", [P, 2, P], ctx=local)
        mask8 = k.sb("mask_bytes", [P, B * L], U8, ctx=local)
        len_i = k.sb("lens_int", [P, B], I32, ctx=local)
        sa_b = k.sb("sa_bcast", [P, P], ctx=local)
        big_loaded = k.sem("ffn1_loaded")
        k.big_loaded = big_loaded
        summed, spectra, mixed = k.sem("setup_summed"), k.sem("setup_spectra"), k.sem("setup_mixed")
        prepared = k.sem("setup_prepared")
        with nc.Block() as block:
            @block.sync
            def _(sp):
                sp.dma_start(k.x[:], k.d["x"].rearrange("b (t p) d -> p (b t) d", p=P)).then_inc(loaded, 16)
                sp.dma_start(raw[:], k.d["ternary"]).then_inc(loaded, 16)
                sp.dma_start(mask8[:], k.d["mask_bytes"].partition_broadcast(P)).then_inc(loaded, 16)
                sp.dma_start(len_i[:], k.d["lens"].partition_broadcast(P)).then_inc(loaded, 16)
                for n in small:
                    sp.dma_start(w[n][:], k.d[n]).then_inc(loaded, 16)
                for n in ("up_w", "down_w"):
                    sp.dma_start(w[n][:], k.d["L1_" + n]).then_inc(big_loaded, 16)

            @block.vector
            def _(v):
                order = Order(k, v, "dve")
                nc.vector.memset(ones[:], 1.0)
                nc.vector.memset(w["eps"][:], EPS)
                nc.vector.memset(w["eps_rms"][:], EPS_RMS)
                nc.vector.memset(w["minus_half"][:], -0.5).then_inc(prepared, 1)
                v.wait_ge(loaded, n_small)
                order.mark(nc.vector.tensor_reduce(rowsum[:], raw[:], AX.X, ALU.add, apply_absolute_value=True))
                order.settle()
                nc.vector.tensor_scalar(rowsum[:], rowsum[:], 1.0 / (512 * P), None, ALU.mult).then_inc(prepared, 1)
                nc.vector.tensor_copy(w["mask"][:], mask8[:])
                order.mark(nc.vector.tensor_copy(w["lens"][:], len_i[:]))
                v.wait_ge(summed, 1)
                order.mark(nc.vector.tensor_scalar(rowsum[:], k.bank[0][:, 0:3], EPS, None, ALU.max))
                order.settle()
                order.mark(nc.vector.reciprocal(inv[:], rowsum[:]))
                order.settle()
                for j, n in enumerate(("gate", "up", "down")):
                    order.mark(nc.vector.tensor_scalar(ratio[:, j, :], raw[:, j, :], inv[:, j:j + 1], ROUND, ALU.mult, ALU.add))
                    order.settle()
                    order.mark(nc.vector.tensor_scalar(ratio[:, j, :], ratio[:, j, :], -ROUND, 1.0, ALU.add, ALU.min))
                    order.settle()
                    nc.vector.tensor_scalar(w["tern_" + n][:], ratio[:, j, :], -1.0, None, ALU.max)
                    order.mark(nc.vector.tensor_copy(w["scale_" + n][:], rowsum[:, j:j + 1]))
                v.wait_ge(spectra, 1)
                nc.vector.tensor_copy(flat(spec[:]), k.bank[1][:, 0:2 * P]).then_inc(prepared, 1)
                v.wait_ge(mixed, 1)
                nc.vector.tensor_scalar(w["fourier"][:], k.bank[2][:, 0:P], 1.0 / P, None, ALU.mult)
                nc.vector.tensor_copy(w["sa"][:], k.bank[3][:, 0:P])
                order.mark(nc.vector.tensor_tensor(w["sa_bias"][:], k.bank[3][:, P:2 * P], w["L2_vecs"][:, 0, :], ALU.add))
                order.settle()
                order.close()

            @block.tensor
            def _(pe):
                mm = nc.tensor.matmul
                pe.wait_ge(loaded, n_small)
                pe.wait_ge(prepared, 2)
                mm(k.bank[0][:, 0:3], ones[:], rowsum[:], start=True, stop=True).then_inc(summed, 1)
                wr, wi = w["L2_ffn_w_freq_real"], w["L2_ffn_w_freq_imag"]
                c, s, ns = w["fourier_cos"], w["fourier_sin"], w["fourier_nsin"]
                mm(k.bank[1][:, 0:P], wr[:], c[:], start=True, stop=False)
                mm(k.bank[1][:, 0:P], wi[:], s[:], start=False, stop=True)
                mm(k.bank[1][:, P:2 * P], wi[:], c[:], start=True, stop=False)
                mm(k.bank[1][:, P:2 * P], wr[:], ns[:], start=False, stop=True).then_inc(spectra, 1)
                mm(k.bank[3][:, 0:P], w["L2_sa_v"][:], w["L2_saT"][:], start=True, stop=True)
                mm(k.bank[3][:, P:2 * P], w["L2_sa_vb"][:], w["L2_saT"][:], start=True, stop=True)
                pe.wait_ge(prepared, 3)
                mm(k.bank[2][:, 0:P], spec[:, 0, :], c[:], start=True, stop=False)
                mm(k.bank[2][:, 0:P], spec[:, 1, :], ns[:], start=False, stop=True).then_inc(mixed, 1)


def ln_stats(k, order, src, six, two, last):
    nc, tiles = k.nc, src.shape[1]
    for t in range(tiles):
        ins = nc.vector.bn_stats(six[:, t, :], src[:, t, :])
    order.mark(ins)
    order.settle_apart()
    for t in range(tiles):
        ins = nc.vector.bn_aggr(two[:, t, :], six[:, t, :])
    return last(ins)


def rstd_on_pool(k, order, var, rstd, n, eps=EPS):
    nc = k.nc
    order.mark(nc.gpsimd.tensor_tensor(rstd, var, k.w["eps"][:, 0:n] if eps == EPS else k.w["eps_rms"][:, 0:n], ALU.add))
    order.settle()
    return nc.gpsimd.tensor_tensor(rstd, rstd, k.w["minus_half"][:, 0:n], ALU.pow)


def stage_autocorrelation(k):
    nc, w, S = k.nc, k.w, 4
    TURNS = B // S
    TOP = int(np.floor(np.log(L)))
    with ExitStack() as local:
        sb = lambda n, s, d=F32: [k.sb(f"ac_{n}{j}", s, d, local) for j in range(S)]
        ctx, ctxT = sb("ctx", [P, T2, P]), sb("ctxT", [P, L])
        six, two, rstd = sb("six", [P, T2, 6]), sb("two", [P, T2, 2]), sb("rstd", [P, T2])
        xn, xnT, qk = sb("xn", [P, T2, P]), sb("xnT", [P, L]), sb("qk", [P, T2, 2 * P])
        freq, prod, cross = sb("freq", [P, 2, 2 * P]), sb("prod", [P, 2, P]), sb("cross", [P, 2, P])
        spec = sb("spec", [P, 2, P])
        top, neg, at = sb("top", [P, 8]), sb("neg", [P, 1]), sb("at", [P, 8], U32)
        e5, den, shift, shift_i = sb("e5", [P, 8]), sb("den", [P, 1]), sb("shift", [P, 8]), sb("shift_i", [P, 8], I32)
        hit, roll, mix = sb("hit", [P, 8, TOP]), sb("roll", [P, 8]), sb("mix", [P, P])
        ctx_wo, val_wo, spread = sb("ctx_wo", [P, L]), sb("val_wo", [P, L]), sb("spread", [P, 4, P])
        sem = lambda n: k.sem("ac_" + n)
        ctx_in = [sem(f"ctx_in{j}") for j in range(S)]
        stats, rs, n0 = k.norms(B)
        xn_r, tr, evac = sem("xn"), sem("pe"), sem("evac")
        prod_r, spec_r, mix_r, done, topped, exped = sem("prod"), sem("spec"), sem("mix"), sem("done"), sem("topped"), sem("exped")
        PE, EV = 8, 6

        with nc.Block() as block:
            @block.sync
            def _(sp):
                with sp.Fori(0, TURNS) as i:
                    for s in range(S):
                        n = i * S + s
                        sp.wait_ge(done, n + 1)
                        sp.dma_start(ctx[s][:], k.d["ctx"][bass.ds(n, 1)].rearrange("b (t p) d -> p (b t) d", p=P)).then_inc(ctx_in[s], 16)
                        sp.dma_start(ctxT[s][:], k.d["ctxT"][bass.ds(n, 1)].rearrange("b d l -> (b d) l")).then_inc(ctx_in[s], 16)

            @block.gpsimd
            def _(pool):
                with pool.Fori(0, TURNS) as i:
                    order = Order(k, pool, "pool", i, TURNS, S)
                    for s in range(S):
                        pool.wait_ge(stats, n0 + i * S + s + 1)
                        rstd_on_pool(k, order, two[s][:, :, 1], rstd[s][:], T2).then_inc(rs, 1)
                    for s in range(S):
                        pool.wait_ge(evac, i * S * EV + 2 * S + s + 1)
                        nc.gpsimd.tensor_tensor(cross[s][:, 0, :], freq[s][:, 0, 0:P], freq[s][:, 1, P:2 * P], ALU.mult)
                        nc.gpsimd.tensor_tensor(cross[s][:, 1, :], freq[s][:, 1, 0:P], freq[s][:, 0, P:2 * P], ALU.mult).then_inc(prod_r, 1)
                    order.close()

            @block.vector
            def _(v):
                v.sem_inc(done, S)
                with v.Fori(0, TURNS) as i:
                    order = Order(k, v, "dve", i, TURNS, 11 * S)
                    for s in range(S):
                        ln_stats(k, order, k.x[:, bass.ds((i * S + s) * T2, T2), :], six[s], two[s], lambda ins: ins.then_inc(stats, 1))
                    for s in range(S):
                        v.wait_ge(rs, n0 + i * S + s + 1)
                        for t in range(T2):
                            ins = nc.vector.tensor_scalar(xn[s][:, t, :], k.x[:, bass.ds((i * S + s) * T2 + t, 1), :].rearrange("p a b -> p (a b)"),
                                                          two[s][:, t, 0:1], rstd[s][:, t:t + 1], ALU.subtract, ALU.mult)
                        ins.then_inc(xn_r, 1)
                    for s in range(S):
                        v.wait_ge(evac, i * S * EV + 2 * S + s + 1)
                        order.mark(nc.vector.tensor_tensor(prod[s][:], freq[s][:, :, 0:P], freq[s][:, :, P:2 * P], ALU.mult))
                    for s in range(S):
                        order.settle()
                        nc.vector.scalar_tensor_tensor(spec[s][:, 0, :], prod[s][:, 1, :], w["not_first"][:, 0:1], prod[s][:, 0, :], ALU.mult, ALU.add)
                        v.wait_ge(prod_r, i * S + s + 1)
                        order.mark(nc.vector.tensor_tensor(spec[s][:, 1, :], cross[s][:, 0, :], cross[s][:, 1, :], ALU.subtract))
                    order.settle()
                    for s in range(S):
                        nc.vector.tensor_copy(spec[s][0:1, 1, :], prod[s][0:1, 1, :]).then_inc(spec_r, 1)
                    for s in range(S):
                        v.wait_ge(tr, i * S * PE + 5 * S + s + 1)
                        corr = k.bank[2 * s][:, 0:L]
                        k.carry(v)
                        order.mark(nc.vector.max(top[s][:], corr))
                        order.settle_apart()
                        order.mark(nc.vector.max_index(at[s][:], top[s][:], corr))
                        nc.vector.tensor_scalar(neg[s][:], top[s][:, 0:1], -1.0, None, ALU.mult).then_inc(topped, 1)
                    for s in range(S):
                        order.settle()
                        order.mark(nc.vector.tensor_scalar(shift_i[s][:], at[s][:], -1.0, w["rolled_base"][:, 0:1], ALU.mult, ALU.add))
                    order.settle()
                    for s in range(S):
                        order.mark(nc.vector.tensor_single_scalar(shift_i[s][:], shift_i[s][:], 7, ALU.bitwise_and))
                    order.settle()
                    for s in range(S):
                        order.mark(nc.vector.tensor_copy(shift[s][:], shift_i[s][:]))
                    order.settle()
                    for s in range(S):
                        order.mark(nc.vector.tensor_tensor(
                            hit[s][:], shift[s][:, 0:TOP].unsqueeze(1).to_broadcast([P, 8, TOP]),
                            w["iota8"][:].unsqueeze(2).to_broadcast([P, 8, TOP]), ALU.is_equal))
                    order.settle()
                    for s in range(S):
                        v.wait_ge(exped, i * S + s + 1)
                        nc.vector.reciprocal(den[s][:], den[s][:])
                        order.mark(nc.vector.tensor_tensor(hit[s][:], hit[s][:], e5[s][:, 0:TOP].unsqueeze(1).to_broadcast([P, 8, TOP]), ALU.mult))
                    order.settle()
                    for s in range(S):
                        order.mark(nc.vector.tensor_reduce(roll[s][:], hit[s][:], AX.X, ALU.add))
                    order.settle()
                    for s in range(S):
                        nc.vector.scalar_tensor_tensor(
                            mix[s][:].rearrange("p (g m) -> p g m", m=8), w["head_block"][:].rearrange("p (g m) -> p g m", m=8), den[s][:, 0:1],
                            roll[s][:].unsqueeze(1).to_broadcast([P, 16, 8]), ALU.mult, ALU.mult).then_inc(mix_r, 1)
                    for s in range(S):
                        v.wait_ge(tr, i * S * PE + 7 * S + s + 1)
                        xs = k.x[:, bass.ds((i * S + s) * T2, T2), :]
                        nc.vector.tensor_tensor(xs, xs, k.bank[2 * s][:, L:2 * L].rearrange("p (t d) -> p t d", t=T2), ALU.add).then_inc(done, 1)
                    order.close()

            @block.scalar
            def _(act):
                with act.Fori(0, TURNS) as i:
                    for step, (src, dst) in enumerate((
                            (lambda s: k.bank[2 * s][:, 0:L], lambda s: xnT[s][:]),
                            (lambda s: k.bank[2 * s + 1][:], lambda s: flat(qk[s][:])),
                            (lambda s: k.bank[2 * s][:], lambda s: flat(freq[s][:])),
                            (lambda s: k.bank[2 * s + 1][:, 0:L], lambda s: ctx_wo[s][:]),
                            (lambda s: k.bank[2 * s + 1][:, L:2 * L], lambda s: val_wo[s][:]))):
                        for s in range(S):
                            act.wait_ge(tr, i * S * PE + step * S + s + 1)
                            nc.scalar.copy(dst(s), src(s)).then_inc(evac, 1)
                    for s in range(S):
                        act.wait_ge(topped, i * S + s + 1)
                        nc.scalar.activation(e5[s][:, 0:TOP], top[s][:, 0:TOP], ACT.Exp, bias=neg[s][:, 0:1], accum_out=den[s][:, 0:1]).then_inc(exped, 1)
                    for s in range(S):
                        act.wait_ge(tr, i * S * PE + 6 * S + s + 1)
                        nc.scalar.copy(flat(spread[s][:]), k.bank[2 * s + 1][:]).then_inc(evac, 1)

            @block.tensor
            def _(pe):
                mm = nc.tensor.matmul
                with pe.Fori(0, TURNS) as i:
                    for s in range(S):
                        a = k.bank[2 * s]
                        pe.wait_ge(xn_r, i * S + s + 1)
                        for t in range(T2):
                            ins = nc.tensor.transpose(a[:, t * P:(t + 1) * P], xn[s][:, t, :], w["ident"][:])
                        ins.then_inc(tr, 1)
                    for s in range(S):
                        b = k.bank[2 * s + 1]
                        pe.wait_ge(evac, i * S * EV + s + 1)
                        pe.wait_ge(ctx_in[s], i * 32 + 32)
                        for t in range(T2):
                            mm(b[:, t * L:t * L + P], xnT[s][:, t * P:(t + 1) * P], w["q0_wq"][:], start=True, stop=True)
                            ins = mm(b[:, t * L + P:(t + 1) * L], ctxT[s][:, t * P:(t + 1) * P], w["q0_wk"][:], start=True, stop=True)
                        ins.then_inc(tr, 1)
                    for s in range(S):
                        a = k.bank[2 * s]
                        pe.wait_ge(evac, i * S * EV + S + s + 1)
                        for f in range(2):
                            for t in range(T2):
                                ins = mm(a[:, f * L:(f + 1) * L], w["dft"][:, t, f * P:(f + 1) * P], qk[s][:, t, :], start=(t == 0), stop=(t == T2 - 1))
                        ins.then_inc(tr, 1)
                    for s in range(S):
                        b = k.bank[2 * s + 1]
                        pe.wait_ge(evac, i * S * EV + S + s + 1)
                        for t in range(T2):
                            ins = mm(b[:, t * P:(t + 1) * P], ctx[s][:, t, :], w["q0_wo"][:], start=True, stop=True)
                        ins.then_inc(tr, 1)
                    for s in range(S):
                        pe.wait_ge(evac, i * S * EV + 3 * S + s + 1)
                        mm(k.bank[2 * s + 1][:, L:2 * L], w["q0_wv"][:], ctx_wo[s][:], start=True, stop=True).then_inc(tr, 1)
                    for s in range(S):
                        a = k.bank[2 * s]
                        pe.wait_ge(spec_r, i * S + s + 1)
                        mm(a[:, 0:L], spec[s][:, 0, :], w["idft"][:, 0, :], start=True, stop=False)
                        mm(a[:, 0:L], spec[s][:, 1, :], w["idft"][:, 1, :], start=False, stop=True).then_inc(tr, 1)
                    for s in range(S):
                        pe.wait_ge(mix_r, i * S + s + 1)
                        pe.wait_ge(evac, i * S * EV + 4 * S + s + 1)
                        mm(k.bank[2 * s + 1][:], mix[s][:], w["spread_rows"][:], start=True, stop=True).then_inc(tr, 1)
                    for s in range(S):
                        pe.wait_ge(evac, i * S * EV + 5 * S + s + 1)
                        for t in range(T2):
                            for half in range(2):
                                ins = mm(k.bank[2 * s][:, L + t * P:L + (t + 1) * P], spread[s][:, 2 * t + half, :], val_wo[s][:, half * P:(half + 1) * P],
                                         start=(half == 0), stop=(half == 1))
                        ins.then_inc(tr, 1)




def stage_ternary_ffn(k):
    nc, w, S = k.nc, k.w, 4
    TURNS, HID = NT // S, 512
    with ExitStack() as local:
        sb = lambda n, s, d=F32: [k.sb(f"tf_{n}{j}", s, d, local) for j in range(S)]
        six, two, rstd, xn = sb("six", [P, 1, 6]), sb("two", [P, 1, 2]), sb("rstd", [P, 1]), sb("xn", [P, P])
        am, up_scale, xr, xq, xqT = sb("am", [P, 4]), sb("us", [P, 4]), sb("xr", [P, P]), sb("xq", [P, P], BF16), sb("xqT", [P, P], BF16)
        g, h, hq, hqT = sb("g", [P, HID]), sb("h", [P, HID]), sb("hq", [P, HID], BF16), sb("hqT", [P, 4, P], BF16)
        sem = lambda n: k.sem("tf_" + n)
        stats, rs, n0 = k.norms(NT)
        xq_r, scaled, pe_r, ev, act_r, done = (sem(n) for n in ("xq", "scaled", "pe", "evac", "silu", "done"))
        hq_r = sem("hq")
        PE = 4
        with nc.Block() as block:
            @block.gpsimd
            def _(pool):
                with pool.Fori(0, TURNS) as i:
                    order = Order(k, pool, "pool", i, TURNS, S)
                    for s in range(S):
                        pool.wait_ge(stats, n0 + i * S + s + 1)
                        rstd_on_pool(k, order, two[s][:, 0, 1:2], rstd[s][:], 1).then_inc(rs, 1)
                    order.close()

            def scale_of(order, src, a):
                order.mark(nc.vector.tensor_reduce(a[:, 0:1], src, AX.X, ALU.max, apply_absolute_value=True))
                order.settle()
                order.mark(nc.vector.tensor_scalar(a[:, 2:3], a[:, 0:1], EPS, 1.0 / 127, ALU.max, ALU.mult))
                order.settle()
                order.mark(nc.vector.reciprocal(a[:, 1:2], a[:, 2:3]))
                order.settle()

            def quantise(order, dst, src, a):
                order.mark(nc.vector.tensor_scalar(src, src, a[:, 1:2], ROUND, ALU.mult, ALU.add))
                order.settle()
                order.mark(nc.vector.tensor_scalar(src, src, -ROUND, 127.0, ALU.add, ALU.min))
                order.settle()
                return nc.vector.tensor_scalar(dst, src, -128.0, None, ALU.max)

            @block.vector
            def _(v):
                with v.Fori(0, TURNS) as i:
                    order = Order(k, v, "dve", i, TURNS, 14 * S)
                    for s in range(S):
                        ln_stats(k, order, k.x[:, bass.ds(i * S + s, 1), :], six[s], two[s], lambda ins: ins.then_inc(stats, 1))
                    for s in range(S):
                        v.wait_ge(rs, n0 + i * S + s + 1)
                        order.mark(nc.vector.tensor_scalar(xn[s][:], flat(k.x[:, bass.ds(i * S + s, 1), :]), two[s][:, 0, 0:1], rstd[s][:, 0:1], ALU.subtract, ALU.mult))
                        order.settle()
                        scale_of(order, xn[s][:], am[s])
                        quantise(order, xq[s][:], xn[s][:], am[s]).then_inc(xq_r, 1)
                    for s in range(S):
                        nc.vector.tensor_scalar(up_scale[s][:, 0:1], am[s][:, 2:3], w["scale_gate"][:, 0:1], None, ALU.mult)
                        nc.vector.tensor_scalar(up_scale[s][:, 1:2], am[s][:, 2:3], w["scale_up"][:, 0:1], None, ALU.mult).then_inc(scaled, 1)
                    for s in range(S):
                        v.wait_ge(act_r, i * S + s + 1)
                        v.wait_ge(pe_r, i * S * PE + S + s + 1)
                        v.wait_ge(scaled, i * S + s + 1)
                        order.mark(nc.vector.scalar_tensor_tensor(h[s][:], k.bank[2 * s + 1][:], up_scale[s][:, 1:2], g[s][:], ALU.mult, ALU.mult))
                        order.settle()
                        scale_of(order, h[s][:], am[s])
                        quantise(order, hq[s][:], h[s][:], am[s]).then_inc(hq_r, 1)
                    for s in range(S):
                        order.mark(nc.vector.tensor_scalar(am[s][:, 3:4], am[s][:, 2:3], w["scale_down"][:, 0:1], None, ALU.mult))
                    order.settle()
                    for s in range(S):
                        v.wait_ge(pe_r, i * S * PE + 3 * S + s + 1)
                        xs = flat(k.x[:, bass.ds(i * S + s, 1), :])
                        nc.vector.scalar_tensor_tensor(xs, k.bank[2 * s + 1][:, 0:P], am[s][:, 3:4], xs, ALU.mult, ALU.add).then_inc(done, 1)
                    order.close()

            @block.scalar
            def _(act):
                with act.Fori(0, TURNS) as i:
                    for s in range(S):
                        act.wait_ge(pe_r, i * S * PE + s + 1)
                        nc.scalar.copy(xqT[s][:], k.bank[2 * s][:].bitcast(BF16)[:, 0:P]).then_inc(ev, 1)
                    for s in range(S):
                        act.wait_ge(pe_r, i * S * PE + S + s + 1)
                        act.wait_ge(scaled, i * S + s + 1)
                        nc.scalar.activation(g[s][:], k.bank[2 * s][:], ACT.Silu, scale=up_scale[s][:, 0:1]).then_inc(act_r, 1)
                    for s in range(S):
                        act.wait_ge(pe_r, i * S * PE + 2 * S + s + 1)
                        nc.scalar.copy(flat(hqT[s][:]), k.bank[2 * s][:].bitcast(BF16)[:, 0:HID]).then_inc(ev, 1)

            @block.tensor
            def _(pe):
                mm = nc.tensor.matmul
                with pe.Fori(0, TURNS) as i:
                    for s in range(S):
                        pe.wait_ge(xq_r, i * S + s + 1)
                        nc.tensor.transpose(k.bank[2 * s][:].bitcast(BF16)[:, 0:P], xq[s][:], w["ident_bf"][:]).then_inc(pe_r, 1)
                    for s in range(S):
                        pe.wait_ge(ev, i * S * 2 + s + 1)
                        mm(k.bank[2 * s][:], xqT[s][:], w["tern_gate"][:], start=True, stop=True)
                        mm(k.bank[2 * s + 1][:], xqT[s][:], w["tern_up"][:], start=True, stop=True).then_inc(pe_r, 1)
                    for s in range(S):
                        pe.wait_ge(hq_r, i * S + s + 1)
                        for c in range(4):
                            ins = nc.tensor.transpose(k.bank[2 * s][:].bitcast(BF16)[:, c * P:(c + 1) * P], hq[s][:, c * P:(c + 1) * P], w["ident_bf"][:])
                        ins.then_inc(pe_r, 1)
                    for s in range(S):
                        pe.wait_ge(ev, i * S * 2 + S + s + 1)
                        for c in range(4):
                            ins = mm(k.bank[2 * s + 1][:, 0:P], hqT[s][:, c, :], w["tern_down"][:, c * P:(c + 1) * P], start=(c == 0), stop=(c == 3))
                        ins.then_inc(pe_r, 1)


def stage_fourier(k):
    nc, w, S = k.nc, k.w, 4
    TURNS = B // S
    with ExitStack() as local:
        sb = lambda n, s, d=F32: [k.sb(f"fo_{n}{j}", s, d, local) for j in range(S)]
        six, two, rstd, xn, xnT = sb("six", [P, T2, 6]), sb("two", [P, T2, 2]), sb("rstd", [P, T2]), sb("xn", [P, T2, P]), sb("xnT", [P, L])
        sem = lambda n: k.sem("fo_" + n)
        stats, rs, n0 = k.norms(B)
        xn_r, pe_r, ev, done = (sem(n) for n in ("xn", "pe", "evac", "done"))
        with nc.Block() as block:
            @block.gpsimd
            def _(pool):
                with pool.Fori(0, TURNS) as i:
                    order = Order(k, pool, "pool", i, TURNS, S)
                    for s in range(S):
                        pool.wait_ge(stats, n0 + i * S + s + 1)
                        rstd_on_pool(k, order, two[s][:, :, 1], rstd[s][:], T2).then_inc(rs, 1)
                    order.close()

            @block.vector
            def _(v):
                with v.Fori(0, TURNS) as i:
                    order = Order(k, v, "dve", i, TURNS, 2 * S)
                    for s in range(S):
                        ln_stats(k, order, k.x[:, bass.ds((i * S + s) * T2, T2), :], six[s], two[s], lambda ins: ins.then_inc(stats, 1))
                    for s in range(S):
                        v.wait_ge(rs, n0 + i * S + s + 1)
                        for t in range(T2):
                            ins = nc.vector.tensor_scalar(xn[s][:, t, :], flat(k.x[:, bass.ds((i * S + s) * T2 + t, 1), :]),
                                                          two[s][:, t, 0:1], rstd[s][:, t:t + 1], ALU.subtract, ALU.mult)
                        ins.then_inc(xn_r, 1)
                    for s in range(S):
                        xs = k.x[:, bass.ds((i * S + s) * T2, T2), :]
                        v.wait_ge(xn_r, i * S + s + 1)
                        order.mark(nc.vector.tensor_tensor(xs, xs, w["L2_bias"][:].unsqueeze(1).to_broadcast([P, T2, P]), ALU.add))
                        order.settle()
                        v.wait_ge(pe_r, i * S * 2 + S + s + 1)
                        nc.vector.tensor_tensor(xs, xs, k.bank[2 * s + 1][:, 0:L].rearrange("p (t d) -> p t d", t=T2), ALU.add).then_inc(done, 1)
                    order.close()

            @block.scalar
            def _(act):
                with act.Fori(0, TURNS) as i:
                    for s in range(S):
                        act.wait_ge(pe_r, i * S * 2 + s + 1)
                        nc.scalar.copy(xnT[s][:], k.bank[2 * s][:, 0:L]).then_inc(ev, 1)

            @block.tensor
            def _(pe):
                with pe.Fori(0, TURNS) as i:
                    for s in range(S):
                        pe.wait_ge(xn_r, i * S + s + 1)
                        for t in range(T2):
                            ins = nc.tensor.transpose(k.bank[2 * s][:, t * P:(t + 1) * P], xn[s][:, t, :], w["ident"][:])
                        ins.then_inc(pe_r, 1)
                    for s in range(S):
                        pe.wait_ge(ev, i * S + s + 1)
                        for t in range(T2):
                            ins = nc.tensor.matmul(k.bank[2 * s + 1][:, t * P:(t + 1) * P], xnT[s][:, t * P:(t + 1) * P], w["fourier"][:], start=True, stop=True)
                        ins.then_inc(pe_r, 1)


def stage_causal_attention(k):
    nc, w, S = k.nc, k.w, 2
    TURNS, H, D = B // S, 16, 64
    PAIRS, SCALE = H // 2, 64 ** -0.5
    NS, NP = 3, 2
    with ExitStack() as local:
        sb = lambda n, s, d=F32, c=S: [k.sb(f"ca_{n}{j}", s, d, local) for j in range(c)]
        ctxT, six, two, rstd = sb("ctxT", [P, L]), sb("six", [P, T2, 6]), sb("two", [P, T2, 2]), sb("rstd", [P, T2])
        xn, xnT = sb("xn", [P, T2, P]), sb("xnT", [P, L])
        q, kk, val, heads = sb("q", [P, H, L]), sb("k", [P, PAIRS, L]), sb("v", [P, T2, H * D]), sb("heads", [P, PAIRS, L])
        bar, ln1, z, zc = sb("bar", [P, 3 * P]), sb("len", [P, 1]), sb("z", [P, 1]), sb("zc", [P, 1])
        nz = sb("nz", [P, 1])
        sm, mx, nmx, den = sb("sm", [P, 3 * P], c=NS), sb("mx", [P, 2], c=NS), sb("nmx", [P, 2], c=NS), sb("den", [P, 2], c=NS)
        rden, prob = sb("rden", [P, 2], c=NS), sb("prob", [P, 3 * P], c=NS)
        pT = sb("pT", [P, 4 * P], c=NP * S)
        sem = lambda n: k.sem("ca_" + n)
        ctx_in = [sem(f"ctx_in{j}") for j in range(S)]
        stats, rs, n0 = k.norms(B)
        xn_r, tr_x, x_ev, proj, pev, vev = (sem(n) for n in ("xn", "xnT_ps", "xnT", "proj", "qk", "v"))
        bar_r, s_ps, s_sm, ex, rd, nrm, t_ps, t_ev, o_ps, o_ev, y_ps, done = (
            sem(n) for n in ("bar", "scores", "masked", "exp", "rden", "norm", "pT_ps", "pT", "o_ps", "heads", "y_ps", "done"))
        v_ps, kev = sem("v_ps"), sem("kev")
        HS = S * H
        NPROJ = 2 * PAIRS

        with nc.Block() as block:
            @block.sync
            def _(sp):
                with sp.Fori(0, TURNS) as i:
                    for s in range(S):
                        n = i * S + s
                        sp.wait_ge(done, n + 1)
                        sp.dma_start(ctxT[s][:], k.d["ctxT"][bass.ds(n, 1)].rearrange("b d l -> (b d) l")).then_inc(ctx_in[s], 16)

            @block.gpsimd
            def _(pool):
                with pool.Fori(0, TURNS) as i:
                    order = Order(k, pool, "pool", i, TURNS, S)
                    for s in range(S):
                        pool.wait_ge(stats, n0 + i * S + s + 1)
                        rstd_on_pool(k, order, two[s][:, :, 1], rstd[s][:], T2).then_inc(rs, 1)
                    for g in range(HS):
                        s, m = g // H, g % NS
                        pool.wait_ge(rd, i * HS + g + 1)
                        k.carry(pool)
                        nc.gpsimd.tensor_scalar(prob[m][:, 0:P], prob[m][:, 0:P], rden[m][:, 0:1], zc[s][:, 0:1], ALU.mult, ALU.add)
                        nc.gpsimd.tensor_scalar(prob[m][:, P:3 * P], prob[m][:, P:3 * P], rden[m][:, 1:2], zc[s][:, 0:1], ALU.mult, ALU.add).then_inc(nrm, 1)
                    order.close()

            def head_sum(v, order, i, g):
                s, m = g // H, g % NS
                v.wait_ge(ex, i * HS + g + 1)
                order.mark(nc.vector.reciprocal(rden[m][:], den[m][:]))
                order.settle()
                nc.vector.tensor_scalar(rden[m][:], rden[m][:], nz[s][:, 0:1], None, ALU.mult).then_inc(rd, 1)

            @block.vector
            def _(v):
                v.sem_inc(done, S)
                with v.Fori(0, TURNS) as i:
                    order = Order(k, v, "dve", i, TURNS, 5 * S + 2 * HS)
                    for s in range(S):
                        ln_stats(k, order, k.x[:, bass.ds((i * S + s) * T2, T2), :], six[s], two[s], lambda ins: ins.then_inc(stats, 1))
                    for s in range(S):
                        v.wait_ge(rs, n0 + i * S + s + 1)
                        for t in range(T2):
                            ins = nc.vector.tensor_scalar(xn[s][:, t, :], flat(k.x[:, bass.ds((i * S + s) * T2 + t, 1), :]),
                                                          two[s][:, t, 0:1], rstd[s][:, t:t + 1], ALU.subtract, ALU.mult)
                        ins.then_inc(xn_r, 1)
                    for s in range(S):
                        order.mark(nc.vector.tensor_copy(ln1[s][:], w["lens"][:, bass.ds(i * S + s, 1)]))
                    order.settle()
                    for s in range(S):
                        nc.vector.tensor_scalar(z[s][:], ln1[s][:], 0.0, None, ALU.is_le)
                        order.mark(nc.vector.tensor_scalar(bar[s][:], w["iota_k"][:], ln1[s][:, 0:1], NEG, ALU.is_ge, ALU.mult))
                    order.settle()
                    for s in range(S):
                        nc.vector.tensor_scalar(nz[s][:], z[s][:], -1.0, 1.0, ALU.mult, ALU.add)
                        nc.vector.tensor_scalar(zc[s][:], z[s][:], 1.0 / L, None, ALU.mult)
                        order.mark(nc.vector.tensor_tensor(bar[s][:], bar[s][:], w["causal"][:], ALU.add))
                    order.settle()
                    for s in range(S):
                        for r in range(NP):
                            ins = nc.vector.tensor_scalar(pT[s * NP + r][:, 0:P], w["ident"][:], 0.0, zc[s][:, 0:1], ALU.mult, ALU.add)
                        ins.then_inc(bar_r, 1)
                    for s in range(S):
                        for t in range(T2):
                            for c in range(2):
                                j = (s * T2 + t) * 2 + c
                                v.wait_ge(v_ps, i * S * 4 + j + 1)
                                nc.vector.tensor_copy(val[s][:, t, c * 512:(c + 1) * 512], k.bank[j % 2][:]).then_inc(vev, 1)
                    for s in range(S):
                        for p in range(PAIRS):
                            v.wait_ge(proj, i * S * NPROJ + s * NPROJ + 2 * p + 1)
                            for o in range(2):
                                ins = nc.vector.tensor_scalar(q[s][:, 2 * p + o, :], k.bank[2 * (p % 2)][:, 0:L], w["L1_bQ"][:, p:p + 1], w["head_pick"][:, o:o + 1], ALU.add, ALU.mult)
                            ins.then_inc(pev, 1)
                    for g in range(HS):
                        s, m = g // H, g % NS
                        v.wait_ge(s_ps, i * HS + g + 1)
                        if g >= NS:
                            v.wait_ge(ex, i * HS + g - NS + 1)
                        k.carry(v)
                        for a, b, j in ((0, P, 0), (P, 3 * P, 1)):
                            ins = nc.vector.tensor_tensor_reduce(out=sm[m][:, a:b], in0=k.bank[2 + m][:, a:b], in1=bar[s][:, a:b], scale=1.0, scalar=2 * NEG,
                                                                 op0=ALU.add, op1=ALU.max, accum_out=mx[m][:, j:j + 1])
                        order.mark(ins)
                        order.settle()
                        nc.vector.tensor_scalar(nmx[m][:], mx[m][:], -SCALE, None, ALU.mult).then_inc(s_sm, 1)
                        if g >= 1:
                            head_sum(v, order, i, g - 1)
                    head_sum(v, order, i, HS - 1)
                    for s in range(S):
                        xs = k.x[:, bass.ds((i * S + s) * T2, T2), :]
                        order.mark(nc.vector.tensor_tensor(xs, xs, w["L1_bO"][:].unsqueeze(1).to_broadcast([P, T2, P]), ALU.add))
                        order.settle()
                        v.wait_ge(y_ps, i * S + s + 1)
                        nc.vector.tensor_tensor(xs, xs, k.bank[s][:, 0:L].rearrange("p (t d) -> p t d", t=T2), ALU.add).then_inc(done, 1)
                    order.close()

            def head_out(act, i, pr):
                act.wait_ge(o_ps, i * HS + 2 * pr + 2)
                nc.scalar.activation(heads[pr // PAIRS][:, pr % PAIRS, :], k.bank[(7, 1)[pr % 2]][:, 0:L], ACT.Identity,
                                     bias=w["L1_bV"][:, pr % PAIRS:pr % PAIRS + 1]).then_inc(o_ev, 1)

            @block.scalar
            def _(act):
                with act.Fori(0, TURNS) as i:
                    for s in range(S):
                        act.wait_ge(tr_x, i * S + s + 1)
                        nc.scalar.copy(xnT[s][:], k.bank[s][:, 0:L]).then_inc(x_ev, 1)
                    for s in range(S):
                        for p in range(PAIRS):
                            act.wait_ge(proj, i * S * NPROJ + s * NPROJ + 2 * p + 2)
                            nc.scalar.activation(kk[s][:, p, :], k.bank[2 * (p % 2) + 1][:, 0:L], ACT.Identity, bias=w["L1_bK"][:, p:p + 1]).then_inc(kev, 1)
                    for g in range(HS + 1):
                        if g < HS:
                            m = g % NS
                            act.wait_ge(s_sm, i * HS + g + 1)
                            if g >= NS:
                                act.wait_ge(t_ps, i * HS + g - NS + 1)
                            nc.scalar.activation(prob[m][:, 0:P], sm[m][:, 0:P], ACT.Exp, bias=nmx[m][:, 0:1], scale=SCALE, accum_out=den[m][:, 0:1])
                            nc.scalar.activation(prob[m][:, P:3 * P], sm[m][:, P:3 * P], ACT.Exp, bias=nmx[m][:, 1:2], scale=SCALE, accum_out=den[m][:, 1:2]).then_inc(ex, 1)
                        if g >= 1:
                            h, r = g - 1, (g - 1) // H * NP + (g - 1) % NP
                            act.wait_ge(t_ps, i * HS + h + 1)
                            if h >= NP:
                                act.wait_ge(o_ps, i * HS + h - NP + 1)
                            nc.scalar.copy(pT[r][:, P:4 * P], k.bank[5 + h % NP][:, 0:3 * P]).then_inc(t_ev, 1)
                            if h >= 3 and (h - 2) % 2 == 1:
                                head_out(act, i, (h - 3) // 2)
                    head_out(act, i, HS // 2 - 1)

            @block.tensor
            def _(pe):
                mm = nc.tensor.matmul
                with pe.Fori(0, TURNS) as i:
                    for s in range(S):
                        pe.wait_ge(xn_r, i * S + s + 1)
                        for t in range(T2):
                            ins = nc.tensor.transpose(k.bank[s][:, t * P:(t + 1) * P], xn[s][:, t, :], w["ident"][:])
                        ins.then_inc(tr_x, 1)
                    pe.wait_ge(x_ev, i * S + S)
                    for s in range(S):
                        pe.wait_ge(ctx_in[s], i * 16 + 16)
                        for t in range(T2):
                            for c in range(2):
                                j = (s * T2 + t) * 2 + c
                                if j >= 2:
                                    pe.wait_ge(vev, i * S * 4 + j - 1)
                                mm(k.bank[j % 2][:], ctxT[s][:, t * P:(t + 1) * P], w["L1_WV"][:, c * 512:(c + 1) * 512], start=True, stop=True).then_inc(v_ps, 1)
                    for s in range(S):
                        for p in range(PAIRS):
                            a, done_q = s * PAIRS + p, i * S * PAIRS + s * PAIRS + p
                            if a == 0:
                                pe.wait_ge(vev, (i + 1) * S * 4)
                            if a >= 2:
                                pe.wait_ge(pev, done_q - 1)
                                pe.wait_ge(kev, done_q - 1)
                            mm(k.bank[2 * (p % 2)][:, 0:L], w["L1_WQ"][:, p * P:(p + 1) * P], xnT[s][:], start=True, stop=True).then_inc(proj, 1)
                            mm(k.bank[2 * (p % 2) + 1][:, 0:L], w["L1_WK"][:, p * P:(p + 1) * P], ctxT[s][:], start=True, stop=True).then_inc(proj, 1)
                    pe.wait_ge(pev, (i + 1) * S * PAIRS)
                    pe.wait_ge(kev, (i + 1) * S * PAIRS)
                    for g in range(HS + 3):
                        if g < HS:
                            s, h, bank = g // H, g % H, k.bank[2 + g % NS]
                            if g >= NS:
                                pe.wait_ge(s_sm, i * HS + g - NS + 1)
                            mm(bank[:, 0:P], q[s][:, h, 0:P], kk[s][:, h // 2, 0:P], start=True, stop=True)
                            mm(bank[:, P:3 * P], q[s][:, h, P:2 * P], kk[s][:, h // 2, :], start=True, stop=True).then_inc(s_ps, 1)
                        if 2 <= g < HS + 2:
                            u = g - 2
                            pe.wait_ge(nrm, i * HS + u + 1)
                            if u >= NP:
                                pe.wait_ge(t_ev, i * HS + u - NP + 1)
                            for c in range(3):
                                ins = nc.tensor.transpose(k.bank[5 + u % NP][:, c * P:(c + 1) * P], prob[u % NS][:, c * P:(c + 1) * P], w["ident"][:])
                            ins.then_inc(t_ps, 1)
                        if g >= 3:
                            u = g - 3
                            s, h, pr = u // H, u % H, u // 2
                            pe.wait_ge(t_ev, i * HS + u + 1)
                            if h == 0:
                                pe.wait_ge(bar_r, i * S + s + 1)
                            if h % 2 == 0 and pr >= 2:
                                pe.wait_ge(o_ev, i * PAIRS * S + pr - 1)
                            o = k.bank[(7, 1)[pr % 2]][(h % 2) * D:(h % 2 + 1) * D, 0:L]
                            r = pT[s * NP + u % NP]
                            mm(o, val[s][:, 0, h * D:(h + 1) * D], r[:, P:3 * P], start=True, stop=False)
                            mm(o.rearrange("p (a b) -> p a b", a=2), val[s][:, 1, h * D:(h + 1) * D], r[:].rearrange("p (a b) -> p a b", b=P)[:, 0:4:3, :],
                               start=False, stop=True).then_inc(o_ps, 1)
                    for s in range(S):
                        pe.wait_ge(o_ev, i * PAIRS * S + (s + 1) * PAIRS)
                        for t in range(T2):
                            for p in range(PAIRS):
                                ins = mm(k.bank[s][:, t * P:(t + 1) * P], heads[s][:, p, t * P:(t + 1) * P], w["L1_WO"][:, p, :], start=(p == 0), stop=(p == PAIRS - 1))
                        ins.then_inc(y_ps, 1)


def stage_experts(k, tag, first, second, act_fn, shared, top, bias):
    nc, w, T = k.nc, k.w, 4
    TURNS, N, RE = NT // T, T * P, 8
    E = RE + shared
    NU, ND = 3, 2
    with ExitStack() as local:
        sb = lambda n, s, d=F32, c=None: (k.sb(f"{tag}_{n}", s, d, local) if c is None else [k.sb(f"{tag}_{n}{j}", s, d, local) for j in range(c)])
        six, two, rstd, sq = sb("six", [P, T, 6]), sb("two", [P, T, 2]), sb("rstd", [P, T]), sb("sq", [P, T])
        r2, un = sb("r2", [P, T]), sb("un", [P, T, P] if bias else [P, T, 1])
        back, xn, xT = sb("back", [P, T]), sb("xn", [P, T, P]), sb("xT", [P, N])
        xin = [sb("xs", [P, N]), sb("xr", [P, N])] if bias else [xT, xT]
        h = sb("h", [P, 4, N], c=2)
        logit, mx, val = sb("logit", [P, T, RE]), sb("mx", [P, T]), sb("val", [P, T, RE])
        above, tie, rank = sb("above", [P, T, RE * RE]), sb("tie", [P, T, RE * RE]), sb("rank", [P, T, RE])
        den, gate, gateT = sb("den", [P, T]), sb("gate", [P, T, E]), sb("gateT", [E, N])
        sem = lambda n: k.sem(f"{tag}_" + n)
        stats, rs, n0 = k.norms(TURNS)
        xn_r, pe_r, ev, dev, soft, gate_r = (sem(n) for n in ("xn", "front_ps", "evac", "gains", "soft", "gate"))
        up_ps, act_r, dn_ps, done = sem("up_ps"), sem("hidden"), sem("down_ps"), sem("done")
        FRONT = 3 if bias else 2
        with nc.Block() as block:
            @block.gpsimd
            def _(pool):
                with pool.Fori(0, TURNS) as i:
                    order = Order(k, pool, "pool", i, TURNS, 5 if bias else 1)
                    pool.wait_ge(stats, n0 + i + 1)
                    ins = rstd_on_pool(k, order, two[:, :, 1], rstd[:], T)
                    if bias:
                        for factor in (two[:, :, 1], sq[:]):
                            order.mark(ins)
                            order.settle()
                            ins = nc.gpsimd.tensor_tensor(sq[:], factor, rstd[:], ALU.mult)
                        order.mark(ins)
                        order.settle()
                        ins = rstd_on_pool(k, order, sq[:], r2[:], T, EPS_RMS)
                    ins.then_inc(rs, 1)
                    order.close()

            @block.vector
            def _(v):
                tt, ts = nc.vector.tensor_tensor, nc.vector.tensor_scalar
                if bias:
                    nc.vector.memset(gate[:], 1.0)
                v.wait_ge(k.big_loaded, 32)
                with v.Fori(0, TURNS) as i:
                    order = Order(k, v, "dve", i, TURNS, 13 if bias else 10)
                    xs = k.x[:, bass.ds(i * T, T), :]
                    ln_stats(k, order, xs, six, two, lambda ins: ins.then_inc(stats, 1))
                    v.wait_ge(rs, n0 + i + 1)
                    normed = un if bias else xn
                    for t in range(T):
                        ins = ts(normed[:, t, :], flat(k.x[:, bass.ds(i * T + t, 1), :]), two[:, t, 0:1], rstd[:, t:t + 1], ALU.subtract, ALU.mult)
                    if bias:
                        order.mark(ins)
                        order.settle()
                        tt(xs, xs, un[:], ALU.add)
                        for t in range(T):
                            ins = ts(xn[:, t, :], un[:, t, :], r2[:, t:t + 1], None, ALU.mult)
                    ins.then_inc(xn_r, 1)
                    if bias:
                        order.mark(nc.vector.reciprocal(back[:], r2[:]))
                        order.settle()
                        ts(back[:], back[:], -1.0, None, ALU.mult).then_inc(gate_r, 1)
                        v.wait_ge(pe_r, i * FRONT + 1)
                        v.wait_ge(ev, i + 1)
                        ts(xin[0][:], k.bank[0][:], w["L3_g"][:, 0:1], None, ALU.mult)
                        ts(xin[1][:], k.bank[0][:], w["L3_g"][:, 1:2], None, ALU.mult).then_inc(dev, 1)
                        v.wait_ge(soft, i + 1)
                        order.mark(ts(val[:], val[:], 1.0, None, ALU.add))
                        order.settle()
                        order.mark(nc.vector.reciprocal(val[:], val[:]))
                        order.settle()
                    else:
                        v.wait_ge(pe_r, i * FRONT + 2)
                        lg = k.bank[1][:, 0:T * RE].rearrange("p (t e) -> p t e", t=T)
                        order.mark(nc.vector.tensor_reduce(mx[:], lg, AX.X, ALU.max))
                        order.settle()
                        tt(logit[:], lg, mx[:].unsqueeze(2).to_broadcast([P, T, RE]), ALU.subtract).then_inc(dev, 1)
                        v.wait_ge(soft, i + 1)
                    mine = val[:].unsqueeze(3).to_broadcast([P, T, RE, RE])
                    other = val[:].unsqueeze(2).to_broadcast([P, T, RE, RE])
                    grid = lambda x: x[:].rearrange("p t (e j) -> p t e j", e=RE)
                    tt(grid(above), other, mine, ALU.is_gt)
                    order.mark(tt(grid(tie), other, mine, ALU.is_equal))
                    order.settle()
                    order.mark(tt(tie[:], tie[:], w["prefix"][:].rearrange("p a b -> p (a b)").unsqueeze(1).to_broadcast([P, T, RE * RE]), ALU.mult))
                    order.settle()
                    order.mark(tt(above[:], above[:], tie[:], ALU.add))
                    order.settle()
                    order.mark(nc.vector.tensor_reduce(rank[:], grid(above), AX.X, ALU.add))
                    order.settle()
                    order.mark(ts(rank[:], rank[:], float(top), None, ALU.is_lt))
                    order.settle()
                    order.mark(tt(rank[:], rank[:], val[:], ALU.mult))
                    order.settle()
                    order.mark(nc.vector.tensor_reduce(den[:], val[:] if bias else rank[:], AX.X, ALU.add))
                    order.settle()
                    order.mark(nc.vector.reciprocal(den[:], den[:]))
                    order.settle()
                    ins = tt(gate[:, :, shared:E], rank[:], den[:].unsqueeze(2).to_broadcast([P, T, RE]), ALU.mult)
                    ins.then_inc(gate_r, 1)
                    v.wait_ge(gate_r, (i + 1) * (2 if bias else 1))
                    if bias:
                        v.wait_ge(pe_r, i * FRONT + 3)
                        nc.vector.tensor_copy(gateT[:], k.bank[1][0:E, 0:N]).then_inc(dev, 1)
                    for e in range(E):
                        v.wait_ge(dn_ps, i * E + e + 1)
                        for t in range(T):
                            xt = flat(k.x[:, bass.ds(i * T + t, 1), :])
                            ins = nc.vector.scalar_tensor_tensor(xt, k.bank[4 + e % ND][:, t * P:(t + 1) * P], gate[:, t, e:e + 1], xt, ALU.mult, ALU.add)
                        ins.then_inc(done, 1)
                        v.wait_ge(done, i * E + e + 1)
                    order.close()

            @block.scalar
            def _(act):
                with act.Fori(0, TURNS) as i:
                    act.wait_ge(pe_r, i * FRONT + 1)
                    nc.scalar.copy(xT[:], k.bank[0][:]).then_inc(ev, 1)
                    if bias:
                        act.wait_ge(pe_r, i * FRONT + 2)
                        act.wait_ge(gate_r, i * 2 + 1)
                        for t in range(T):
                            ins = nc.scalar.activation(val[:, t, :], k.bank[1][:, t * RE:(t + 1) * RE], ACT.Exp, scale=back[:, t:t + 1])
                        ins.then_inc(soft, 1)
                    else:
                        act.wait_ge(dev, i + 1)
                        nc.scalar.activation(val[:], logit[:], ACT.Exp).then_inc(soft, 1)
                    for e in range(E):
                        for c in range(4):
                            u = e * 4 + c
                            act.wait_ge(up_ps, i * E * 4 + u + 1)
                            if c == 0 and e >= 2:
                                act.wait_ge(dn_ps, i * E + e - 1)
                            nc.scalar.activation(h[e % 2][:, c, :], k.bank[(2, 3, 6)[u % NU]][:], act_fn, bias=w["L3_b1"][:, u:u + 1] if bias else 0.0).then_inc(act_r, 1)

            def down(pe, i, e):
                if e >= ND:
                    pe.wait_ge(done, i * E + e - ND + 1)
                pe.wait_ge(act_r, i * E * 4 + e * 4 + 4)
                if bias and e == 0:
                    pe.wait_ge(dev, i * 2 + 2)
                for t in range(T):
                    o = k.bank[4 + e % ND][:, t * P:(t + 1) * P]
                    for c in range(4):
                        ins = nc.tensor.matmul(o, h[e % 2][:, c, t * P:(t + 1) * P], second[:, e, c * P:(c + 1) * P], start=(c == 0), stop=(c == 3 and not (bias and e == 0)))
                    if bias and e == 0:
                        ins = nc.tensor.matmul(o, gateT[:, t * P:(t + 1) * P], w["L3_b2"][:], start=False, stop=True)
                ins.then_inc(dn_ps, 1)

            @block.tensor
            def _(pe):
                with pe.Fori(0, TURNS) as i:
                    pe.wait_ge(xn_r, i + 1)
                    for t in range(T):
                        ins = nc.tensor.transpose(k.bank[0][:, t * P:(t + 1) * P], xn[:, t, :], w["ident"][:])
                    ins.then_inc(pe_r, 1)
                    pe.wait_ge(ev, i + 1)
                    for t in range(T):
                        ins = nc.tensor.matmul(k.bank[1][:, t * RE:(t + 1) * RE], xT[:, t * P:(t + 1) * P], w["L3_centroids" if bias else "L1_router"][:], start=True, stop=True)
                    ins.then_inc(pe_r, 1)
                    if bias:
                        pe.wait_ge(dev, i * 2 + 1)
                    for e in range(E):
                        for c in range(4):
                            u = e * 4 + c
                            if u >= NU:
                                pe.wait_ge(act_r, i * E * 4 + u - NU + 1)
                            nc.tensor.matmul(k.bank[(2, 3, 6)[u % NU]][:], first[:, e, c * P:(c + 1) * P], xin[0 if e < shared else 1][:], start=True, stop=True).then_inc(up_ps, 1)
                        if bias and e == 0:
                            pe.wait_ge(gate_r, i * 2 + 2)
                            for t in range(T):
                                ins = nc.tensor.transpose(k.bank[1][0:E, t * P:(t + 1) * P], gate[:, t, :], w["ident"][:])
                            ins.then_inc(pe_r, 1)
                        if e >= 1:
                            down(pe, i, e - 1)
                    down(pe, i, E - 1)


def stage_load_last(k):
    k.layer1.close()
    for n in ("L3_W1", "L3_W2"):
        k.w[n] = k.sb("w_" + n, [P, 10, 512])
    k.last_loaded = k.sem("last_loaded")
    with k.nc.Block() as block:
        @block.sync
        def _(sp):
            for n in ("L3_W1", "L3_W2"):
                sp.dma_start(k.w[n][:], k.d[n]).then_inc(k.last_loaded, 16)


def stage_experts_gelu(k):
    stage_experts(k, "e1", k.w["up_w"], k.w["down_w"], ACT.Gelu_apprx_tanh, 0, 4, False)


def stage_experts_shared(k):
    with k.nc.Block() as block:
        @block.tensor
        def _(pe):
            pe.wait_ge(k.last_loaded, 32)
    stage_experts(k, "e3", k.w["L3_W1"], k.w["L3_W2"], ACT.Gelu, 2, 2, True)


def stage_self_attention(k):
    nc, w, S = k.nc, k.w, 4
    TURNS = B // S
    k.y = k.sb("y_stream", [P, NT, P], F32, k.layer2)
    with ExitStack() as local:
        sb = lambda n, s, d=F32: [k.sb(f"sa_{n}{j}", s, d, local) for j in range(S)]
        six, two, rstd, xn, xnT = sb("six", [P, T2, 6]), sb("two", [P, T2, 2]), sb("rstd", [P, T2]), sb("xn", [P, T2, P]), sb("xnT", [P, L])
        t = sb("t", [P, T2, P])
        sem = lambda n: k.sem("sa_" + n)
        stats, rs, n0 = k.norms(2 * B)
        xn_r, pe_r, ev = (sem(n) for n in ("xn", "pe", "evac"))
        with nc.Block() as block:
            @block.gpsimd
            def _(pool):
                with pool.Fori(0, TURNS) as i:
                    order = Order(k, pool, "pool", i, TURNS, 2 * S)
                    for part in range(2):
                        for s in range(S):
                            pool.wait_ge(stats, n0 + (i * 2 + part) * S + s + 1)
                            rstd_on_pool(k, order, two[s][:, :, 1], rstd[s][:], T2).then_inc(rs, 1)
                    order.close()

            @block.vector
            def _(v):
                with v.Fori(0, TURNS) as i:
                    order = Order(k, v, "dve", i, TURNS, 7 * S)
                    for s in range(S):
                        ln_stats(k, order, k.x[:, bass.ds((i * S + s) * T2, T2), :], six[s], two[s], lambda ins: ins.then_inc(stats, 1))
                    for s in range(S):
                        v.wait_ge(rs, n0 + i * 2 * S + s + 1)
                        for j in range(T2):
                            ins = nc.vector.tensor_scalar(xn[s][:, j, :], flat(k.x[:, bass.ds((i * S + s) * T2 + j, 1), :]),
                                                          two[s][:, j, 0:1], rstd[s][:, j:j + 1], ALU.subtract, ALU.mult)
                        ins.then_inc(xn_r, 1)
                    for s in range(S):
                        v.wait_ge(xn_r, i * S + s + 1)
                        order.mark(nc.vector.tensor_tensor(t[s][:], xn[s][:], w["sa_bias"][:].unsqueeze(1).to_broadcast([P, T2, P]), ALU.add))
                        order.settle()
                        v.wait_ge(pe_r, i * S * 2 + S + s + 1)
                        order.mark(nc.vector.tensor_tensor(t[s][:], t[s][:], k.bank[2 * s + 1][:, 0:L].rearrange("p (t d) -> p t d", t=T2), ALU.add))
                        order.settle()
                        ln_stats(k, order, t[s], six[s], two[s], lambda ins: ins.then_inc(stats, 1))
                    for s in range(S):
                        v.wait_ge(rs, n0 + (i * 2 + 1) * S + s + 1)
                        apply_gain(k, order, t[s], two[s], rstd[s], w["L2_vecs"][:, 1, :], w["L2_vecs"][:, 2, :], k.y[:, bass.ds((i * S + s) * T2, T2), :])
                    order.close()

            @block.scalar
            def _(act):
                with act.Fori(0, TURNS) as i:
                    for s in range(S):
                        act.wait_ge(pe_r, i * S * 2 + s + 1)
                        nc.scalar.copy(xnT[s][:], k.bank[2 * s][:, 0:L]).then_inc(ev, 1)

            @block.tensor
            def _(pe):
                with pe.Fori(0, TURNS) as i:
                    for s in range(S):
                        pe.wait_ge(xn_r, i * S + s + 1)
                        for j in range(T2):
                            ins = nc.tensor.transpose(k.bank[2 * s][:, j * P:(j + 1) * P], xn[s][:, j, :], w["ident"][:])
                        ins.then_inc(pe_r, 1)
                    for s in range(S):
                        pe.wait_ge(ev, i * S + s + 1)
                        for j in range(T2):
                            ins = nc.tensor.matmul(k.bank[2 * s + 1][:, j * P:(j + 1) * P], xnT[s][:, j * P:(j + 1) * P], w["sa"][:], start=True, stop=True)
                        ins.then_inc(pe_r, 1)


def apply_gain(k, order, t, two, rstd, gain, offset, dst):
    nc = k.nc
    for j in range(T2):
        ins = nc.vector.tensor_scalar(t[:, j, :], t[:, j, :], two[:, j, 0:1], rstd[:, j:j + 1], ALU.subtract, ALU.mult)
    order.mark(ins)
    order.settle()
    order.mark(nc.vector.tensor_tensor(t[:], t[:], gain.unsqueeze(1).to_broadcast([P, T2, P]), ALU.mult))
    order.settle()
    return order.mark(nc.vector.tensor_tensor(dst, t[:], offset.unsqueeze(1).to_broadcast([P, T2, P]), ALU.add))


def stage_relu_ffn(k):
    nc, w, S = k.nc, k.w, 4
    TURNS = B // S
    with ExitStack() as local:
        sb = lambda n, s, d=F32: [k.sb(f"rf_{n}{j}", s, d, local) for j in range(S)]
        six, two, rstd, yT = sb("six", [P, T2, 6]), sb("two", [P, T2, 2]), sb("rstd", [P, T2]), sb("yT", [P, L])
        t, y2, h = sb("t", [P, T2, P]), sb("y2", [P, T2, P]), sb("h", [P, 4, L])
        sem = lambda n: k.sem("rf_" + n)
        stats, rs, n0 = k.norms(2 * B)
        y_r, pe_r, ev = (sem(n) for n in ("y", "pe", "evac"))
        PE, EV = 4, 3
        with nc.Block() as block:
            @block.gpsimd
            def _(pool):
                with pool.Fori(0, TURNS) as i:
                    order = Order(k, pool, "pool", i, TURNS, 2 * S)
                    for part in range(2):
                        for s in range(S):
                            pool.wait_ge(stats, n0 + (i * 2 + part) * S + s + 1)
                            rstd_on_pool(k, order, two[s][:, :, 1], rstd[s][:], T2).then_inc(rs, 1)
                    order.close()

            @block.vector
            def _(v):
                with v.Fori(0, TURNS) as i:
                    order = Order(k, v, "dve", i, TURNS, 11 * S)
                    for s in range(S):
                        ys = k.y[:, bass.ds((i * S + s) * T2, T2), :]
                        order.mark(nc.vector.tensor_copy(t[s][:], ys))
                        order.settle()
                        ln_stats(k, order, t[s], six[s], two[s], lambda ins: ins.then_inc(stats, 1))
                    for s in range(S):
                        v.wait_ge(rs, n0 + i * 2 * S + s + 1)
                        apply_gain(k, order, t[s], two[s], rstd[s], w["L2_vecs"][:, 3, :], w["L2_vecs"][:, 4, :], y2[s][:])
                        order.settle()
                        nc.vector.tensor_tensor(t[s][:], y2[s][:], w["L2_vecs"][:, 5, :].unsqueeze(1).to_broadcast([P, T2, P]), ALU.add).then_inc(y_r, 1)
                    for s in range(S):
                        v.wait_ge(y_r, i * S + s + 1)
                        v.wait_ge(pe_r, i * S * PE + 3 * S + s + 1)
                        order.mark(nc.vector.tensor_tensor(t[s][:], t[s][:], k.bank[2 * s][:, L:2 * L].rearrange("p (t d) -> p t d", t=T2), ALU.add))
                        order.settle()
                        ln_stats(k, order, t[s], six[s], two[s], lambda ins: ins.then_inc(stats, 1))
                    for s in range(S):
                        v.wait_ge(rs, n0 + (i * 2 + 1) * S + s + 1)
                        apply_gain(k, order, t[s], two[s], rstd[s], w["L2_vecs"][:, 6, :], w["L2_vecs"][:, 7, :], y2[s][:])
                        order.settle()
                        xs = k.x[:, bass.ds((i * S + s) * T2, T2), :]
                        order.mark(nc.vector.tensor_tensor(xs, xs, y2[s][:], ALU.add))
                    order.close()

            @block.scalar
            def _(act):
                with act.Fori(0, TURNS) as i:
                    for s in range(S):
                        act.wait_ge(pe_r, i * S * PE + s + 1)
                        nc.scalar.copy(yT[s][:], k.bank[2 * s][:, 0:L]).then_inc(ev, 1)
                    for c in range(2):
                        for s in range(S):
                            act.wait_ge(pe_r, i * S * PE + (1 + c) * S + s + 1)
                            for m in range(2):
                                ins = nc.scalar.activation(h[s][:, 2 * c + m, :], k.bank[2 * s + 1][:, m * L:(m + 1) * L], ACT.Relu, bias=w["L2_lin1b"][:, 2 * c + m:2 * c + m + 1])
                            ins.then_inc(ev, 1)

            @block.tensor
            def _(pe):
                mm = nc.tensor.matmul
                with pe.Fori(0, TURNS) as i:
                    for s in range(S):
                        pe.wait_ge(y_r, i * S + s + 1)
                        for j in range(T2):
                            ins = nc.tensor.transpose(k.bank[2 * s][:, j * P:(j + 1) * P], y2[s][:, j, :], w["ident"][:])
                        ins.then_inc(pe_r, 1)
                    for c in range(2):
                        for s in range(S):
                            pe.wait_ge(ev, i * S * EV + c * S + s + 1)
                            for m in range(2):
                                ins = mm(k.bank[2 * s + 1][:, m * L:(m + 1) * L], w["L2_lin1T"][:, (2 * c + m) * P:(2 * c + m + 1) * P], yT[s][:], start=True, stop=True)
                            ins.then_inc(pe_r, 1)
                    for s in range(S):
                        pe.wait_ge(ev, i * S * EV + 2 * S + s + 1)
                        for j in range(T2):
                            for c in range(4):
                                ins = mm(k.bank[2 * s][:, L + j * P:L + (j + 1) * P], h[s][:, c, j * P:(j + 1) * P], w["L2_lin2T"][:, c, :], start=(c == 0), stop=(c == 3))
                        ins.then_inc(pe_r, 1)


def bf16_parts(value):
    parts, rest = [], np.float32(value)
    for _ in range(3):
        bits = np.array(rest, np.float32).view(np.uint32)
        part = ((bits + np.uint32(0x7FFF) + ((bits >> np.uint32(16)) & np.uint32(1))) & np.uint32(0xFFFF0000)).view(np.float32)
        parts.append(float(part))
        rest = np.float32(rest - part)
    return parts


def stage_cross_attention(k, tag, H, stream, norm, masked):
    nc, w, S = k.nc, k.w, 2
    TURNS, D = B // S, P // H
    R, HL, HB, G = 6 * D, H * L, H // 2, H // 4
    ROWS = R + (6 if masked else 3)
    SCALE = float(D) ** -0.5
    stack = nc.dram_tensor(f"{tag}_stack", [B, 2, ROWS * HL], BF16).ap()
    maxima = nc.dram_tensor(f"{tag}_maxima", [B, 2, 6 * HB * P], BF16).ap()
    NS, NE, NP = 3, 2, 3
    HS = S * H
    NB = 3 if 6 * HB <= 32 else P // (2 * HB)
    with ExitStack() as local:
        sb = lambda n, s, d=F32, c=S: [k.sb(f"{tag}_{n}{j}", s, d, local) for j in range(c)]
        ctxT, six, two, rstd = sb("ctxT", [P, L]), sb("six", [P, T2, 6]), sb("two", [P, T2, 2]), sb("rstd", [P, T2])
        xn, xnT, qk, rest = sb("xn", [P, T2, P]), sb("xnT", [P, L]), sb("qk", [P, 2 * L]), sb("rest", [P, 2 * L])
        parts = sb("parts", [P, 3, 2 * L], BF16)
        qs, ks = sb("qs", [P, HL], BF16), sb("ks", [P, HL], BF16)
        val = sb("val", [P, T2, H, 32])
        nmax, nrest, nparts, nT = sb("nmax", [P, 2 * H]), sb("nrest", [P, 2 * HB]), sb("nparts", [P, NB, 2 * HB], BF16), sb("nT", [6 * HB, P], BF16)
        prob = sb("prob", [P, 2, L], c=NP)
        out32, rden, o, oT = sb("out32", [P, G, L]), sb("rden", [P, H]), sb("o", [P, T2, P]), sb("oT", [P, L])
        mrow, mfloat, mpart = (k.sb(f"{tag}_mrow", [B, L], U8, local), k.sb(f"{tag}_mfloat", [B, L], F32, local), k.sb(f"{tag}_mpart", [B, 3, L], BF16, local)) if masked else (None,) * 3
        sem = lambda n: k.sem(f"{tag}_" + n)
        each = lambda n: [sem(f"{n}{j}") for j in range(S)]
        ctx_in, wrote, stacked, nwrote = each("ctx_in"), each("wrote"), each("stacked"), each("nwrote")
        nrow = [each("nrow_a"), each("nrow_b")]
        stats, rs, n0 = k.norms(B if norm else 0)
        fill, xn_r, ev, part_r, v_r, pe_r = (sem(n) for n in ("fill", "xn", "evac", "parts", "v", "front_ps"))
        s_ps, mx_r, np_r, nt_ps, nt_r, e_ps, ex_r, pv_ps, o_ev = (sem(n) for n in ("s_ps", "max", "nparts", "nT_ps", "nT", "e_ps", "exp", "pv_ps", "out32"))
        out_ps, o_r, done, const_r = sem("out_ps"), sem("o"), sem("done"), sem("const")
        FR = 3

        with nc.Block() as block:
            @block.sync
            def _(sp):
                sp.dma_start(stack[:, 0, R * HL:ROWS * HL].rearrange("b (r c) -> b r c", c=HL), k.d["stack_fill"][0:1, 0:ROWS - R, 0:HL].to_broadcast([B, ROWS - R, HL])).then_inc(fill, 16)
                sp.dma_start(stack[:, 1, R * HL:(R + 3) * HL].rearrange("b (r c) -> b r c", c=HL), k.d["stack_fill"][1:2, 0:3, 0:HL].to_broadcast([B, 3, HL])).then_inc(fill, 16)
                if masked:
                    sp.dma_start(mrow[:], k.d["mask_rows"]).then_inc(fill, 16)
                    sp.wait_ge(const_r, 1)
                    for j in range(3):
                        sp.dma_start(stack[:, 1, (R + 3 + j) * HL:(R + 4 + j) * HL].rearrange("b (h t) -> b h t", h=H), mpart[:, j, :].unsqueeze(1).to_broadcast([B, H, L])).then_inc(fill, 16)
                sp.wait_ge(fill, 16 * (6 if masked else 2))
                sp.wait_ge(const_r, 2 if masked else 1)
                with sp.Fori(0, TURNS) as i:
                    for s in range(S):
                        n = i * S + s
                        sp.wait_ge(done, n + 1)
                        sp.dma_start(ctxT[s][:], k.d["ctxT"][bass.ds(n, 1)].rearrange("b d l -> (b d) l")).then_inc(ctx_in[s], 16)
                    for s in range(S):
                        n = i * S + s
                        sp.wait_ge(part_r, n + 1)
                        slot = lambda qk_, a, b: stack[bass.ds(n, 1), qk_, a * P * L:b * P * L].rearrange("b (j p t) -> p (b j) t", p=P, t=L)
                        for a, b, j in ((0, 3, 0), (3, 5, 1), (5, 6, 2)):
                            sp.dma_start(slot(0, a, b), parts[s][:, j:j + 1, 0:L].to_broadcast([P, b - a, L])).then_inc(wrote[s], 16)
                            sp.dma_start(slot(1, a, b), parts[s][:, 0:b - a, L:2 * L]).then_inc(wrote[s], 16)
                        sp.wait_ge(wrote[s], (i + 1) * 96)
                        for qk_, dst in ((0, qs), (1, ks)):
                            sp.dma_start(dst[s][0:ROWS, :], stack[bass.ds(n, 1), qk_, :].rearrange("b (r c) -> (b r) c", c=HL)).then_inc(stacked[s], 16)
                    for s in range(S):
                        n = i * S + s
                        for half in range(2):
                            sp.wait_ge(nt_r, (i * S + s) * 2 + half + 1)
                            mx = maxima[bass.ds(n, 1), half, :]
                            sp.dma_start(mx.rearrange("b (c q) -> (b c) q", q=P), nT[s][:]).then_inc(nwrote[s], 16)
                            sp.wait_ge(nwrote[s], (i * 2 + half + 1) * 16)
                            sp.dma_start(qs[s][R:R + 3, half * HB * L:(half + 1) * HB * L], mx.rearrange("b (r c) -> (b r) c", r=3)).then_inc(nrow[half][s], 16)

            @block.gpsimd
            def _(pool):
                if norm:
                    with pool.Fori(0, TURNS) as i:
                        order = Order(k, pool, "pool", i, TURNS, S)
                        for s in range(S):
                            pool.wait_ge(stats, n0 + i * S + s + 1)
                            rstd_on_pool(k, order, two[s][:, :, 1], rstd[s][:], T2).then_inc(rs, 1)
                        order.close()

            @block.vector
            def _(v):
                tt, ts, cp = nc.vector.tensor_tensor, nc.vector.tensor_scalar, nc.vector.tensor_copy
                order = Order(k, v, "dve")
                if masked:
                    v.wait_ge(fill, 48)
                    order.mark(cp(mfloat[:], mrow[:]))
                    order.settle()
                    order.mark(ts(mfloat[:], mfloat[:], -1.0, 1.0, ALU.mult, ALU.add))
                    order.settle()
                    for j, c in enumerate(bf16_parts(-1e4 * np.sqrt(np.float32(D)))):
                        ins = ts(mpart[:, j, :], mfloat[:], c, None, ALU.mult)
                    ins.then_inc(const_r, 1)
                for s in range(S):
                    nc.vector.memset(qs[s][:], 0.0)
                    nc.vector.memset(ks[s][:], 0.0)
                    nc.vector.memset(nparts[s][:], 0.0)
                    ins = nc.vector.memset(val[s][:], 0.0)
                order.mark(ins)
                order.settle()
                for s in range(S):
                    ins = nc.vector.memset(val[s][:, :, :, 0:1], 1.0)
                ins.then_inc(const_r, 1)
                v.sem_inc(done, S)
                order.close()
                with v.Fori(0, TURNS) as i:
                    order = Order(k, v, "dve", i, TURNS, (S if norm else 0) + 15 * S)
                    st = lambda s, n=T2, j=0: stream[:, bass.ds((i * S + s) * T2 + j, n), :]
                    for s in range(S):
                        if norm:
                            ln_stats(k, order, st(s), six[s], two[s], lambda ins: ins.then_inc(stats, 1))
                    for s in range(S):
                        if norm:
                            v.wait_ge(rs, n0 + i * S + s + 1)
                            for j in range(T2):
                                ins = ts(xn[s][:, j, :], flat(st(s, 1, j)), two[s][:, j, 0:1], rstd[s][:, j:j + 1], ALU.subtract, ALU.mult)
                        else:
                            ins = cp(xn[s][:], st(s))
                        ins.then_inc(xn_r, 1)
                    for s in range(S):
                        v.wait_ge(pe_r, i * S * FR + S + s + 1)
                        ts(qk[s][:, 0:L], k.bank[s][:, 0:L], w[f"{tag}_bq"][:, 0:1], None, ALU.add)
                        if masked:
                            order.mark(nc.vector.scalar_tensor_tensor(qk[s][:, L:2 * L], k.bank[s][:, L:2 * L], w[f"{tag}_bk"][:, 0:1], w["mask"][:, bass.ds((i * S + s) * L, L)], ALU.add, ALU.mult))
                        else:
                            order.mark(ts(qk[s][:, L:2 * L], k.bank[s][:, L:2 * L], w[f"{tag}_bk"][:, 0:1], None, ALU.add))
                        order.settle()
                        order.mark(cp(parts[s][:, 0, :], qk[s][:]))
                        order.settle()
                        order.mark(tt(rest[s][:], qk[s][:], parts[s][:, 0, :], ALU.subtract))
                        order.settle()
                        order.mark(cp(parts[s][:, 1, :], rest[s][:]))
                        order.settle()
                        tt(parts[s][:, 2, :], rest[s][:], parts[s][:, 1, :], ALU.subtract).then_inc(part_r, 1)
                    for s in range(S):
                        v.wait_ge(pe_r, i * S * FR + 2 * S + s + 1)
                        for j in range(T2):
                            ins = tt(val[s][:, j, :, 1:1 + D], k.bank[2 + s][:, j * P:(j + 1) * P].rearrange("p (h d) -> p h d", h=H),
                                     w[f"{tag}_bv"][:].rearrange("p (h d) -> p h d", h=H), ALU.add)
                        order.mark(ins)
                    order.settle()
                    cp(rden[0][:, 0:1], val[0][:, 0, 0, 0:1]).then_inc(v_r, 1)
                    for u in range(HS):
                        s, h = u // H, u % H
                        v.wait_ge(s_ps, i * HS + u + 1)
                        nc.vector.tensor_reduce(nmax[s][:, 2 * h:2 * h + 2], k.bank[2 + u % NS][:].rearrange("p (t l) -> p t l", t=2), AX.X, ALU.max, negate=True).then_inc(mx_r, 1)
                        if h % HB == HB - 1:
                            half = h // HB
                            src = nmax[s][:, half * 2 * HB:(half + 1) * 2 * HB]
                            v.wait_ge(mx_r, i * HS + u + 1)
                            order.mark(cp(nparts[s][:, 0, :], src))
                            order.settle()
                            order.mark(tt(nrest[s][:], src, nparts[s][:, 0, :], ALU.subtract))
                            order.settle()
                            order.mark(cp(nparts[s][:, 1, :], nrest[s][:]))
                            order.settle()
                            tt(nparts[s][:, 2, :], nrest[s][:], nparts[s][:, 1, :], ALU.subtract).then_inc(np_r, 1)
                            j = s * 2 + half
                            v.wait_ge(nt_ps, i * S * 2 + j + 1)
                            cp(nT[s][:], k.bank[1][:].bitcast(BF16)[0:6 * HB, 0:P]).then_inc(nt_r, 1)
                    for s in range(S):
                        v.wait_ge(out_ps, i * S * 3 + s + 1)
                        for j in range(T2):
                            heads = k.bank[1 + 2 * s + j][:, 0:G * P].rearrange("p (h c) -> p h c", c=32)
                            order.mark(nc.vector.reciprocal(rden[s][:], heads[:, :, 0]))
                            order.settle()
                            ins = tt(o[s][:, j, :].rearrange("p (h d) -> p h d", h=H), heads[:, :, 1:1 + D], rden[s][:].unsqueeze(2).to_broadcast([P, H, D]), ALU.mult)
                            if j == 0:
                                order.mark(ins)
                                order.settle()
                        ins.then_inc(o_r, 1)
                    for s in range(S):
                        order.mark(tt(st(s), st(s), w[f"{tag}_bo"][:].unsqueeze(1).to_broadcast([P, T2, P]), ALU.add))
                        order.settle()
                        v.wait_ge(out_ps, i * S * 3 + 2 * S + s + 1)
                        tt(st(s), st(s), k.bank[5 + s][:, L:2 * L].rearrange("p (t d) -> p t d", t=T2), ALU.add).then_inc(done, 1)
                    order.close()

            def gather(act, i, g):
                act.wait_ge(pv_ps, i * HS + 4 * g + 4)
                nc.scalar.copy(out32[g // G][:, g % G, :], k.bank[(7, 0)[g % 2]][:, 0:L]).then_inc(o_ev, 1)

            @block.scalar
            def _(act):
                with act.Fori(0, TURNS) as i:
                    for s in range(S):
                        act.wait_ge(pe_r, i * S * FR + s + 1)
                        nc.scalar.copy(xnT[s][:], k.bank[s][:, 0:L]).then_inc(ev, 1)
                    for u in range(HS):
                        act.wait_ge(e_ps, i * HS + u + 1)
                        if u >= NP:
                            act.wait_ge(pv_ps, i * HS + u - NP + 1)
                        nc.scalar.activation(flat(prob[u % NP][:]), k.bank[5 + u % NE][:], ACT.Exp, scale=SCALE).then_inc(ex_r, 1)
                        if u % 4 == 1 and u > 4:
                            gather(act, i, u // 4 - 1)
                    gather(act, i, HS // 4 - 1)
                    for s in range(S):
                        act.wait_ge(out_ps, i * S * 3 + S + s + 1)
                        nc.scalar.copy(oT[s][:], k.bank[5 + s][:, 0:L]).then_inc(ev, 1)

            def new_maxima(pe, i, j):
                s = j // 2
                pe.wait_ge(np_r, i * S * 2 + j + 1)
                nc.tensor.transpose(k.bank[1][:].bitcast(BF16)[0:2 * NB * HB, 0:P], flat(nparts[s][:]), w["ident_bf"][:]).then_inc(nt_ps, 1)

            def head_values(pe, i, u):
                s, h, g = u // H, u % H, u // 4
                pe.wait_ge(ex_r, i * HS + u + 1)
                if u % 4 == 0 and g >= 2:
                    pe.wait_ge(o_ev, i * (HS // 4) + g - 1)
                r = 32 * (h % 4)
                for c in range(2):
                    ins = nc.tensor.matmul(k.bank[(7, 0)[g % 2]][r:r + 32, 0:L], val[s][:, c, h, :], prob[u % NP][:, c, :], start=(c == 0), stop=(c == 1), tile_position=(0, r))
                ins.then_inc(pv_ps, 1)

            @block.tensor
            def _(pe):
                mm = nc.tensor.matmul
                with pe.Fori(0, TURNS) as i:
                    for s in range(S):
                        pe.wait_ge(xn_r, i * S + s + 1)
                        for j in range(T2):
                            ins = nc.tensor.transpose(k.bank[s][:, j * P:(j + 1) * P], xn[s][:, j, :], w["ident"][:])
                        ins.then_inc(pe_r, 1)
                    for s in range(S):
                        pe.wait_ge(ev, i * S * 2 + s + 1)
                        pe.wait_ge(ctx_in[s], i * 16 + 16)
                        mm(k.bank[s][:, 0:L], w[f"{tag}_wq"][:], xnT[s][:], start=True, stop=True)
                        mm(k.bank[s][:, L:2 * L], w[f"{tag}_wk"][:], ctxT[s][:], start=True, stop=True).then_inc(pe_r, 1)
                    for s in range(S):
                        for j in range(T2):
                            ins = mm(k.bank[2 + s][:, j * P:(j + 1) * P], ctxT[s][:, j * P:(j + 1) * P], w[f"{tag}_wv"][:], start=True, stop=True)
                        ins.then_inc(pe_r, 1)
                    pe.wait_ge(v_r, i + 1)
                    for u in range(HS + H + 1):
                        if u < HS:
                            s, h = u // H, u % H
                            if h == 0:
                                pe.wait_ge(stacked[s], (i + 1) * 32)
                            if u >= NS:
                                pe.wait_ge(mx_r, i * HS + u - NS + 1)
                            for j in range(2):
                                ins = mm(k.bank[2 + u % NS][:, j * L:(j + 1) * L], qs[s][:, h * L + j * P:h * L + (j + 1) * P], ks[s][:, h * L:(h + 1) * L], start=True, stop=True)
                            ins.then_inc(s_ps, 1)
                        if u > HB and u <= 2 * HS and (u - 1) % HB == 0 and (u - 1) // HB - 1 < 2 * S:
                            new_maxima(pe, i, (u - 1) // HB - 1)
                        if H <= u < H + HS:
                            x = u - H
                            s, h = x // H, x % H
                            if h % HB == 0:
                                pe.wait_ge(nrow[h // HB][s], i * 16 + 16)
                            if x >= NE:
                                pe.wait_ge(ex_r, i * HS + x - NE + 1)
                            for c in range(2):
                                ins = mm(k.bank[5 + x % NE][:, c * L:(c + 1) * L], ks[s][:, h * L + c * P:h * L + (c + 1) * P], qs[s][:, h * L:(h + 1) * L], start=True, stop=True)
                            ins.then_inc(e_ps, 1)
                        if u > H:
                            head_values(pe, i, u - H - 1)
                    for s in range(S):
                        pe.wait_ge(o_ev, i * (HS // 4) + (s + 1) * G)
                        for j in range(2):
                            for g in range(G):
                                ins = nc.tensor.transpose(k.bank[1 + 2 * s + j][:, g * P:(g + 1) * P], out32[s][:, g, j * P:(j + 1) * P], w["ident"][:])
                        ins.then_inc(out_ps, 1)
                    for s in range(S):
                        pe.wait_ge(o_r, i * S + s + 1)
                        for j in range(2):
                            ins = nc.tensor.transpose(k.bank[5 + s][:, j * P:(j + 1) * P], o[s][:, j, :], w["ident"][:])
                        ins.then_inc(out_ps, 1)
                    for s in range(S):
                        pe.wait_ge(ev, i * S * 2 + S + s + 1)
                        for j in range(2):
                            ins = mm(k.bank[5 + s][:, L + j * P:L + (j + 1) * P], oT[s][:, j * P:(j + 1) * P], w[f"{tag}_wo"][:], start=True, stop=True)
                        ins.then_inc(out_ps, 1)


def stage_attention_8(k):
    stage_cross_attention(k, "L2", 8, k.y, False, False)


def stage_attention_16(k):
    stage_cross_attention(k, "L3", 16, k.x, True, True)


def stage_store(k):
    stored = k.sem("stored")
    with k.nc.Block() as block:
        @block.sync
        def _(sp):
            sp.dma_start(k.out.rearrange("b (t p) d -> p (b t) d", p=P), k.x[:]).then_inc(stored, 16)
            sp.wait_ge(stored, 16)


LAYERS = [("layer0", [stage_autocorrelation, stage_ternary_ffn]),
          ("layer1", [stage_causal_attention, stage_experts_gelu, stage_load_last]),
          ("layer2", [stage_self_attention, stage_attention_8, stage_relu_ffn]),
          ("rest", [stage_fourier, stage_attention_16, stage_experts_shared])]


def host_layout(a):
    bf16 = mybir.dt.np(BF16)

    f = np.float32
    t = {}
    rows = lambda v: np.ascontiguousarray(np.broadcast_to(v, (P,) + v.shape))
    cols = lambda v, n: np.ascontiguousarray(v.reshape(n, P).T)
    t["x"] = a["x"]
    t["ctx"] = a["ctx_1024"]
    t["ctxT"] = np.ascontiguousarray(a["ctx_1024"].transpose(0, 2, 1))
    t["ternary"] = np.ascontiguousarray(np.stack([
        a["L0_ffn_w_gate"].T, a["L0_ffn_w_up"].T,
        a["L0_ffn_w_down"].T.reshape(4, P, P).transpose(1, 0, 2).reshape(P, 512)], 1))
    t["mask_bytes"] = a["mask_BxS2_bf1"].view(np.uint8).reshape(B * L)
    t["mask_rows"] = a["mask_BxS2_bf1"].view(np.uint8)
    t["lens"] = a["_lenS2"]
    t["ident"] = np.eye(P, dtype=f)
    t["ident_bf"] = np.eye(P, dtype=bf16)
    tok, fr = np.arange(L)[:, None], np.arange(P)[None, :]
    cosine, sine = np.cos(2 * np.pi * tok * fr / L), np.sin(2 * np.pi * tok * fr / L)
    nyq = (-1.0) ** np.arange(L)
    second = sine.copy()
    second[:, 0] = nyq
    t["dft"] = np.ascontiguousarray(np.concatenate([cosine, second], 1).reshape(T2, P, L).transpose(1, 0, 2)).astype(f)
    first_i, second_i = 2 * cosine.T / L, -2 * sine.T / L
    first_i[0] = 1.0 / L
    second_i[0] = nyq / L
    t["idft"] = np.ascontiguousarray(np.stack([first_i, second_i], 1)).astype(f)
    ch = np.arange(P)
    t["head_block"] = (ch[:, None] // 8 == ch[None, :] // 8).astype(f)
    out_row = 2 * (ch % 8 * 16 + ch // 8)
    spread = np.zeros((P, T2, 2, P), f)
    for half in range(2):
        spread[ch, (out_row + half) // P, half, (out_row + half) % P] = 1
    t["spread_rows"] = spread.reshape(P, 4 * P)
    t["iota8"] = rows(np.arange(8, dtype=f))
    t["rolled_base"] = (ch % 8 + L).astype(f)[:, None]
    t["not_first"] = (ch > 0).astype(f)[:, None]
    ang = 2 * np.pi * (ch[:, None] * ch[None, :] % P) / P
    t["fourier_cos"], t["fourier_sin"], t["fourier_nsin"] = np.cos(ang).astype(f), np.sin(ang).astype(f), (-np.sin(ang)).astype(f)
    kk = np.concatenate([np.arange(P), np.arange(L)])
    qq = np.concatenate([np.zeros(P), np.full(L, P)])
    t["iota_k"] = rows(kk.astype(f))
    t["causal"] = np.where(kk[None] <= qq[None] + ch[:, None], 0, NEG).astype(f)
    t["head_pick"] = np.stack([ch < 64, ch >= 64], 1).astype(f)
    t["prefix"] = rows((np.arange(8)[None, :] < np.arange(8)[:, None]).astype(f))
    for n in ("wq", "wk", "wv", "wo"):
        t["q0_" + n] = a["L0_xattn_" + n]
    for n in ("Q", "K", "V"):
        t["L1_W" + n] = np.ascontiguousarray(a["L1_xattn_W" + n].transpose(1, 0, 2).reshape(P, 1024))
        t["L1_b" + n] = cols(a["L1_xattn_b" + n], 8)
    t["L1_WO"] = np.ascontiguousarray(a["L1_xattn_WO"].reshape(8, P, P).transpose(1, 0, 2))
    t["L1_bO"] = rows(a["L1_xattn_bO"])
    t["L1_router"] = a["L1_ffn_router_w"]
    t["L1_up_w"] = np.ascontiguousarray(a["L1_ffn_up_w"].transpose(1, 0, 2))
    t["L1_down_w"] = np.ascontiguousarray(a["L1_ffn_down_w"].reshape(8, 4, P, P).transpose(2, 0, 1, 3).reshape(P, 8, 512))
    t["L2_ffn_w_freq_real"], t["L2_ffn_w_freq_imag"] = a["L2_ffn_w_freq_real"], a["L2_ffn_w_freq_imag"]
    t["L2_bias"] = rows(a["L2_ffn_bias"])
    t["L2_saT"] = np.ascontiguousarray(a["L2_xattn_sa_out_w"].T)
    t["L2_sa_v"] = np.ascontiguousarray(a["L2_xattn_qkv_w"][2 * P:])
    t["L2_sa_vb"] = np.ascontiguousarray(np.broadcast_to(a["L2_xattn_qkv_b"][2 * P:, None], (P, P)))
    t["L2_vecs"] = rows(np.stack([a["L2_xattn_" + n] for n in ("sa_out_b", "ln1_g", "ln1_b", "ln2_g", "ln2_b", "lin2_b", "ln3_g", "ln3_b")]))
    t["L2_lin1T"] = np.ascontiguousarray(a["L2_xattn_lin1_w"].T)
    t["L2_lin1b"] = cols(a["L2_xattn_lin1_b"], 4)
    t["L2_lin2T"] = np.ascontiguousarray(a["L2_xattn_lin2_w"].T.reshape(4, P, P).transpose(1, 0, 2))
    for name, heads, ws, bs, wo, bo in (
            ("L2", 8, np.split(a["L2_xattn_in_proj_w"], 3), np.split(a["L2_xattn_in_proj_b"], 3), a["L2_xattn_mha_out_w"], a["L2_xattn_mha_out_b"]),
            ("L3", 16, [a["L3_xattn_W" + n] for n in "qkv"], [a["L3_xattn_b" + n] for n in "qkv"], a["L3_xattn_Wo"], a["L3_xattn_bo"])):
        by_dim = np.arange(P).reshape(heads, P // heads).T.reshape(P)
        t[name + "_wq"], t[name + "_wk"] = (np.ascontiguousarray(m.T[:, by_dim]) for m in ws[:2])
        t[name + "_bq"], t[name + "_bk"] = (np.ascontiguousarray(v[by_dim][:, None]) for v in bs[:2])
        t[name + "_wv"], t[name + "_bv"] = np.ascontiguousarray(ws[2].T), rows(bs[2])
        t[name + "_wo"], t[name + "_bo"] = np.ascontiguousarray(wo.T), rows(bo)
    t["stack_fill"] = np.stack([np.concatenate([np.zeros((3, 4096)), np.ones((3, 4096))]), np.concatenate([np.ones((3, 4096)), np.zeros((3, 4096))])]).astype(bf16)
    t["L3_centroids"] = a["L3_ffn_centroids"]
    t["L3_g"] = np.stack([a["L3_ffn_g_shared"], a["L3_ffn_g_routed"]], 1)
    both = lambda n: np.concatenate([a[f"L3_ffn_{n}_s"], a[f"L3_ffn_{n}_r"]])
    t["L3_W1"] = np.ascontiguousarray(both("W1").transpose(1, 0, 2))
    t["L3_W2"] = np.ascontiguousarray(both("W2").reshape(10, 4, P, P).transpose(2, 0, 1, 3).reshape(P, 10, 512))
    t["L3_b1"] = cols(both("b1").reshape(40, P), 40)
    t["L3_b2"] = both("b2")
    return t


def program(nc, dram, out, only=None):
    with ExitStack() as ctx:
        k = Kit(nc, ctx, dram, out)
        stage_setup(k)
        for name, stages in LAYERS:
            for stage in stages:
                if only is None or stage in only:
                    stage(k)
            memory = {"layer0": k.layer0, "layer1": k.layer1, "layer2": k.layer2, "rest": k.rest}[name]
            memory.close()
        stage_store(k)


def kernel(**inputs):
    from concourse import bacc
    from concourse.bass_utils import run_bass_kernel_spmd

    arrays = host_layout(inputs)
    nc = bacc.Bacc("TRN2", target_bir_lowering=False, num_devices=1)
    dram = {n: nc.dram_tensor("in_" + n, v.shape, mybir.dt.from_np(v.dtype), kind="ExternalInput").ap() for n, v in arrays.items()}
    out = nc.dram_tensor("out", (B, L, P), F32, kind="ExternalOutput").ap()
    program(nc, dram, out)
    r = run_bass_kernel_spmd(nc, [{"in_" + n: v for n, v in arrays.items()}], core_ids=[0])
    return r.results[0]["out"]
```

```python
from contextlib import ExitStack

import concourse.bass as bass
import numpy as np
from concourse import mybir

F32, BF16, F32R = mybir.dt.float32, mybir.dt.bfloat16, mybir.dt.float32r
I32, U32, U8 = mybir.dt.int32, mybir.dt.uint32, mybir.dt.uint8
ACT, ALU, AX = mybir.ActivationFunctionType, mybir.AluOpType, mybir.AxisListType

P = 128
B, L = 8, 256
T2 = L // P
NT = B * T2
EPS = 1e-5
EPS_RMS = float(np.finfo(np.float32).eps)
ROUND = float(3 << 22)
NEG = -1e30


class Order:

    def __init__(self, k, eng, name, turn=0, turns=1, per=None):
        self.k, self.eng, self.name, self.turns, self.per = k, eng, name, turns, per
        self.count = 0
        self.start = k.ordered[name] + (turn * per if turns > 1 else 0)

    def mark(self, ins):
        self.count += 1
        return ins.then_inc(self.k.order[self.name], 1)

    def settle(self):
        self.eng.wait_ge(self.k.order[self.name], self.start + self.count)

    def settle_apart(self):
        self.settle()
        self.k.carry(self.eng)

    def close(self):
        assert self.turns == 1 or self.count == self.per, (self.name, self.count)
        self.k.ordered[self.name] += self.turns * self.count


class Kit:

    def __init__(self, nc, ctx, dram, out):
        self.nc, self.ctx, self.d, self.out = nc, ctx, dram, out
        self.order = {e: ctx.enter_context(nc.semaphore(f"{e}_order")) for e in ("dve", "act", "pool")}
        self.ordered = dict.fromkeys(self.order, 0)
        self.bank = [self.psum(f"bank{n}") for n in range(8)]
        self.x = self.sb("x_stream", [P, NT, P])
        self.sems = []
        self.tick, self.ticks = self.sb("tick", [1, 256]), 0
        self.stats, self.rstd, self.normed = self.sem("norm_stats"), self.sem("norm_rstd"), 0
        self.all_xn, self.all_ps, self.all_ev, self.alls = self.sem("all_xn"), self.sem("all_ps"), self.sem("all_ev"), 0
        self.rest, self.layer2, self.layer1, self.layer0 = ExitStack(), ExitStack(), ExitStack(), ExitStack()
        self.w = {}

    def sb(self, name, shape, dt=F32, ctx=None):
        return (ctx or self.ctx).enter_context(self.nc.sbuf_tensor(name, shape, dt))

    def norms(self, count):
        self.normed += count
        return self.stats, self.rstd, self.normed - count

    def carry(self, eng):
        self.ticks += 1
        own = self.tick[:, self.ticks - 1:self.ticks]
        if eng is self.nc.gpsimd:
            eng.tensor_tensor(own, self.w["eps"][0:1, 0:1], self.w["eps"][0:1, 0:1], ALU.add)
        else:
            eng.memset(own, 0.0)

    def psum(self, name):
        return self.ctx.enter_context(self.nc.psum_tensor(name, [P, 512], F32))

    def sem(self, name):
        found = self.nc.alloc_semaphore(name=name)
        self.sems.append(found)
        return found

    def retire_semaphores(self, since):
        with self.nc.Block() as block:
            @block.gpsimd
            def _(pool):
                for s in self.sems[since:]:
                    pool.sem_clear(s)
        for s in self.sems[since:]:
            self.nc.release_semaphore(s)
        del self.sems[since:]


def flat(ap):
    return ap.rearrange("p a b -> p (a b)")


def stage_setup(k):
    nc = k.nc
    loaded = k.sem("setup_loaded")
    first = ["dft", "idft", "head_block", "iota8", "rolled_base", "not_first",
             "q0_wq", "q0_wk", "q0_wv", "q0_wo", "spread_rows", "fourier_cos", "fourier_sin", "fourier_nsin",
             "L2_ffn_w_freq_real", "L2_ffn_w_freq_imag", "L2_saT", "L2_sa_v", "L2_sa_vb"]
    later = ["ident", "ident_bf", "L2_bias", "L2_vecs", "L2_lin1T", "L2_lin1b", "L2_lin2T",
             "L2_wq", "L2_wk", "L2_wv", "L2_wo", "L2_bq", "L2_bk", "L2_bv", "L2_bo",
             "L3_wq", "L3_wk", "L3_wv", "L3_wo", "L3_bq", "L3_bk", "L3_bv", "L3_bo",
             "L3_centroids", "L3_g", "L3_b1", "L3_b2", "prefix"]
    second = ["L1_WQ", "L1_WK", "L1_WV", "L1_WO", "L1_bQ", "L1_bK", "L1_bV", "L1_bO", "L1_router",
              "causal", "iota_k", "head_pick"]
    w = k.w
    small = first + second + later
    for n in later:
        w[n] = k.sb("w_" + n, list(k.d[n].shape), k.d[n].dtype)
    n_small = 16 * (4 + len(small))
    w["fourier"] = k.sb("fourier", [P, P])
    w["minus_half"] = k.sb("minus_half", [P, NT])
    w["eps"], w["eps_rms"] = k.sb("eps", [P, NT]), k.sb("eps_rms", [P, NT])
    w["sa"] = k.sb("sa", [P, P])
    w["sa_bias"] = k.sb("sa_bias", [P, P])
    w["mask_bytes"] = k.sb("mask_bytes", [P, B * L], U8)
    w["lens"] = k.sb("lens", [P, B])
    for n in second:
        w[n] = k.sb("w_" + n, list(k.d[n].shape), k.d[n].dtype, k.layer1)
    for n in ("up_w", "down_w"):
        w[n] = k.sb(n, [P, 8, 512], F32, k.layer1)
    for n in first:
        w[n] = k.sb("w_" + n, list(k.d[n].shape), k.d[n].dtype, k.layer0)
    for n in ("gate", "up", "down"):
        w["tern_" + n] = k.sb("tern_" + n, [P, 512], BF16, k.layer0)
        w["scale_" + n] = k.sb("scale_" + n, [P, 1], F32, k.layer0)
    with ExitStack() as local:
        raw = k.sb("raw_ternary", [P, 3, 512], ctx=local)
        ratio = k.sb("ternary_ratio", [P, 3, 512], ctx=local)
        rowsum = k.sb("ternary_rowsum", [P, 3], ctx=local)
        inv = k.sb("ternary_inv", [P, 3], ctx=local)
        ones = k.sb("ones128", [P, P], ctx=local)
        spec = k.sb("fourier_ab", [P, 2, P], ctx=local)
        len_i = k.sb("lens_int", [P, B], I32, ctx=local)
        sa_b = k.sb("sa_bcast", [P, P], ctx=local)
        big_loaded = k.sem("ffn1_loaded")
        k.big_loaded = big_loaded
        summed, spectra, mixed = k.sem("setup_summed"), k.sem("setup_spectra"), k.sem("setup_mixed")
        prepared = k.sem("setup_prepared")
        with nc.Block() as block:
            @block.sync
            def _(sp):
                sp.dma_start(k.x[:], k.d["x"].rearrange("b (t p) d -> p (b t) d", p=P)).then_inc(loaded, 16)
                sp.dma_start(raw[:], k.d["ternary"]).then_inc(loaded, 16)
                sp.dma_start(w["mask_bytes"][:], k.d["mask_bytes"].partition_broadcast(P)).then_inc(loaded, 16)
                sp.dma_start(len_i[:], k.d["lens"].partition_broadcast(P)).then_inc(loaded, 16)
                for n in small:
                    sp.dma_start(w[n][:], k.d[n]).then_inc(loaded, 16)
                for n in ("up_w", "down_w"):
                    sp.dma_start(w[n][:], k.d["L1_" + n]).then_inc(big_loaded, 16)

            @block.vector
            def _(v):
                order = Order(k, v, "dve")
                nc.vector.memset(ones[:], 1.0)
                nc.vector.memset(w["eps"][:], EPS)
                nc.vector.memset(w["eps_rms"][:], EPS_RMS)
                nc.vector.memset(w["minus_half"][:], -0.5).then_inc(prepared, 1)
                v.wait_ge(loaded, n_small)
                order.mark(nc.vector.tensor_reduce(rowsum[:], raw[:], AX.X, ALU.add, apply_absolute_value=True))
                order.settle()
                nc.vector.tensor_scalar(rowsum[:], rowsum[:], 1.0 / (512 * P), None, ALU.mult).then_inc(prepared, 1)
                order.mark(nc.vector.tensor_copy(w["lens"][:], len_i[:]))
                v.wait_ge(summed, 1)
                order.mark(nc.vector.tensor_scalar(rowsum[:], k.bank[0][:, 0:3], EPS, None, ALU.max))
                order.settle()
                order.mark(nc.vector.reciprocal(inv[:], rowsum[:]))
                order.settle()
                for j, n in enumerate(("gate", "up", "down")):
                    order.mark(nc.vector.tensor_scalar(ratio[:, j, :], raw[:, j, :], inv[:, j:j + 1], ROUND, ALU.mult, ALU.add))
                    order.settle()
                    order.mark(nc.vector.tensor_scalar(ratio[:, j, :], ratio[:, j, :], -ROUND, 1.0, ALU.add, ALU.min))
                    order.settle()
                    nc.vector.tensor_scalar(w["tern_" + n][:], ratio[:, j, :], -1.0, None, ALU.max)
                    order.mark(nc.vector.tensor_copy(w["scale_" + n][:], rowsum[:, j:j + 1]))
                v.wait_ge(spectra, 1)
                nc.vector.tensor_copy(flat(spec[:]), k.bank[1][:, 0:2 * P]).then_inc(prepared, 1)
                v.wait_ge(mixed, 1)
                nc.vector.tensor_scalar(w["fourier"][:], k.bank[2][:, 0:P], 1.0 / P, None, ALU.mult)
                nc.vector.tensor_copy(w["sa"][:], k.bank[3][:, 0:P])
                order.mark(nc.vector.tensor_tensor(w["sa_bias"][:], k.bank[3][:, P:2 * P], w["L2_vecs"][:, 0, :], ALU.add))
                order.settle()
                order.close()

            @block.tensor
            def _(pe):
                mm = nc.tensor.matmul
                pe.wait_ge(loaded, n_small)
                pe.wait_ge(prepared, 2)
                mm(k.bank[0][:, 0:3], ones[:], rowsum[:], start=True, stop=True).then_inc(summed, 1)
                wr, wi = w["L2_ffn_w_freq_real"], w["L2_ffn_w_freq_imag"]
                c, s, ns = w["fourier_cos"], w["fourier_sin"], w["fourier_nsin"]
                mm(k.bank[1][:, 0:P], wr[:], c[:], start=True, stop=False)
                mm(k.bank[1][:, 0:P], wi[:], s[:], start=False, stop=True)
                mm(k.bank[1][:, P:2 * P], wi[:], c[:], start=True, stop=False)
                mm(k.bank[1][:, P:2 * P], wr[:], ns[:], start=False, stop=True).then_inc(spectra, 1)
                mm(k.bank[3][:, 0:P], w["L2_sa_v"][:], w["L2_saT"][:], start=True, stop=True)
                mm(k.bank[3][:, P:2 * P], w["L2_sa_vb"][:], w["L2_saT"][:], start=True, stop=True)
                pe.wait_ge(prepared, 3)
                mm(k.bank[2][:, 0:P], spec[:, 0, :], c[:], start=True, stop=False)
                mm(k.bank[2][:, 0:P], spec[:, 1, :], ns[:], start=False, stop=True).then_inc(mixed, 1)


def ln_stats(k, order, src, six, two, last):
    nc, tiles = k.nc, src.shape[1]
    for t in range(tiles):
        ins = nc.vector.bn_stats(six[:, t, :], src[:, t, :])
    order.mark(ins)
    order.settle_apart()
    for t in range(tiles):
        ins = nc.vector.bn_aggr(two[:, t, :], six[:, t, :])
    return last(ins)


def rstd_on_pool(k, order, var, rstd, n, eps=EPS):
    nc = k.nc
    order.mark(nc.gpsimd.tensor_tensor(rstd, var, k.w["eps"][:, 0:n] if eps == EPS else k.w["eps_rms"][:, 0:n], ALU.add))
    order.settle()
    return nc.gpsimd.tensor_tensor(rstd, rstd, k.w["minus_half"][:, 0:n], ALU.pow)


def stage_autocorrelation(k):
    nc, w, S = k.nc, k.w, 4
    TURNS = B // S
    TOP = int(np.floor(np.log(L)))
    with ExitStack() as local:
        sb = lambda n, s, d=F32: [k.sb(f"ac_{n}{j}", s, d, local) for j in range(S)]
        ctx, ctxT = sb("ctx", [P, T2, P]), sb("ctxT", [P, L])
        six, two, rstd = sb("six", [P, T2, 6]), sb("two", [P, T2, 2]), sb("rstd", [P, T2])
        xn, xnT, qk = sb("xn", [P, T2, P]), sb("xnT", [P, L]), sb("qk", [P, T2, 2 * P])
        freq, prod, cross = sb("freq", [P, 2, 2 * P]), sb("prod", [P, 2, P]), sb("cross", [P, 2, P])
        spec = sb("spec", [P, 2, P])
        top, neg, at = sb("top", [P, 8]), sb("neg", [P, 1]), sb("at", [P, 8], U32)
        e5, den, shift, shift_i = sb("e5", [P, 8]), sb("den", [P, 1]), sb("shift", [P, 8]), sb("shift_i", [P, 8], I32)
        hit, roll, mix = sb("hit", [P, 8, TOP]), sb("roll", [P, 8]), sb("mix", [P, P])
        ctx_wo, val_wo, spread = sb("ctx_wo", [P, L]), sb("val_wo", [P, L]), sb("spread", [P, 4, P])
        sem = lambda n: k.sem("ac_" + n)
        ctx_in = [sem(f"ctx_in{j}") for j in range(S)]
        stats, rs, n0 = k.norms(B)
        xn_r, tr, evac = sem("xn"), sem("pe"), sem("evac")
        prod_r, spec_r, mix_r, done, topped, exped = sem("prod"), sem("spec"), sem("mix"), sem("done"), sem("topped"), sem("exped")
        PE, EV = 8, 6

        with nc.Block() as block:
            @block.sync
            def _(sp):
                with sp.Fori(0, TURNS) as i:
                    for s in range(S):
                        n = i * S + s
                        sp.wait_ge(done, n + 1)
                        sp.dma_start(ctx[s][:], k.d["ctx"][bass.ds(n, 1)].rearrange("b (t p) d -> p (b t) d", p=P)).then_inc(ctx_in[s], 16)
                        sp.dma_start(ctxT[s][:], k.d["ctxT"][bass.ds(n, 1)].rearrange("b d l -> (b d) l")).then_inc(ctx_in[s], 16)

            @block.gpsimd
            def _(pool):
                with pool.Fori(0, TURNS) as i:
                    order = Order(k, pool, "pool", i, TURNS, S)
                    for s in range(S):
                        pool.wait_ge(stats, n0 + i * S + s + 1)
                        rstd_on_pool(k, order, two[s][:, :, 1], rstd[s][:], T2).then_inc(rs, 1)
                    for s in range(S):
                        pool.wait_ge(evac, i * S * EV + 2 * S + s + 1)
                        nc.gpsimd.tensor_tensor(cross[s][:, 0, :], freq[s][:, 0, 0:P], freq[s][:, 1, P:2 * P], ALU.mult)
                        nc.gpsimd.tensor_tensor(cross[s][:, 1, :], freq[s][:, 1, 0:P], freq[s][:, 0, P:2 * P], ALU.mult).then_inc(prod_r, 1)
                    order.close()

            @block.vector
            def _(v):
                v.sem_inc(done, S)
                with v.Fori(0, TURNS) as i:
                    order = Order(k, v, "dve", i, TURNS, 11 * S)
                    for s in range(S):
                        ln_stats(k, order, k.x[:, bass.ds((i * S + s) * T2, T2), :], six[s], two[s], lambda ins: ins.then_inc(stats, 1))
                    for s in range(S):
                        v.wait_ge(rs, n0 + i * S + s + 1)
                        for t in range(T2):
                            ins = nc.vector.tensor_scalar(xn[s][:, t, :], k.x[:, bass.ds((i * S + s) * T2 + t, 1), :].rearrange("p a b -> p (a b)"),
                                                          two[s][:, t, 0:1], rstd[s][:, t:t + 1], ALU.subtract, ALU.mult)
                        ins.then_inc(xn_r, 1)
                    for s in range(S):
                        v.wait_ge(evac, i * S * EV + 2 * S + s + 1)
                        order.mark(nc.vector.tensor_tensor(prod[s][:], freq[s][:, :, 0:P], freq[s][:, :, P:2 * P], ALU.mult))
                    for s in range(S):
                        order.settle()
                        nc.vector.scalar_tensor_tensor(spec[s][:, 0, :], prod[s][:, 1, :], w["not_first"][:, 0:1], prod[s][:, 0, :], ALU.mult, ALU.add)
                        v.wait_ge(prod_r, i * S + s + 1)
                        order.mark(nc.vector.tensor_tensor(spec[s][:, 1, :], cross[s][:, 0, :], cross[s][:, 1, :], ALU.subtract))
                    order.settle()
                    for s in range(S):
                        nc.vector.tensor_copy(spec[s][0:1, 1, :], prod[s][0:1, 1, :]).then_inc(spec_r, 1)
                    for s in range(S):
                        v.wait_ge(tr, i * S * PE + 5 * S + s + 1)
                        corr = k.bank[2 * s][:, 0:L]
                        k.carry(v)
                        order.mark(nc.vector.max(top[s][:], corr))
                        order.settle_apart()
                        order.mark(nc.vector.max_index(at[s][:], top[s][:], corr))
                        nc.vector.tensor_scalar(neg[s][:], top[s][:, 0:1], -1.0, None, ALU.mult).then_inc(topped, 1)
                    for s in range(S):
                        order.settle()
                        order.mark(nc.vector.tensor_scalar(shift_i[s][:], at[s][:], -1.0, w["rolled_base"][:, 0:1], ALU.mult, ALU.add))
                    order.settle()
                    for s in range(S):
                        order.mark(nc.vector.tensor_single_scalar(shift_i[s][:], shift_i[s][:], 7, ALU.bitwise_and))
                    order.settle()
                    for s in range(S):
                        order.mark(nc.vector.tensor_copy(shift[s][:], shift_i[s][:]))
                    order.settle()
                    for s in range(S):
                        order.mark(nc.vector.tensor_tensor(
                            hit[s][:], shift[s][:, 0:TOP].unsqueeze(1).to_broadcast([P, 8, TOP]),
                            w["iota8"][:].unsqueeze(2).to_broadcast([P, 8, TOP]), ALU.is_equal))
                    order.settle()
                    for s in range(S):
                        v.wait_ge(exped, i * S + s + 1)
                        nc.vector.reciprocal(den[s][:], den[s][:])
                        order.mark(nc.vector.tensor_tensor(hit[s][:], hit[s][:], e5[s][:, 0:TOP].unsqueeze(1).to_broadcast([P, 8, TOP]), ALU.mult))
                    order.settle()
                    for s in range(S):
                        order.mark(nc.vector.tensor_reduce(roll[s][:], hit[s][:], AX.X, ALU.add))
                    order.settle()
                    for s in range(S):
                        nc.vector.scalar_tensor_tensor(
                            mix[s][:].rearrange("p (g m) -> p g m", m=8), w["head_block"][:].rearrange("p (g m) -> p g m", m=8), den[s][:, 0:1],
                            roll[s][:].unsqueeze(1).to_broadcast([P, 16, 8]), ALU.mult, ALU.mult).then_inc(mix_r, 1)
                    for s in range(S):
                        v.wait_ge(tr, i * S * PE + 7 * S + s + 1)
                        xs = k.x[:, bass.ds((i * S + s) * T2, T2), :]
                        nc.vector.tensor_tensor(xs, xs, k.bank[2 * s][:, L:2 * L].rearrange("p (t d) -> p t d", t=T2), ALU.add).then_inc(done, 1)
                    order.close()

            @block.scalar
            def _(act):
                with act.Fori(0, TURNS) as i:
                    for step, (src, dst) in enumerate((
                            (lambda s: k.bank[2 * s][:, 0:L], lambda s: xnT[s][:]),
                            (lambda s: k.bank[2 * s + 1][:], lambda s: flat(qk[s][:])),
                            (lambda s: k.bank[2 * s][:], lambda s: flat(freq[s][:])),
                            (lambda s: k.bank[2 * s + 1][:, 0:L], lambda s: ctx_wo[s][:]),
                            (lambda s: k.bank[2 * s + 1][:, L:2 * L], lambda s: val_wo[s][:]))):
                        for s in range(S):
                            act.wait_ge(tr, i * S * PE + step * S + s + 1)
                            nc.scalar.copy(dst(s), src(s)).then_inc(evac, 1)
                    for s in range(S):
                        act.wait_ge(topped, i * S + s + 1)
                        nc.scalar.activation(e5[s][:, 0:TOP], top[s][:, 0:TOP], ACT.Exp, bias=neg[s][:, 0:1], accum_out=den[s][:, 0:1]).then_inc(exped, 1)
                    for s in range(S):
                        act.wait_ge(tr, i * S * PE + 6 * S + s + 1)
                        nc.scalar.copy(flat(spread[s][:]), k.bank[2 * s + 1][:]).then_inc(evac, 1)

            @block.tensor
            def _(pe):
                mm = nc.tensor.matmul
                with pe.Fori(0, TURNS) as i:
                    for s in range(S):
                        a = k.bank[2 * s]
                        pe.wait_ge(xn_r, i * S + s + 1)
                        for t in range(T2):
                            ins = nc.tensor.transpose(a[:, t * P:(t + 1) * P], xn[s][:, t, :], w["ident"][:])
                        ins.then_inc(tr, 1)
                    for s in range(S):
                        b = k.bank[2 * s + 1]
                        pe.wait_ge(evac, i * S * EV + s + 1)
                        pe.wait_ge(ctx_in[s], i * 32 + 32)
                        for t in range(T2):
                            mm(b[:, t * L:t * L + P], xnT[s][:, t * P:(t + 1) * P], w["q0_wq"][:], start=True, stop=True)
                            ins = mm(b[:, t * L + P:(t + 1) * L], ctxT[s][:, t * P:(t + 1) * P], w["q0_wk"][:], start=True, stop=True)
                        ins.then_inc(tr, 1)
                    for s in range(S):
                        a = k.bank[2 * s]
                        pe.wait_ge(evac, i * S * EV + S + s + 1)
                        for f in range(2):
                            for t in range(T2):
                                ins = mm(a[:, f * L:(f + 1) * L], w["dft"][:, t, f * P:(f + 1) * P], qk[s][:, t, :], start=(t == 0), stop=(t == T2 - 1))
                        ins.then_inc(tr, 1)
                    for s in range(S):
                        b = k.bank[2 * s + 1]
                        pe.wait_ge(evac, i * S * EV + S + s + 1)
                        for t in range(T2):
                            ins = mm(b[:, t * P:(t + 1) * P], ctx[s][:, t, :], w["q0_wo"][:], start=True, stop=True)
                        ins.then_inc(tr, 1)
                    for s in range(S):
                        pe.wait_ge(evac, i * S * EV + 3 * S + s + 1)
                        mm(k.bank[2 * s + 1][:, L:2 * L], w["q0_wv"][:], ctx_wo[s][:], start=True, stop=True).then_inc(tr, 1)
                    for s in range(S):
                        a = k.bank[2 * s]
                        pe.wait_ge(spec_r, i * S + s + 1)
                        mm(a[:, 0:L], spec[s][:, 0, :], w["idft"][:, 0, :], start=True, stop=False)
                        mm(a[:, 0:L], spec[s][:, 1, :], w["idft"][:, 1, :], start=False, stop=True).then_inc(tr, 1)
                    for s in range(S):
                        pe.wait_ge(mix_r, i * S + s + 1)
                        pe.wait_ge(evac, i * S * EV + 4 * S + s + 1)
                        mm(k.bank[2 * s + 1][:], mix[s][:], w["spread_rows"][:], start=True, stop=True).then_inc(tr, 1)
                    for s in range(S):
                        pe.wait_ge(evac, i * S * EV + 5 * S + s + 1)
                        for t in range(T2):
                            for half in range(2):
                                ins = mm(k.bank[2 * s][:, L + t * P:L + (t + 1) * P], spread[s][:, 2 * t + half, :], val_wo[s][:, half * P:(half + 1) * P],
                                         start=(half == 0), stop=(half == 1))
                        ins.then_inc(tr, 1)




def stage_ternary_ffn(k):
    nc, w, S = k.nc, k.w, 4
    TURNS, HID = NT // S, 512
    with ExitStack() as local:
        sb = lambda n, s, d=F32: [k.sb(f"tf_{n}{j}", s, d, local) for j in range(S)]
        six, two, rstd, xn = sb("six", [P, 1, 6]), sb("two", [P, 1, 2]), sb("rstd", [P, 1]), sb("xn", [P, P])
        am, up_scale, xr, xq, xqT = sb("am", [P, 4]), sb("us", [P, 4]), sb("xr", [P, P]), sb("xq", [P, P], BF16), sb("xqT", [P, P], BF16)
        g, h, hq, hqT = sb("g", [P, HID]), sb("h", [P, HID]), sb("hq", [P, HID], BF16), sb("hqT", [P, 4, P], BF16)
        sem = lambda n: k.sem("tf_" + n)
        stats, rs, n0 = k.norms(NT)
        xq_r, scaled, pe_r, ev, act_r, done = (sem(n) for n in ("xq", "scaled", "pe", "evac", "silu", "done"))
        hq_r = sem("hq")
        PE = 4
        with nc.Block() as block:
            @block.gpsimd
            def _(pool):
                with pool.Fori(0, TURNS) as i:
                    order = Order(k, pool, "pool", i, TURNS, S)
                    for s in range(S):
                        pool.wait_ge(stats, n0 + i * S + s + 1)
                        rstd_on_pool(k, order, two[s][:, 0, 1:2], rstd[s][:], 1).then_inc(rs, 1)
                    order.close()

            def scale_of(order, src, a):
                order.mark(nc.vector.tensor_reduce(a[:, 0:1], src, AX.X, ALU.max, apply_absolute_value=True))
                order.settle()
                order.mark(nc.vector.tensor_scalar(a[:, 2:3], a[:, 0:1], EPS, 1.0 / 127, ALU.max, ALU.mult))
                order.settle()
                order.mark(nc.vector.reciprocal(a[:, 1:2], a[:, 2:3]))
                order.settle()

            def quantise(order, dst, src, a):
                order.mark(nc.vector.tensor_scalar(src, src, a[:, 1:2], ROUND, ALU.mult, ALU.add))
                order.settle()
                order.mark(nc.vector.tensor_scalar(src, src, -ROUND, 127.0, ALU.add, ALU.min))
                order.settle()
                return nc.vector.tensor_scalar(dst, src, -128.0, None, ALU.max)

            @block.vector
            def _(v):
                with v.Fori(0, TURNS) as i:
                    order = Order(k, v, "dve", i, TURNS, 14 * S)
                    for s in range(S):
                        ln_stats(k, order, k.x[:, bass.ds(i * S + s, 1), :], six[s], two[s], lambda ins: ins.then_inc(stats, 1))
                    for s in range(S):
                        v.wait_ge(rs, n0 + i * S + s + 1)
                        order.mark(nc.vector.tensor_scalar(xn[s][:], flat(k.x[:, bass.ds(i * S + s, 1), :]), two[s][:, 0, 0:1], rstd[s][:, 0:1], ALU.subtract, ALU.mult))
                        order.settle()
                        scale_of(order, xn[s][:], am[s])
                        quantise(order, xq[s][:], xn[s][:], am[s]).then_inc(xq_r, 1)
                    for s in range(S):
                        nc.vector.tensor_scalar(up_scale[s][:, 0:1], am[s][:, 2:3], w["scale_gate"][:, 0:1], None, ALU.mult)
                        nc.vector.tensor_scalar(up_scale[s][:, 1:2], am[s][:, 2:3], w["scale_up"][:, 0:1], None, ALU.mult).then_inc(scaled, 1)
                    for s in range(S):
                        v.wait_ge(act_r, i * S + s + 1)
                        v.wait_ge(pe_r, i * S * PE + S + s + 1)
                        v.wait_ge(scaled, i * S + s + 1)
                        order.mark(nc.vector.scalar_tensor_tensor(h[s][:], k.bank[2 * s + 1][:], up_scale[s][:, 1:2], g[s][:], ALU.mult, ALU.mult))
                        order.settle()
                        scale_of(order, h[s][:], am[s])
                        quantise(order, hq[s][:], h[s][:], am[s]).then_inc(hq_r, 1)
                    for s in range(S):
                        order.mark(nc.vector.tensor_scalar(am[s][:, 3:4], am[s][:, 2:3], w["scale_down"][:, 0:1], None, ALU.mult))
                    order.settle()
                    for s in range(S):
                        v.wait_ge(pe_r, i * S * PE + 3 * S + s + 1)
                        xs = flat(k.x[:, bass.ds(i * S + s, 1), :])
                        nc.vector.scalar_tensor_tensor(xs, k.bank[2 * s + 1][:, 0:P], am[s][:, 3:4], xs, ALU.mult, ALU.add).then_inc(done, 1)
                    order.close()

            @block.scalar
            def _(act):
                with act.Fori(0, TURNS) as i:
                    for s in range(S):
                        act.wait_ge(pe_r, i * S * PE + s + 1)
                        nc.scalar.copy(xqT[s][:], k.bank[2 * s][:].bitcast(BF16)[:, 0:P]).then_inc(ev, 1)
                    for s in range(S):
                        act.wait_ge(pe_r, i * S * PE + S + s + 1)
                        act.wait_ge(scaled, i * S + s + 1)
                        nc.scalar.activation(g[s][:], k.bank[2 * s][:], ACT.Silu, scale=up_scale[s][:, 0:1]).then_inc(act_r, 1)
                    for s in range(S):
                        act.wait_ge(pe_r, i * S * PE + 2 * S + s + 1)
                        nc.scalar.copy(flat(hqT[s][:]), k.bank[2 * s][:].bitcast(BF16)[:, 0:HID]).then_inc(ev, 1)

            @block.tensor
            def _(pe):
                mm = nc.tensor.matmul
                with pe.Fori(0, TURNS) as i:
                    for s in range(S):
                        pe.wait_ge(xq_r, i * S + s + 1)
                        nc.tensor.transpose(k.bank[2 * s][:].bitcast(BF16)[:, 0:P], xq[s][:], w["ident_bf"][:]).then_inc(pe_r, 1)
                    for s in range(S):
                        pe.wait_ge(ev, i * S * 2 + s + 1)
                        mm(k.bank[2 * s][:], xqT[s][:], w["tern_gate"][:], start=True, stop=True)
                        mm(k.bank[2 * s + 1][:], xqT[s][:], w["tern_up"][:], start=True, stop=True).then_inc(pe_r, 1)
                    for s in range(S):
                        pe.wait_ge(hq_r, i * S + s + 1)
                        for c in range(4):
                            ins = nc.tensor.transpose(k.bank[2 * s][:].bitcast(BF16)[:, c * P:(c + 1) * P], hq[s][:, c * P:(c + 1) * P], w["ident_bf"][:])
                        ins.then_inc(pe_r, 1)
                    for s in range(S):
                        pe.wait_ge(ev, i * S * 2 + S + s + 1)
                        for c in range(4):
                            ins = mm(k.bank[2 * s + 1][:, 0:P], hqT[s][:, c, :], w["tern_down"][:, c * P:(c + 1) * P], start=(c == 0), stop=(c == 3))
                        ins.then_inc(pe_r, 1)


def stage_fourier(k):
    nc, w, S = k.nc, k.w, 4
    TURNS = B // S
    with ExitStack() as local:
        sb = lambda n, s, d=F32: [k.sb(f"fo_{n}{j}", s, d, local) for j in range(S)]
        six, two, rstd, xn, xnT = sb("six", [P, T2, 6]), sb("two", [P, T2, 2]), sb("rstd", [P, T2]), sb("xn", [P, T2, P]), sb("xnT", [P, L])
        sem = lambda n: k.sem("fo_" + n)
        stats, rs, n0 = k.norms(B)
        xn_r, pe_r, ev, done = (sem(n) for n in ("xn", "pe", "evac", "done"))
        with nc.Block() as block:
            @block.gpsimd
            def _(pool):
                with pool.Fori(0, TURNS) as i:
                    order = Order(k, pool, "pool", i, TURNS, S)
                    for s in range(S):
                        pool.wait_ge(stats, n0 + i * S + s + 1)
                        rstd_on_pool(k, order, two[s][:, :, 1], rstd[s][:], T2).then_inc(rs, 1)
                    order.close()

            @block.vector
            def _(v):
                with v.Fori(0, TURNS) as i:
                    order = Order(k, v, "dve", i, TURNS, 2 * S)
                    for s in range(S):
                        ln_stats(k, order, k.x[:, bass.ds((i * S + s) * T2, T2), :], six[s], two[s], lambda ins: ins.then_inc(stats, 1))
                    for s in range(S):
                        v.wait_ge(rs, n0 + i * S + s + 1)
                        for t in range(T2):
                            ins = nc.vector.tensor_scalar(xn[s][:, t, :], flat(k.x[:, bass.ds((i * S + s) * T2 + t, 1), :]),
                                                          two[s][:, t, 0:1], rstd[s][:, t:t + 1], ALU.subtract, ALU.mult)
                        ins.then_inc(xn_r, 1)
                    for s in range(S):
                        xs = k.x[:, bass.ds((i * S + s) * T2, T2), :]
                        v.wait_ge(xn_r, i * S + s + 1)
                        order.mark(nc.vector.tensor_tensor(xs, xs, w["L2_bias"][:].unsqueeze(1).to_broadcast([P, T2, P]), ALU.add))
                        order.settle()
                        v.wait_ge(pe_r, i * S * 2 + S + s + 1)
                        nc.vector.tensor_tensor(xs, xs, k.bank[2 * s + 1][:, 0:L].rearrange("p (t d) -> p t d", t=T2), ALU.add).then_inc(done, 1)
                    order.close()

            @block.scalar
            def _(act):
                with act.Fori(0, TURNS) as i:
                    for s in range(S):
                        act.wait_ge(pe_r, i * S * 2 + s + 1)
                        nc.scalar.copy(xnT[s][:], k.bank[2 * s][:, 0:L]).then_inc(ev, 1)

            @block.tensor
            def _(pe):
                with pe.Fori(0, TURNS) as i:
                    for s in range(S):
                        pe.wait_ge(xn_r, i * S + s + 1)
                        for t in range(T2):
                            ins = nc.tensor.transpose(k.bank[2 * s][:, t * P:(t + 1) * P], xn[s][:, t, :], w["ident"][:])
                        ins.then_inc(pe_r, 1)
                    for s in range(S):
                        pe.wait_ge(ev, i * S + s + 1)
                        for t in range(T2):
                            ins = nc.tensor.matmul(k.bank[2 * s + 1][:, t * P:(t + 1) * P], xnT[s][:, t * P:(t + 1) * P], w["fourier"][:], start=True, stop=True)
                        ins.then_inc(pe_r, 1)


def norm_and_transpose(k, xnT):
    nc, w, T = k.nc, k.w, 4
    with ExitStack() as local:
        six, two, rstd = (k.sb(f"nt{k.normed}_{n}", s, F32, local) for n, s in (("six", [P, NT, 6]), ("two", [P, NT, 2]), ("rstd", [P, NT])))
        xn = k.sb(f"nt{k.normed}_xn", [P, NT, P], F32, local)
        stats, rs, n0 = k.norms(1)
        with nc.Block() as block:
            @block.gpsimd
            def _(pool):
                order = Order(k, pool, "pool")
                pool.wait_ge(stats, n0 + 1)
                rstd_on_pool(k, order, two[:, :, 1], rstd[:], NT).then_inc(rs, 1)
                order.close()

            @block.vector
            def _(v):
                order = Order(k, v, "dve")
                ln_stats(k, order, k.x, six, two, lambda ins: ins.then_inc(stats, 1))
                order.close()
                v.wait_ge(rs, n0 + 1)
                for t in range(NT):
                    ins = nc.vector.tensor_scalar(xn[:, t, :], k.x[:, t, :], two[:, t, 0:1], rstd[:, t:t + 1], ALU.subtract, ALU.mult)
                    if t % T == T - 1:
                        ins.then_inc(k.all_xn, 1)

            @block.scalar
            def _(act):
                for j in range(NT // T):
                    act.wait_ge(k.all_ps, k.alls + j + 1)
                    nc.scalar.copy(flat(xnT[:, j * T:(j + 1) * T, :]), k.bank[j][:]).then_inc(k.all_ev, 1)

            @block.tensor
            def _(pe):
                for j in range(NT // T):
                    pe.wait_ge(k.all_xn, k.alls + j + 1)
                    for t in range(T):
                        ins = nc.tensor.transpose(k.bank[j][:, t * P:(t + 1) * P], xn[:, j * T + t, :], w["ident"][:])
                    ins.then_inc(k.all_ps, 1)
        k.alls += NT // T


def stage_causal_attention(k):
    nc, w, S = k.nc, k.w, 2
    TURNS, H, D = B // S, 16, 64
    PAIRS, SCALE = H // 2, 64 ** -0.5
    NS, NR, NB, NP = 3, 5, 2, 3
    TSK, OSK = 3, 5
    with ExitStack() as local:
        sb = lambda n, s, d=F32, c=S: [k.sb(f"ca_{n}{j}", s, d, local) for j in range(c)]
        xnT = k.sb("ca_xnT", [P, NT, P], ctx=local)
        norm_and_transpose(k, xnT)
        ctxT = sb("ctxT", [P, L])
        q, kk, val, heads = sb("q", [P, H, L]), sb("k", [P, PAIRS, L]), sb("v", [P, T2, H * D]), sb("heads", [P, PAIRS, L])
        bar, ln1, z, zc = sb("bar", [P, 3 * P]), sb("len", [P, 1]), sb("z", [P, 1]), sb("zc", [P, 1])
        nz = sb("nz", [P, 1])
        sm, mx, nmx, den = sb("sm", [P, 3 * P], c=NR), sb("mx", [P, 2], c=NR), sb("nmx", [P, 2], c=NR), sb("den", [P, 2], c=NR)
        rden, prob = sb("rden", [P, 2], c=NR), sb("prob", [P, 3 * P], c=NR)
        pT = sb("pT", [P, 4 * P], c=NP * S)
        sem = lambda n: k.sem("ca_" + n)
        ctx_in = [sem(f"ctx_in{j}") for j in range(S)]
        ctx_used, proj, pev, vev = (sem(n) for n in ("ctx_used", "proj", "qk", "v"))
        bar_r, s_ps, s_sm, ex, rd, nrm, t_ps, t_ev, o_ps, o_ev, y_ps, done = (
            sem(n) for n in ("bar", "scores", "masked", "exp", "rden", "norm", "pT_ps", "pT", "o_ps", "heads", "y_ps", "done"))
        v_ps, kev = sem("v_ps"), sem("kev")
        HS = S * H
        NPROJ = 2 * PAIRS

        with nc.Block() as block:
            @block.sync
            def _(sp):
                with sp.Fori(0, TURNS) as i:
                    for s in range(S):
                        n = i * S + s
                        sp.wait_ge(ctx_used, n + 1)
                        sp.dma_start(ctxT[s][:], k.d["ctxT"][bass.ds(n, 1)].rearrange("b d l -> (b d) l")).then_inc(ctx_in[s], 16)

            @block.gpsimd
            def _(pool):
                with pool.Fori(0, TURNS) as i:
                    for g in range(HS):
                        s, m = g // H, g % NR
                        pool.wait_ge(rd, i * HS + g + 1)
                        k.carry(pool)
                        nc.gpsimd.tensor_scalar(prob[m][:, 0:P], prob[m][:, 0:P], rden[m][:, 0:1], zc[s][:, 0:1], ALU.mult, ALU.add)
                        nc.gpsimd.tensor_scalar(prob[m][:, P:3 * P], prob[m][:, P:3 * P], rden[m][:, 1:2], zc[s][:, 0:1], ALU.mult, ALU.add).then_inc(nrm, 1)

            def head_sum(v, order, i, g):
                s, m = g // H, g % NR
                v.wait_ge(ex, i * HS + g + 1)
                order.mark(nc.vector.reciprocal(rden[m][:], den[m][:]))
                order.settle()
                nc.vector.tensor_scalar(rden[m][:], rden[m][:], nz[s][:, 0:1], None, ALU.mult).then_inc(rd, 1)

            @block.vector
            def _(v):
                v.sem_inc(ctx_used, S)
                v.sem_inc(done, S)
                with v.Fori(0, TURNS) as i:
                    order = Order(k, v, "dve", i, TURNS, 4 * S + 2 * HS)
                    for s in range(S):
                        order.mark(nc.vector.tensor_copy(ln1[s][:], w["lens"][:, bass.ds(i * S + s, 1)]))
                    order.settle()
                    for s in range(S):
                        nc.vector.tensor_scalar(z[s][:], ln1[s][:], 0.0, None, ALU.is_le)
                        order.mark(nc.vector.tensor_scalar(bar[s][:], w["iota_k"][:], ln1[s][:, 0:1], NEG, ALU.is_ge, ALU.mult))
                    order.settle()
                    for s in range(S):
                        nc.vector.tensor_scalar(nz[s][:], z[s][:], -1.0, 1.0, ALU.mult, ALU.add)
                        nc.vector.tensor_scalar(zc[s][:], z[s][:], 1.0 / L, None, ALU.mult)
                        order.mark(nc.vector.tensor_tensor(bar[s][:], bar[s][:], w["causal"][:], ALU.add))
                    order.settle()
                    for s in range(S):
                        for r in range(NP):
                            ins = nc.vector.tensor_scalar(pT[s * NP + r][:, 0:P], w["ident"][:], 0.0, zc[s][:, 0:1], ALU.mult, ALU.add)
                        ins.then_inc(bar_r, 1)
                    for s in range(S):
                        for p in range(PAIRS):
                            v.wait_ge(proj, i * S * NPROJ + s * NPROJ + 2 * p + 1)
                            for o in range(2):
                                ins = nc.vector.tensor_scalar(q[s][:, 2 * p + o, :], k.bank[2 * (p % 2)][:, 0:L], w["L1_bQ"][:, p:p + 1], w["head_pick"][:, o:o + 1], ALU.add, ALU.mult)
                            ins.then_inc(pev, 1)
                    for g in range(HS):
                        s, m = g // H, g % NR
                        v.wait_ge(s_ps, i * HS + g + 1)
                        if g >= NR:
                            v.wait_ge(ex, i * HS + g - NR + 1)
                        k.carry(v)
                        for a, b, j in ((0, P, 0), (P, 3 * P, 1)):
                            ins = nc.vector.tensor_tensor_reduce(out=sm[m][:, a:b], in0=k.bank[2 + g % NS][:, a:b], in1=bar[s][:, a:b], scale=1.0, scalar=2 * NEG,
                                                                 op0=ALU.add, op1=ALU.max, accum_out=mx[m][:, j:j + 1])
                        order.mark(ins)
                        order.settle()
                        nc.vector.tensor_scalar(nmx[m][:], mx[m][:], -SCALE, None, ALU.mult).then_inc(s_sm, 1)
                        if g >= 1:
                            head_sum(v, order, i, g - 1)
                    head_sum(v, order, i, HS - 1)
                    for s in range(S):
                        xs = k.x[:, bass.ds((i * S + s) * T2, T2), :]
                        order.mark(nc.vector.tensor_tensor(xs, xs, w["L1_bO"][:].unsqueeze(1).to_broadcast([P, T2, P]), ALU.add))
                        order.settle()
                        v.wait_ge(y_ps, i * S + s + 1)
                        nc.vector.tensor_tensor(xs, xs, k.bank[s][:, 0:L].rearrange("p (t d) -> p t d", t=T2), ALU.add).then_inc(done, 1)
                    order.close()

            def head_out(act, i, pr):
                act.wait_ge(o_ps, i * HS + 2 * pr + 2)
                nc.scalar.activation(heads[pr // PAIRS][:, pr % PAIRS, :], k.bank[(7, 1)[pr % 2]][:, 0:L], ACT.Identity,
                                     bias=w["L1_bV"][:, pr % PAIRS:pr % PAIRS + 1]).then_inc(o_ev, 1)

            @block.scalar
            def _(act):
                with act.Fori(0, TURNS) as i:
                    for s in range(S):
                        for t in range(T2):
                            for c in range(2):
                                j = (s * T2 + t) * 2 + c
                                act.wait_ge(v_ps, i * S * 4 + j + 1)
                                nc.scalar.copy(val[s][:, t, c * 512:(c + 1) * 512], k.bank[5 + j % 2][:]).then_inc(vev, 1)
                    for s in range(S):
                        for p in range(PAIRS):
                            act.wait_ge(proj, i * S * NPROJ + s * NPROJ + 2 * p + 2)
                            nc.scalar.activation(kk[s][:, p, :], k.bank[2 * (p % 2) + 1][:, 0:L], ACT.Identity, bias=w["L1_bK"][:, p:p + 1]).then_inc(kev, 1)
                        act.sem_inc(ctx_used, 1)
                    for g in range(HS + TSK - 1):
                        if g < HS:
                            m = g % NR
                            act.wait_ge(s_sm, i * HS + g + 1)
                            if g >= NR:
                                act.wait_ge(t_ps, i * HS + g - NR + 1)
                            nc.scalar.activation(prob[m][:, 0:P], sm[m][:, 0:P], ACT.Exp, bias=nmx[m][:, 0:1], scale=SCALE, accum_out=den[m][:, 0:1])
                            nc.scalar.activation(prob[m][:, P:3 * P], sm[m][:, P:3 * P], ACT.Exp, bias=nmx[m][:, 1:2], scale=SCALE, accum_out=den[m][:, 1:2]).then_inc(ex, 1)
                        h = g - TSK + 1
                        if h >= 0:
                            r = h // H * NP + h % NP
                            act.wait_ge(t_ps, i * HS + h + 1)
                            if h >= NP:
                                act.wait_ge(o_ps, i * HS + h - NP + 1)
                            nc.scalar.copy(pT[r][:, P:4 * P], k.bank[5 + h % NB][:, 0:3 * P]).then_inc(t_ev, 1)
                            if h >= 4 and h % 2 == 0:
                                head_out(act, i, (h - 4) // 2)
                    head_out(act, i, HS // 2 - 2)
                    head_out(act, i, HS // 2 - 1)

            @block.tensor
            def _(pe):
                mm = nc.tensor.matmul
                with pe.Fori(0, TURNS) as i:
                    for s in range(S):
                        pe.wait_ge(ctx_in[s], i * 16 + 16)
                        for t in range(T2):
                            for c in range(2):
                                j = (s * T2 + t) * 2 + c
                                if j >= 2:
                                    pe.wait_ge(vev, i * S * 4 + j - 1)
                                mm(k.bank[5 + j % 2][:], ctxT[s][:, t * P:(t + 1) * P], w["L1_WV"][:, c * 512:(c + 1) * 512], start=True, stop=True).then_inc(v_ps, 1)
                    for s in range(S):
                        for p in range(PAIRS):
                            a, done_q = s * PAIRS + p, i * S * PAIRS + s * PAIRS + p
                            if a == 0:
                                pe.wait_ge(done, (i + 1) * S)
                            if a >= 2:
                                pe.wait_ge(pev, done_q - 1)
                                pe.wait_ge(kev, done_q - 1)
                            mm(k.bank[2 * (p % 2)][:, 0:L], w["L1_WQ"][:, p * P:(p + 1) * P], flat(xnT[:, bass.ds((i * S + s) * T2, T2), :]), start=True, stop=True).then_inc(proj, 1)
                            mm(k.bank[2 * (p % 2) + 1][:, 0:L], w["L1_WK"][:, p * P:(p + 1) * P], ctxT[s][:], start=True, stop=True).then_inc(proj, 1)
                    pe.wait_ge(vev, (i + 1) * S * 4)
                    pe.wait_ge(pev, (i + 1) * S * PAIRS)
                    pe.wait_ge(kev, (i + 1) * S * PAIRS)
                    for g in range(HS + OSK):
                        if g < HS:
                            s, h, bank = g // H, g % H, k.bank[2 + g % NS]
                            if g >= NS:
                                pe.wait_ge(s_sm, i * HS + g - NS + 1)
                            mm(bank[:, 0:P], q[s][:, h, 0:P], kk[s][:, h // 2, 0:P], start=True, stop=True)
                            mm(bank[:, P:3 * P], q[s][:, h, P:2 * P], kk[s][:, h // 2, :], start=True, stop=True).then_inc(s_ps, 1)
                        if TSK <= g < HS + TSK:
                            u = g - TSK
                            pe.wait_ge(nrm, i * HS + u + 1)
                            if u >= NB:
                                pe.wait_ge(t_ev, i * HS + u - NB + 1)
                            for c in range(3):
                                ins = nc.tensor.transpose(k.bank[5 + u % NB][:, c * P:(c + 1) * P], prob[u % NR][:, c * P:(c + 1) * P], w["ident"][:])
                            ins.then_inc(t_ps, 1)
                        if g >= OSK:
                            u = g - OSK
                            s, h, pr = u // H, u % H, u // 2
                            pe.wait_ge(t_ev, i * HS + u + 1)
                            if h == 0:
                                pe.wait_ge(bar_r, i * S + s + 1)
                            if h % 2 == 0 and pr >= 2:
                                pe.wait_ge(o_ev, i * PAIRS * S + pr - 1)
                            o = k.bank[(7, 1)[pr % 2]][(h % 2) * D:(h % 2 + 1) * D, 0:L]
                            r = pT[s * NP + u % NP]
                            mm(o, val[s][:, 0, h * D:(h + 1) * D], r[:, P:3 * P], start=True, stop=False)
                            mm(o.rearrange("p (a b) -> p a b", a=2), val[s][:, 1, h * D:(h + 1) * D], r[:].rearrange("p (a b) -> p a b", b=P)[:, 0:4:3, :],
                               start=False, stop=True).then_inc(o_ps, 1)
                    for s in range(S):
                        pe.wait_ge(o_ev, i * PAIRS * S + (s + 1) * PAIRS)
                        for t in range(T2):
                            for p in range(PAIRS):
                                ins = mm(k.bank[s][:, t * P:(t + 1) * P], heads[s][:, p, t * P:(t + 1) * P], w["L1_WO"][:, p, :], start=(p == 0), stop=(p == PAIRS - 1))
                        ins.then_inc(y_ps, 1)


def stage_experts(k, tag, loaded, first, second, act_fn, shared, top, bias):
    nc, w, T = k.nc, k.w, 4
    TURNS, N, RE = NT // T, T * P, 8
    E = RE + shared
    UPS, DOWNS, XTS = (2, 3, 6), (4, 5), (0, 7)
    NU, ND = len(UPS), len(DOWNS)
    KINDS = 2 if bias else 1
    with ExitStack() as local:
        sb = lambda n, s, d=F32, c=None: (k.sb(f"{tag}_{n}", s, d, local) if c is None else [k.sb(f"{tag}_{n}{j}", s, d, local) for j in range(c)])
        six, two, rstd, sq, r2 = sb("six", [P, NT, 6]), sb("two", [P, NT, 2]), sb("rstd", [P, NT]), sb("sq", [P, NT]), sb("r2", [P, NT])
        back, both, xn, xT = sb("back", [P, NT]), sb("both", [P, NT]), sb("xn", [P, NT, P]), sb("xT", [P, TURNS, N])
        x_in = sb("x_in", [P, N], c=2) if bias else None
        x_high, x_low = sb("x_high", [P, TURNS, N], F32R, c=KINDS), sb("x_low", [P, TURNS, N], F32R, c=KINDS)
        first_high, first_low = sb("first_high", [P, E, 512], F32R), sb("first_low", [P, E, 512], F32R)
        h = sb("h", [P, 4, N], c=2)
        logit, mx, val = sb("logit", [P, NT, RE]), sb("mx", [P, NT]), sb("val", [P, NT, RE])
        above, tie, rank = sb("above", [P, NT, RE * RE]), sb("tie", [P, NT, RE * RE]), sb("rank", [P, NT, RE])
        den, gate, gateT = sb("den", [P, NT]), sb("gate", [P, NT, E]), sb("gateT", [E, N])
        gate_now = sb("gate_now", [P, T, E])
        sem = lambda n: k.sem(f"{tag}_" + n)
        stats, rs, n0 = k.norms(1)
        xn_r, xT_ps, xT_r, halves, w_high, w_low = (sem(n) for n in ("xn", "xT_ps", "xT", "x_halves", "w_high", "w_low"))
        logit_ps, soft, gate_r, now_r, gT_ps, gT_r = (sem(n) for n in ("logit_ps", "soft", "gate", "gate_now", "gateT_ps", "gateT"))
        up_ps, act_r, dn_ps, done = sem("up_ps"), sem("hidden"), sem("down_ps"), sem("done")
        as_f32 = lambda ap: ap.bitcast(F32)
        with nc.Block() as block:
            @block.gpsimd
            def _(pool):
                order = Order(k, pool, "pool")
                pool.wait_ge(stats, n0 + 1)
                ins = rstd_on_pool(k, order, two[:, :, 1], rstd[:], NT)
                if bias:
                    for factor in (two[:, :, 1], sq[:]):
                        order.mark(ins)
                        order.settle()
                        ins = nc.gpsimd.tensor_tensor(sq[:], factor, rstd[:], ALU.mult)
                    order.mark(ins)
                    order.settle()
                    order.mark(rstd_on_pool(k, order, sq[:], r2[:], NT, EPS_RMS))
                    order.settle()
                    ins = nc.gpsimd.tensor_tensor(both[:], rstd[:], r2[:], ALU.mult)
                ins.then_inc(rs, 1)
                order.close()
                with pool.Fori(0, E) as e:
                    pool.wait_ge(w_high, e + 1)
                    of = lambda x: flat(x[:, bass.ds(e, 1), :])
                    nc.gpsimd.tensor_tensor(of(first_low), of(first), as_f32(of(first_high)), ALU.subtract).then_inc(w_low, 1)

            def gates(v, order):
                tt, ts = nc.vector.tensor_tensor, nc.vector.tensor_scalar
                v.wait_ge(logit_ps, TURNS)
                if bias:
                    v.wait_ge(soft, 1)
                    order.mark(ts(val[:], val[:], 1.0, None, ALU.add))
                    order.settle()
                    order.mark(nc.vector.reciprocal(val[:], val[:]))
                    order.settle()
                else:
                    lg = k.bank[1][:, 0:NT * RE].rearrange("p (t e) -> p t e", t=NT)
                    order.mark(nc.vector.tensor_reduce(mx[:], lg, AX.X, ALU.max))
                    order.settle()
                    tt(logit[:], lg, mx[:].unsqueeze(2).to_broadcast([P, NT, RE]), ALU.subtract).then_inc(gate_r, 1)
                    v.wait_ge(soft, 1)
                mine = val[:].unsqueeze(3).to_broadcast([P, NT, RE, RE])
                other = val[:].unsqueeze(2).to_broadcast([P, NT, RE, RE])
                grid = lambda x: x[:].rearrange("p t (e j) -> p t e j", e=RE)
                tt(grid(above), other, mine, ALU.is_gt)
                order.mark(tt(grid(tie), other, mine, ALU.is_equal))
                order.settle()
                order.mark(tt(tie[:], tie[:], w["prefix"][:].rearrange("p a b -> p (a b)").unsqueeze(1).to_broadcast([P, NT, RE * RE]), ALU.mult))
                order.settle()
                order.mark(tt(above[:], above[:], tie[:], ALU.add))
                order.settle()
                order.mark(nc.vector.tensor_reduce(rank[:], grid(above), AX.X, ALU.add))
                order.settle()
                order.mark(ts(rank[:], rank[:], float(top), None, ALU.is_lt))
                order.settle()
                order.mark(tt(rank[:], rank[:], val[:], ALU.mult))
                order.settle()
                order.mark(nc.vector.tensor_reduce(den[:], val[:] if bias else rank[:], AX.X, ALU.add))
                order.settle()
                order.mark(nc.vector.reciprocal(den[:], den[:]))
                order.settle()
                tt(gate[:, :, 0:RE], rank[:], den[:].unsqueeze(2).to_broadcast([P, NT, RE]), ALU.mult).then_inc(gate_r, 1)
                v.wait_ge(gate_r, 2)

            @block.vector
            def _(v):
                tt, ts = nc.vector.tensor_tensor, nc.vector.tensor_scalar
                first_order = Order(k, v, "dve")
                for t in range(NT):
                    ins = nc.vector.bn_stats(six[:, t, :], k.x[:, t, :])
                first_order.mark(ins)
                first_order.settle()
                for t in range(NT):
                    ins = nc.vector.bn_aggr(two[:, t, :], six[:, t, :])
                ins.then_inc(stats, 1)
                if bias:
                    nc.vector.memset(gate[:], 1.0)
                v.wait_ge(loaded, 32)
                with v.Fori(0, E) as e:
                    nc.vector.tensor_copy(flat(first_high[:, bass.ds(e, 1), :]), flat(first[:, bass.ds(e, 1), :])).then_inc(w_high, 1)
                v.wait_ge(rs, n0 + 1)
                for t in range(NT):
                    ins = ts(xn[:, t, :], k.x[:, t, :], two[:, t, 0:1], (both if bias else rstd)[:, t:t + 1], ALU.subtract, ALU.mult)
                    if t % T == T - 1:
                        ins.then_inc(xn_r, 1)
                if bias:
                    first_order.mark(nc.vector.reciprocal(back[:], r2[:]))
                    first_order.settle()
                    ts(back[:], back[:], -1.0, None, ALU.mult).then_inc(gate_r, 1)
                first_order.close()
                order = Order(k, v, "dve")
                for j in range(TURNS):
                    v.wait_ge(xT_r, j + 1)
                    if bias:
                        for kind in range(KINDS):
                            ins = ts(x_in[kind][:], xT[:, j, :], w["L3_g"][:, kind:kind + 1], None, ALU.mult)
                        order.mark(ins)
                        order.settle()
                    src = [x[:] for x in x_in] if bias else [xT[:, j, :]]
                    for kind in range(KINDS):
                        ins = nc.vector.tensor_copy(x_high[kind][:, j, :], src[kind])
                    order.mark(ins)
                    order.settle()
                    for kind in range(KINDS):
                        ins = order.mark(tt(x_low[kind][:, j, :], src[kind], as_f32(x_high[kind][:, j, :]), ALU.subtract))
                    order.settle()
                    v.sem_inc(halves, 1)
                order.close()
                v.sem_inc(done, ND)
                v.sem_inc(gT_r, 1)
                last_order = Order(k, v, "dve")
                if bias:
                    for t in range(NT):
                        ins = ts(xn[:, t, :], k.x[:, t, :], two[:, t, 0:1], rstd[:, t:t + 1], ALU.subtract, ALU.mult)
                    last_order.mark(ins)
                    last_order.settle()
                    last_order.mark(tt(k.x[:], k.x[:], xn[:], ALU.add))
                gates(v, last_order)
                last_order.close()
                with v.Fori(0, TURNS) as i:
                    nc.vector.tensor_copy(gate_now[:], gate[:, bass.ds(i * T, T), :]).then_inc(now_r, 1)
                    v.wait_ge(now_r, i + 1)
                    for e in range(E):
                        if bias and e == E - 2:
                            v.wait_ge(gT_ps, i + 1)
                            nc.vector.tensor_copy(gateT[:], k.bank[1][0:E, 0:N]).then_inc(gT_r, 1)
                        v.wait_ge(dn_ps, i * E + e + 1)
                        for t in range(T):
                            xt = flat(k.x[:, bass.ds(i * T + t, 1), :])
                            ins = nc.vector.scalar_tensor_tensor(xt, k.bank[DOWNS[e % ND]][:, t * P:(t + 1) * P], gate_now[:, t, e:e + 1], xt, ALU.mult, ALU.add)
                        ins.then_inc(done, 1)
                        v.wait_ge(done, i * E + e + 1 + ND)

            @block.scalar
            def _(act):
                for j in range(TURNS):
                    act.wait_ge(xT_ps, j + 1)
                    nc.scalar.copy(xT[:, j, :], k.bank[XTS[j % 2]][:]).then_inc(xT_r, 1)
                if bias:
                    act.wait_ge(gate_r, 1)
                    act.wait_ge(logit_ps, TURNS)
                    for t in range(NT):
                        ins = nc.scalar.activation(val[:, t, :], k.bank[1][:, t * RE:(t + 1) * RE], ACT.Exp, scale=back[:, t:t + 1])
                    ins.then_inc(soft, 1)
                else:
                    act.wait_ge(gate_r, 1)
                    nc.scalar.activation(val[:], logit[:], ACT.Exp).then_inc(soft, 1)
                with act.Fori(0, TURNS) as i:
                    for e in range(E):
                        for c in range(4):
                            u = e * 4 + c
                            act.wait_ge(up_ps, i * E * 4 + u + 1)
                            if c == 0 and e >= 2:
                                act.wait_ge(dn_ps, i * E + e - 1)
                            nc.scalar.activation(h[e % 2][:, c, :], k.bank[UPS[u % NU]][:], act_fn, bias=w["L3_b1"][:, u:u + 1] if bias else 0.0).then_inc(act_r, 1)

            def logits(pe, j):
                pe.wait_ge(xT_r, j + 1)
                for t in range(T):
                    at = (j * T + t) * RE
                    ins = nc.tensor.matmul(k.bank[1][:, at:at + RE], xT[:, j, t * P:(t + 1) * P], w["L3_centroids" if bias else "L1_router"][:], start=True, stop=True)
                ins.then_inc(logit_ps, 1)

            def down(pe, i, e):
                pe.wait_ge(done, i * E + e + 1)
                pe.wait_ge(act_r, i * E * 4 + e * 4 + 4)
                gated = bias and e == E - 1
                if gated:
                    pe.wait_ge(gT_r, i + 2)
                for t in range(T):
                    o = k.bank[DOWNS[e % ND]][:, t * P:(t + 1) * P]
                    for c in range(4):
                        ins = nc.tensor.matmul(o, h[e % 2][:, c, t * P:(t + 1) * P], second[:, e, c * P:(c + 1) * P], start=(c == 0), stop=(c == 3 and not gated))
                    if gated:
                        ins = nc.tensor.matmul(o, gateT[:, t * P:(t + 1) * P], w["L3_b2"][:], start=False, stop=True)
                ins.then_inc(dn_ps, 1)

            @block.tensor
            def _(pe):
                for j in range(TURNS):
                    pe.wait_ge(xn_r, j + 1)
                    if j >= 2:
                        pe.wait_ge(xT_r, j - 1)
                    for t in range(T):
                        ins = nc.tensor.transpose(k.bank[XTS[j % 2]][:, t * P:(t + 1) * P], xn[:, j * T + t, :], w["ident"][:])
                    ins.then_inc(xT_ps, 1)
                    if j >= 1:
                        logits(pe, j - 1)
                logits(pe, TURNS - 1)
                pe.wait_ge(loaded, 32)
                with pe.Fori(0, TURNS) as i:
                    pe.wait_ge(halves, i + 1)
                    for e in range(E):
                        pe.wait_ge(w_low, e + 1)
                        kind = 0 if e >= RE else KINDS - 1
                        turn = lambda x: flat(x[kind][:, bass.ds(i, 1), :])
                        for c in range(4):
                            u = e * 4 + c
                            if u >= NU:
                                pe.wait_ge(act_r, i * E * 4 + u - NU + 1)
                            hidden = k.bank[UPS[u % NU]][:]
                            high, low = (x[:, e, c * P:(c + 1) * P] for x in (first_high, first_low))
                            nc.tensor.matmul(hidden, high, turn(x_high), start=True, stop=False)
                            nc.tensor.matmul(hidden, high, turn(x_low), start=False, stop=False)
                            nc.tensor.matmul(hidden, low, turn(x_high), start=False, stop=True).then_inc(up_ps, 1)
                        if bias and e == E - 2:
                            pe.wait_ge(now_r, i + 1)
                            pe.wait_ge(gT_r, i + 1)
                            for t in range(T):
                                ins = nc.tensor.transpose(k.bank[1][0:E, t * P:(t + 1) * P], gate_now[:, t, :], w["ident"][:])
                            ins.then_inc(gT_ps, 1)
                        if e >= 1:
                            down(pe, i, e - 1)
                    down(pe, i, E - 1)


def stage_load_last(k):
    k.layer1.close()
    for n in ("L3_W1", "L3_W2"):
        k.w[n] = k.sb("w_" + n, [P, 10, 512])
    k.last_loaded = k.sem("last_loaded")
    with k.nc.Block() as block:
        @block.sync
        def _(sp):
            sp.wait_ge(k.big_loaded, 32)
            for n in ("L3_W1", "L3_W2"):
                sp.dma_start(k.w[n][:], k.d[n]).then_inc(k.last_loaded, 16)


def stage_experts_gelu(k):
    stage_experts(k, "e1", k.big_loaded, k.w["up_w"], k.w["down_w"], ACT.Gelu_apprx_tanh, 0, 4, False)


def stage_experts_shared(k):
    stage_experts(k, "e3", k.last_loaded, k.w["L3_W1"], k.w["L3_W2"], ACT.Gelu, 2, 2, True)


def stage_self_attention(k):
    nc, w, S = k.nc, k.w, 4
    TURNS = B // S
    k.y = k.sb("y_stream", [P, NT, P], F32, k.layer2)
    with ExitStack() as local:
        sb = lambda n, s, d=F32: [k.sb(f"sa_{n}{j}", s, d, local) for j in range(S)]
        six, two, rstd, xn, xnT = sb("six", [P, T2, 6]), sb("two", [P, T2, 2]), sb("rstd", [P, T2]), sb("xn", [P, T2, P]), sb("xnT", [P, L])
        t = sb("t", [P, T2, P])
        sem = lambda n: k.sem("sa_" + n)
        stats, rs, n0 = k.norms(2 * B)
        xn_r, pe_r, ev = (sem(n) for n in ("xn", "pe", "evac"))
        with nc.Block() as block:
            @block.gpsimd
            def _(pool):
                with pool.Fori(0, TURNS) as i:
                    order = Order(k, pool, "pool", i, TURNS, 2 * S)
                    for part in range(2):
                        for s in range(S):
                            pool.wait_ge(stats, n0 + (i * 2 + part) * S + s + 1)
                            rstd_on_pool(k, order, two[s][:, :, 1], rstd[s][:], T2).then_inc(rs, 1)
                    order.close()

            @block.vector
            def _(v):
                with v.Fori(0, TURNS) as i:
                    order = Order(k, v, "dve", i, TURNS, 7 * S)
                    for s in range(S):
                        ln_stats(k, order, k.x[:, bass.ds((i * S + s) * T2, T2), :], six[s], two[s], lambda ins: ins.then_inc(stats, 1))
                    for s in range(S):
                        v.wait_ge(rs, n0 + i * 2 * S + s + 1)
                        for j in range(T2):
                            ins = nc.vector.tensor_scalar(xn[s][:, j, :], flat(k.x[:, bass.ds((i * S + s) * T2 + j, 1), :]),
                                                          two[s][:, j, 0:1], rstd[s][:, j:j + 1], ALU.subtract, ALU.mult)
                        ins.then_inc(xn_r, 1)
                    for s in range(S):
                        v.wait_ge(xn_r, i * S + s + 1)
                        order.mark(nc.vector.tensor_tensor(t[s][:], xn[s][:], w["sa_bias"][:].unsqueeze(1).to_broadcast([P, T2, P]), ALU.add))
                        order.settle()
                        v.wait_ge(pe_r, i * S * 2 + S + s + 1)
                        order.mark(nc.vector.tensor_tensor(t[s][:], t[s][:], k.bank[2 * s + 1][:, 0:L].rearrange("p (t d) -> p t d", t=T2), ALU.add))
                        order.settle()
                        ln_stats(k, order, t[s], six[s], two[s], lambda ins: ins.then_inc(stats, 1))
                    for s in range(S):
                        v.wait_ge(rs, n0 + (i * 2 + 1) * S + s + 1)
                        apply_gain(k, order, t[s], two[s], rstd[s], w["L2_vecs"][:, 1, :], w["L2_vecs"][:, 2, :], k.y[:, bass.ds((i * S + s) * T2, T2), :])
                    order.close()

            @block.scalar
            def _(act):
                with act.Fori(0, TURNS) as i:
                    for s in range(S):
                        act.wait_ge(pe_r, i * S * 2 + s + 1)
                        nc.scalar.copy(xnT[s][:], k.bank[2 * s][:, 0:L]).then_inc(ev, 1)

            @block.tensor
            def _(pe):
                with pe.Fori(0, TURNS) as i:
                    for s in range(S):
                        pe.wait_ge(xn_r, i * S + s + 1)
                        for j in range(T2):
                            ins = nc.tensor.transpose(k.bank[2 * s][:, j * P:(j + 1) * P], xn[s][:, j, :], w["ident"][:])
                        ins.then_inc(pe_r, 1)
                    for s in range(S):
                        pe.wait_ge(ev, i * S + s + 1)
                        for j in range(T2):
                            ins = nc.tensor.matmul(k.bank[2 * s + 1][:, j * P:(j + 1) * P], xnT[s][:, j * P:(j + 1) * P], w["sa"][:], start=True, stop=True)
                        ins.then_inc(pe_r, 1)


def apply_gain(k, order, t, two, rstd, gain, offset, dst):
    nc = k.nc
    for j in range(T2):
        ins = nc.vector.tensor_scalar(t[:, j, :], t[:, j, :], two[:, j, 0:1], rstd[:, j:j + 1], ALU.subtract, ALU.mult)
    order.mark(ins)
    order.settle()
    order.mark(nc.vector.tensor_tensor(t[:], t[:], gain.unsqueeze(1).to_broadcast([P, T2, P]), ALU.mult))
    order.settle()
    return order.mark(nc.vector.tensor_tensor(dst, t[:], offset.unsqueeze(1).to_broadcast([P, T2, P]), ALU.add))


def stage_relu_ffn(k):
    nc, w, S = k.nc, k.w, 4
    TURNS = B // S
    with ExitStack() as local:
        sb = lambda n, s, d=F32: [k.sb(f"rf_{n}{j}", s, d, local) for j in range(S)]
        six, two, rstd, yT = sb("six", [P, T2, 6]), sb("two", [P, T2, 2]), sb("rstd", [P, T2]), sb("yT", [P, L])
        t, y2, h = sb("t", [P, T2, P]), sb("y2", [P, T2, P]), sb("h", [P, 4, L])
        sem = lambda n: k.sem("rf_" + n)
        stats, rs, n0 = k.norms(2 * B)
        y_r, pe_r, ev = (sem(n) for n in ("y", "pe", "evac"))
        PE, EV = 4, 3
        with nc.Block() as block:
            @block.gpsimd
            def _(pool):
                with pool.Fori(0, TURNS) as i:
                    order = Order(k, pool, "pool", i, TURNS, 2 * S)
                    for part in range(2):
                        for s in range(S):
                            pool.wait_ge(stats, n0 + (i * 2 + part) * S + s + 1)
                            rstd_on_pool(k, order, two[s][:, :, 1], rstd[s][:], T2).then_inc(rs, 1)
                    order.close()

            @block.vector
            def _(v):
                with v.Fori(0, TURNS) as i:
                    order = Order(k, v, "dve", i, TURNS, 11 * S)
                    for s in range(S):
                        ys = k.y[:, bass.ds((i * S + s) * T2, T2), :]
                        order.mark(nc.vector.tensor_copy(t[s][:], ys))
                        order.settle()
                        ln_stats(k, order, t[s], six[s], two[s], lambda ins: ins.then_inc(stats, 1))
                    for s in range(S):
                        v.wait_ge(rs, n0 + i * 2 * S + s + 1)
                        apply_gain(k, order, t[s], two[s], rstd[s], w["L2_vecs"][:, 3, :], w["L2_vecs"][:, 4, :], y2[s][:])
                        order.settle()
                        nc.vector.tensor_tensor(t[s][:], y2[s][:], w["L2_vecs"][:, 5, :].unsqueeze(1).to_broadcast([P, T2, P]), ALU.add).then_inc(y_r, 1)
                    for s in range(S):
                        v.wait_ge(y_r, i * S + s + 1)
                        v.wait_ge(pe_r, i * S * PE + 3 * S + s + 1)
                        order.mark(nc.vector.tensor_tensor(t[s][:], t[s][:], k.bank[2 * s][:, L:2 * L].rearrange("p (t d) -> p t d", t=T2), ALU.add))
                        order.settle()
                        ln_stats(k, order, t[s], six[s], two[s], lambda ins: ins.then_inc(stats, 1))
                    for s in range(S):
                        v.wait_ge(rs, n0 + (i * 2 + 1) * S + s + 1)
                        apply_gain(k, order, t[s], two[s], rstd[s], w["L2_vecs"][:, 6, :], w["L2_vecs"][:, 7, :], y2[s][:])
                        order.settle()
                        xs = k.x[:, bass.ds((i * S + s) * T2, T2), :]
                        order.mark(nc.vector.tensor_tensor(xs, xs, y2[s][:], ALU.add))
                    order.close()

            @block.scalar
            def _(act):
                with act.Fori(0, TURNS) as i:
                    for s in range(S):
                        act.wait_ge(pe_r, i * S * PE + s + 1)
                        nc.scalar.copy(yT[s][:], k.bank[2 * s][:, 0:L]).then_inc(ev, 1)
                    for c in range(2):
                        for s in range(S):
                            act.wait_ge(pe_r, i * S * PE + (1 + c) * S + s + 1)
                            for m in range(2):
                                ins = nc.scalar.activation(h[s][:, 2 * c + m, :], k.bank[2 * s + 1][:, m * L:(m + 1) * L], ACT.Relu, bias=w["L2_lin1b"][:, 2 * c + m:2 * c + m + 1])
                            ins.then_inc(ev, 1)

            @block.tensor
            def _(pe):
                mm = nc.tensor.matmul
                with pe.Fori(0, TURNS) as i:
                    for s in range(S):
                        pe.wait_ge(y_r, i * S + s + 1)
                        for j in range(T2):
                            ins = nc.tensor.transpose(k.bank[2 * s][:, j * P:(j + 1) * P], y2[s][:, j, :], w["ident"][:])
                        ins.then_inc(pe_r, 1)
                    for c in range(2):
                        for s in range(S):
                            pe.wait_ge(ev, i * S * EV + c * S + s + 1)
                            for m in range(2):
                                ins = mm(k.bank[2 * s + 1][:, m * L:(m + 1) * L], w["L2_lin1T"][:, (2 * c + m) * P:(2 * c + m + 1) * P], yT[s][:], start=True, stop=True)
                            ins.then_inc(pe_r, 1)
                    for s in range(S):
                        pe.wait_ge(ev, i * S * EV + 2 * S + s + 1)
                        for j in range(T2):
                            for c in range(4):
                                ins = mm(k.bank[2 * s][:, L + j * P:L + (j + 1) * P], h[s][:, c, j * P:(j + 1) * P], w["L2_lin2T"][:, c, :], start=(c == 0), stop=(c == 3))
                        ins.then_inc(pe_r, 1)


def bf16_parts(value):
    parts, rest = [], np.float32(value)
    for _ in range(3):
        bits = np.array(rest, np.float32).view(np.uint32)
        part = ((bits + np.uint32(0x7FFF) + ((bits >> np.uint32(16)) & np.uint32(1))) & np.uint32(0xFFFF0000)).view(np.float32)
        parts.append(float(part))
        rest = np.float32(rest - part)
    return parts


def stage_cross_attention(k, tag, H, stream, norm, masked):
    nc, w, S = k.nc, k.w, 2
    TURNS, D = B // S, P // H
    R, HL, HB, G = 6 * D, H * L, H // 2, H // 4
    ROWS = R + (6 if masked else 3)
    SCALE = float(D) ** -0.5
    stack = nc.dram_tensor(f"{tag}_stack", [B, 2, ROWS * HL], BF16).ap()
    maxima = nc.dram_tensor(f"{tag}_maxima", [B, 2, 6 * HB * P], BF16).ap()
    NS, NE, NP = 3, 2, 3
    HS = S * H
    NB = 3 if 6 * HB <= 32 else P // (2 * HB)
    with ExitStack() as local:
        sb = lambda n, s, d=F32, c=S: [k.sb(f"{tag}_{n}{j}", s, d, local) for j in range(c)]
        mask = k.sb(f"{tag}_mask", [P, B * L], F32, local) if masked else None
        ctxT, six, two, rstd = sb("ctxT", [P, L]), sb("six", [P, T2, 6]), sb("two", [P, T2, 2]), sb("rstd", [P, T2])
        xn, xnT, qk, rest = sb("xn", [P, T2, P]), sb("xnT", [P, L]), sb("qk", [P, 2 * L]), sb("rest", [P, 2 * L])
        parts = sb("parts", [P, 3, 2 * L], BF16)
        qs, ks = sb("qs", [P, HL], BF16), sb("ks", [P, HL], BF16)
        val = sb("val", [P, T2, H, 32])
        nmax, nrest, nparts, nT = sb("nmax", [P, 2 * H]), sb("nrest", [P, 2 * HB]), sb("nparts", [P, NB, 2 * HB], BF16), sb("nT", [6 * HB, P], BF16)
        prob = sb("prob", [P, 2, L], c=NP)
        out32, rden, o, oT = sb("out32", [P, G, L]), sb("rden", [P, H]), sb("o", [P, T2, P]), sb("oT", [P, L])
        mrow, mfloat, mpart = (k.sb(f"{tag}_mrow", [B, L], U8, local), k.sb(f"{tag}_mfloat", [B, L], F32, local), k.sb(f"{tag}_mpart", [B, 3, L], BF16, local)) if masked else (None,) * 3
        sem = lambda n: k.sem(f"{tag}_" + n)
        each = lambda n: [sem(f"{n}{j}") for j in range(S)]
        ctx_in, wrote, stacked, nwrote = each("ctx_in"), each("wrote"), each("stacked"), each("nwrote")
        nrow = [each("nrow_a"), each("nrow_b")]
        stats, rs, n0 = k.norms(B if norm else 0)
        fill, xn_r, ev, part_r, v_r, pe_r = (sem(n) for n in ("fill", "xn", "evac", "parts", "v", "front_ps"))
        s_ps, mx_r, np_r, nt_ps, nt_r, e_ps, ex_r, pv_ps, o_ev = (sem(n) for n in ("s_ps", "max", "nparts", "nT_ps", "nT", "e_ps", "exp", "pv_ps", "out32"))
        out_ps, o_r, done, const_r = sem("out_ps"), sem("o"), sem("done"), sem("const")
        FR = 3

        with nc.Block() as block:
            @block.sync
            def _(sp):
                sp.dma_start(stack[:, 0, R * HL:ROWS * HL].rearrange("b (r c) -> b r c", c=HL), k.d["stack_fill"][0:1, 0:ROWS - R, 0:HL].to_broadcast([B, ROWS - R, HL])).then_inc(fill, 16)
                sp.dma_start(stack[:, 1, R * HL:(R + 3) * HL].rearrange("b (r c) -> b r c", c=HL), k.d["stack_fill"][1:2, 0:3, 0:HL].to_broadcast([B, 3, HL])).then_inc(fill, 16)
                if masked:
                    sp.dma_start(mrow[:], k.d["mask_rows"]).then_inc(fill, 16)
                    sp.wait_ge(const_r, 1)
                    for j in range(3):
                        sp.dma_start(stack[:, 1, (R + 3 + j) * HL:(R + 4 + j) * HL].rearrange("b (h t) -> b h t", h=H), mpart[:, j, :].unsqueeze(1).to_broadcast([B, H, L])).then_inc(fill, 16)
                sp.wait_ge(fill, 16 * (6 if masked else 2))
                sp.wait_ge(const_r, 2 if masked else 1)
                with sp.Fori(0, TURNS) as i:
                    for s in range(S):
                        n = i * S + s
                        sp.wait_ge(done, n + 1)
                        sp.dma_start(ctxT[s][:], k.d["ctxT"][bass.ds(n, 1)].rearrange("b d l -> (b d) l")).then_inc(ctx_in[s], 16)
                    for s in range(S):
                        n = i * S + s
                        sp.wait_ge(part_r, n + 1)
                        slot = lambda qk_, a, b: stack[bass.ds(n, 1), qk_, a * P * L:b * P * L].rearrange("b (j p t) -> p (b j) t", p=P, t=L)
                        for a, b, j in ((0, 3, 0), (3, 5, 1), (5, 6, 2)):
                            sp.dma_start(slot(0, a, b), parts[s][:, j:j + 1, 0:L].to_broadcast([P, b - a, L])).then_inc(wrote[s], 16)
                            sp.dma_start(slot(1, a, b), parts[s][:, 0:b - a, L:2 * L]).then_inc(wrote[s], 16)
                        sp.wait_ge(wrote[s], (i + 1) * 96)
                        for qk_, dst in ((0, qs), (1, ks)):
                            sp.dma_start(dst[s][0:ROWS, :], stack[bass.ds(n, 1), qk_, :].rearrange("b (r c) -> (b r) c", c=HL)).then_inc(stacked[s], 16)
                    for s in range(S):
                        n = i * S + s
                        for half in range(2):
                            sp.wait_ge(nt_r, (i * S + s) * 2 + half + 1)
                            mx = maxima[bass.ds(n, 1), half, :]
                            sp.dma_start(mx.rearrange("b (c q) -> (b c) q", q=P), nT[s][:]).then_inc(nwrote[s], 16)
                            sp.wait_ge(nwrote[s], (i * 2 + half + 1) * 16)
                            sp.dma_start(qs[s][R:R + 3, half * HB * L:(half + 1) * HB * L], mx.rearrange("b (r c) -> (b r) c", r=3)).then_inc(nrow[half][s], 16)

            @block.gpsimd
            def _(pool):
                if norm:
                    with pool.Fori(0, TURNS) as i:
                        order = Order(k, pool, "pool", i, TURNS, S)
                        for s in range(S):
                            pool.wait_ge(stats, n0 + i * S + s + 1)
                            rstd_on_pool(k, order, two[s][:, :, 1], rstd[s][:], T2).then_inc(rs, 1)
                        order.close()

            @block.vector
            def _(v):
                tt, ts, cp = nc.vector.tensor_tensor, nc.vector.tensor_scalar, nc.vector.tensor_copy
                order = Order(k, v, "dve")
                if masked:
                    order.mark(cp(mask[:], w["mask_bytes"][:]))
                    v.wait_ge(fill, 48)
                    order.mark(cp(mfloat[:], mrow[:]))
                    order.settle()
                    order.mark(ts(mfloat[:], mfloat[:], -1.0, 1.0, ALU.mult, ALU.add))
                    order.settle()
                    for j, c in enumerate(bf16_parts(-1e4 * np.sqrt(np.float32(D)))):
                        ins = ts(mpart[:, j, :], mfloat[:], c, None, ALU.mult)
                    ins.then_inc(const_r, 1)
                for s in range(S):
                    nc.vector.memset(qs[s][:], 0.0)
                    nc.vector.memset(ks[s][:], 0.0)
                    nc.vector.memset(nparts[s][:], 0.0)
                    ins = nc.vector.memset(val[s][:], 0.0)
                order.mark(ins)
                order.settle()
                for s in range(S):
                    ins = nc.vector.memset(val[s][:, :, :, 0:1], 1.0)
                ins.then_inc(const_r, 1)
                v.sem_inc(done, S)
                order.close()
                with v.Fori(0, TURNS) as i:
                    order = Order(k, v, "dve", i, TURNS, (S if norm else 0) + 15 * S)
                    st = lambda s, n=T2, j=0: stream[:, bass.ds((i * S + s) * T2 + j, n), :]
                    for s in range(S):
                        if norm:
                            ln_stats(k, order, st(s), six[s], two[s], lambda ins: ins.then_inc(stats, 1))
                    for s in range(S):
                        if norm:
                            v.wait_ge(rs, n0 + i * S + s + 1)
                            for j in range(T2):
                                ins = ts(xn[s][:, j, :], flat(st(s, 1, j)), two[s][:, j, 0:1], rstd[s][:, j:j + 1], ALU.subtract, ALU.mult)
                        else:
                            ins = cp(xn[s][:], st(s))
                        ins.then_inc(xn_r, 1)
                    for s in range(S):
                        v.wait_ge(pe_r, i * S * FR + S + s + 1)
                        ts(qk[s][:, 0:L], k.bank[s][:, 0:L], w[f"{tag}_bq"][:, 0:1], None, ALU.add)
                        if masked:
                            order.mark(nc.vector.scalar_tensor_tensor(qk[s][:, L:2 * L], k.bank[s][:, L:2 * L], w[f"{tag}_bk"][:, 0:1], mask[:, bass.ds((i * S + s) * L, L)], ALU.add, ALU.mult))
                        else:
                            order.mark(ts(qk[s][:, L:2 * L], k.bank[s][:, L:2 * L], w[f"{tag}_bk"][:, 0:1], None, ALU.add))
                        order.settle()
                        order.mark(cp(parts[s][:, 0, :], qk[s][:]))
                        order.settle()
                        order.mark(tt(rest[s][:], qk[s][:], parts[s][:, 0, :], ALU.subtract))
                        order.settle()
                        order.mark(cp(parts[s][:, 1, :], rest[s][:]))
                        order.settle()
                        tt(parts[s][:, 2, :], rest[s][:], parts[s][:, 1, :], ALU.subtract).then_inc(part_r, 1)
                    for s in range(S):
                        v.wait_ge(pe_r, i * S * FR + 2 * S + s + 1)
                        for j in range(T2):
                            ins = tt(val[s][:, j, :, 1:1 + D], k.bank[2 + s][:, j * P:(j + 1) * P].rearrange("p (h d) -> p h d", h=H),
                                     w[f"{tag}_bv"][:].rearrange("p (h d) -> p h d", h=H), ALU.add)
                        order.mark(ins)
                    order.settle()
                    cp(rden[0][:, 0:1], val[0][:, 0, 0, 0:1]).then_inc(v_r, 1)
                    for u in range(HS):
                        s, h = u // H, u % H
                        v.wait_ge(s_ps, i * HS + u + 1)
                        nc.vector.tensor_reduce(nmax[s][:, 2 * h:2 * h + 2], k.bank[2 + u % NS][:].rearrange("p (t l) -> p t l", t=2), AX.X, ALU.max, negate=True).then_inc(mx_r, 1)
                        if h % HB == HB - 1:
                            half = h // HB
                            src = nmax[s][:, half * 2 * HB:(half + 1) * 2 * HB]
                            v.wait_ge(mx_r, i * HS + u + 1)
                            order.mark(cp(nparts[s][:, 0, :], src))
                            order.settle()
                            order.mark(tt(nrest[s][:], src, nparts[s][:, 0, :], ALU.subtract))
                            order.settle()
                            order.mark(cp(nparts[s][:, 1, :], nrest[s][:]))
                            order.settle()
                            tt(nparts[s][:, 2, :], nrest[s][:], nparts[s][:, 1, :], ALU.subtract).then_inc(np_r, 1)
                            j = s * 2 + half
                            v.wait_ge(nt_ps, i * S * 2 + j + 1)
                            cp(nT[s][:], k.bank[1][:].bitcast(BF16)[0:6 * HB, 0:P]).then_inc(nt_r, 1)
                    for s in range(S):
                        v.wait_ge(out_ps, i * S * 3 + s + 1)
                        for j in range(T2):
                            heads = k.bank[1 + 2 * s + j][:, 0:G * P].rearrange("p (h c) -> p h c", c=32)
                            order.mark(nc.vector.reciprocal(rden[s][:], heads[:, :, 0]))
                            order.settle()
                            ins = tt(o[s][:, j, :].rearrange("p (h d) -> p h d", h=H), heads[:, :, 1:1 + D], rden[s][:].unsqueeze(2).to_broadcast([P, H, D]), ALU.mult)
                            if j == 0:
                                order.mark(ins)
                                order.settle()
                        ins.then_inc(o_r, 1)
                    for s in range(S):
                        order.mark(tt(st(s), st(s), w[f"{tag}_bo"][:].unsqueeze(1).to_broadcast([P, T2, P]), ALU.add))
                        order.settle()
                        v.wait_ge(out_ps, i * S * 3 + 2 * S + s + 1)
                        tt(st(s), st(s), k.bank[5 + s][:, L:2 * L].rearrange("p (t d) -> p t d", t=T2), ALU.add).then_inc(done, 1)
                    order.close()

            def gather(act, i, g):
                act.wait_ge(pv_ps, i * HS + 4 * g + 4)
                nc.scalar.copy(out32[g // G][:, g % G, :], k.bank[(7, 0)[g % 2]][:, 0:L]).then_inc(o_ev, 1)

            @block.scalar
            def _(act):
                with act.Fori(0, TURNS) as i:
                    for s in range(S):
                        act.wait_ge(pe_r, i * S * FR + s + 1)
                        nc.scalar.copy(xnT[s][:], k.bank[s][:, 0:L]).then_inc(ev, 1)
                    for u in range(HS):
                        act.wait_ge(e_ps, i * HS + u + 1)
                        if u >= NP:
                            act.wait_ge(pv_ps, i * HS + u - NP + 1)
                        nc.scalar.activation(flat(prob[u % NP][:]), k.bank[5 + u % NE][:], ACT.Exp, scale=SCALE).then_inc(ex_r, 1)
                        if u % 4 == 1 and u > 4:
                            gather(act, i, u // 4 - 1)
                    gather(act, i, HS // 4 - 1)
                    for s in range(S):
                        act.wait_ge(out_ps, i * S * 3 + S + s + 1)
                        nc.scalar.copy(oT[s][:], k.bank[5 + s][:, 0:L]).then_inc(ev, 1)

            def new_maxima(pe, i, j):
                s = j // 2
                pe.wait_ge(np_r, i * S * 2 + j + 1)
                nc.tensor.transpose(k.bank[1][:].bitcast(BF16)[0:2 * NB * HB, 0:P], flat(nparts[s][:]), w["ident_bf"][:]).then_inc(nt_ps, 1)

            def head_values(pe, i, u):
                s, h, g = u // H, u % H, u // 4
                pe.wait_ge(ex_r, i * HS + u + 1)
                if u % 4 == 0 and g >= 2:
                    pe.wait_ge(o_ev, i * (HS // 4) + g - 1)
                r = 32 * (h % 4)
                for c in range(2):
                    ins = nc.tensor.matmul(k.bank[(7, 0)[g % 2]][r:r + 32, 0:L], val[s][:, c, h, :], prob[u % NP][:, c, :], start=(c == 0), stop=(c == 1), tile_position=(0, r))
                ins.then_inc(pv_ps, 1)

            @block.tensor
            def _(pe):
                mm = nc.tensor.matmul
                with pe.Fori(0, TURNS) as i:
                    for s in range(S):
                        pe.wait_ge(xn_r, i * S + s + 1)
                        for j in range(T2):
                            ins = nc.tensor.transpose(k.bank[s][:, j * P:(j + 1) * P], xn[s][:, j, :], w["ident"][:])
                        ins.then_inc(pe_r, 1)
                    for s in range(S):
                        pe.wait_ge(ev, i * S * 2 + s + 1)
                        pe.wait_ge(ctx_in[s], i * 16 + 16)
                        mm(k.bank[s][:, 0:L], w[f"{tag}_wq"][:], xnT[s][:], start=True, stop=True)
                        mm(k.bank[s][:, L:2 * L], w[f"{tag}_wk"][:], ctxT[s][:], start=True, stop=True).then_inc(pe_r, 1)
                    for s in range(S):
                        for j in range(T2):
                            ins = mm(k.bank[2 + s][:, j * P:(j + 1) * P], ctxT[s][:, j * P:(j + 1) * P], w[f"{tag}_wv"][:], start=True, stop=True)
                        ins.then_inc(pe_r, 1)
                    pe.wait_ge(v_r, i + 1)
                    for u in range(HS + H + 1):
                        if u < HS:
                            s, h = u // H, u % H
                            if h == 0:
                                pe.wait_ge(stacked[s], (i + 1) * 32)
                            if u >= NS:
                                pe.wait_ge(mx_r, i * HS + u - NS + 1)
                            for j in range(2):
                                ins = mm(k.bank[2 + u % NS][:, j * L:(j + 1) * L], qs[s][:, h * L + j * P:h * L + (j + 1) * P], ks[s][:, h * L:(h + 1) * L], start=True, stop=True)
                            ins.then_inc(s_ps, 1)
                        if u > HB and u <= 2 * HS and (u - 1) % HB == 0 and (u - 1) // HB - 1 < 2 * S:
                            new_maxima(pe, i, (u - 1) // HB - 1)
                        if H <= u < H + HS:
                            x = u - H
                            s, h = x // H, x % H
                            if h % HB == 0:
                                pe.wait_ge(nrow[h // HB][s], i * 16 + 16)
                            if x >= NE:
                                pe.wait_ge(ex_r, i * HS + x - NE + 1)
                            for c in range(2):
                                ins = mm(k.bank[5 + x % NE][:, c * L:(c + 1) * L], ks[s][:, h * L + c * P:h * L + (c + 1) * P], qs[s][:, h * L:(h + 1) * L], start=True, stop=True)
                            ins.then_inc(e_ps, 1)
                        if u > H:
                            head_values(pe, i, u - H - 1)
                    for s in range(S):
                        pe.wait_ge(o_ev, i * (HS // 4) + (s + 1) * G)
                        for j in range(2):
                            for g in range(G):
                                ins = nc.tensor.transpose(k.bank[1 + 2 * s + j][:, g * P:(g + 1) * P], out32[s][:, g, j * P:(j + 1) * P], w["ident"][:])
                        ins.then_inc(out_ps, 1)
                    for s in range(S):
                        pe.wait_ge(o_r, i * S + s + 1)
                        for j in range(2):
                            ins = nc.tensor.transpose(k.bank[5 + s][:, j * P:(j + 1) * P], o[s][:, j, :], w["ident"][:])
                        ins.then_inc(out_ps, 1)
                    for s in range(S):
                        pe.wait_ge(ev, i * S * 2 + S + s + 1)
                        for j in range(2):
                            ins = mm(k.bank[5 + s][:, L + j * P:L + (j + 1) * P], oT[s][:, j * P:(j + 1) * P], w[f"{tag}_wo"][:], start=True, stop=True)
                        ins.then_inc(out_ps, 1)


def stage_attention_8(k):
    stage_cross_attention(k, "L2", 8, k.y, False, False)


def stage_attention_16(k):
    stage_cross_attention(k, "L3", 16, k.x, True, True)


def stage_store(k):
    stored = k.sem("stored")
    with k.nc.Block() as block:
        @block.sync
        def _(sp):
            sp.dma_start(k.out.rearrange("b (t p) d -> p (b t) d", p=P), k.x[:]).then_inc(stored, 16)
            sp.wait_ge(stored, 16)


LAYERS = [("layer0", [stage_autocorrelation, stage_ternary_ffn]),
          ("layer1", [stage_causal_attention, stage_experts_gelu, stage_load_last]),
          ("layer2", [stage_self_attention, stage_attention_8, stage_relu_ffn]),
          ("rest", [stage_fourier, stage_attention_16, stage_experts_shared])]


def host_layout(a):
    bf16 = mybir.dt.np(BF16)

    f = np.float32
    t = {}
    rows = lambda v: np.ascontiguousarray(np.broadcast_to(v, (P,) + v.shape))
    cols = lambda v, n: np.ascontiguousarray(v.reshape(n, P).T)
    t["x"] = a["x"]
    t["ctx"] = a["ctx_1024"]
    t["ctxT"] = np.ascontiguousarray(a["ctx_1024"].transpose(0, 2, 1))
    t["ternary"] = np.ascontiguousarray(np.stack([
        a["L0_ffn_w_gate"].T, a["L0_ffn_w_up"].T,
        a["L0_ffn_w_down"].T.reshape(4, P, P).transpose(1, 0, 2).reshape(P, 512)], 1))
    t["mask_bytes"] = a["mask_BxS2_bf1"].view(np.uint8).reshape(B * L)
    t["mask_rows"] = a["mask_BxS2_bf1"].view(np.uint8)
    t["lens"] = a["_lenS2"]
    t["ident"] = np.eye(P, dtype=f)
    t["ident_bf"] = np.eye(P, dtype=bf16)
    tok, fr = np.arange(L)[:, None], np.arange(P)[None, :]
    cosine, sine = np.cos(2 * np.pi * tok * fr / L), np.sin(2 * np.pi * tok * fr / L)
    nyq = (-1.0) ** np.arange(L)
    second = sine.copy()
    second[:, 0] = nyq
    t["dft"] = np.ascontiguousarray(np.concatenate([cosine, second], 1).reshape(T2, P, L).transpose(1, 0, 2)).astype(f)
    first_i, second_i = 2 * cosine.T / L, -2 * sine.T / L
    first_i[0] = 1.0 / L
    second_i[0] = nyq / L
    t["idft"] = np.ascontiguousarray(np.stack([first_i, second_i], 1)).astype(f)
    ch = np.arange(P)
    t["head_block"] = (ch[:, None] // 8 == ch[None, :] // 8).astype(f)
    out_row = 2 * (ch % 8 * 16 + ch // 8)
    spread = np.zeros((P, T2, 2, P), f)
    for half in range(2):
        spread[ch, (out_row + half) // P, half, (out_row + half) % P] = 1
    t["spread_rows"] = spread.reshape(P, 4 * P)
    t["iota8"] = rows(np.arange(8, dtype=f))
    t["rolled_base"] = (ch % 8 + L).astype(f)[:, None]
    t["not_first"] = (ch > 0).astype(f)[:, None]
    ang = 2 * np.pi * (ch[:, None] * ch[None, :] % P) / P
    t["fourier_cos"], t["fourier_sin"], t["fourier_nsin"] = np.cos(ang).astype(f), np.sin(ang).astype(f), (-np.sin(ang)).astype(f)
    kk = np.concatenate([np.arange(P), np.arange(L)])
    qq = np.concatenate([np.zeros(P), np.full(L, P)])
    t["iota_k"] = rows(kk.astype(f))
    t["causal"] = np.where(kk[None] <= qq[None] + ch[:, None], 0, NEG).astype(f)
    t["head_pick"] = np.stack([ch < 64, ch >= 64], 1).astype(f)
    t["prefix"] = rows((np.arange(8)[None, :] < np.arange(8)[:, None]).astype(f))
    for n in ("wq", "wk", "wv", "wo"):
        t["q0_" + n] = a["L0_xattn_" + n]
    for n in ("Q", "K", "V"):
        t["L1_W" + n] = np.ascontiguousarray(a["L1_xattn_W" + n].transpose(1, 0, 2).reshape(P, 1024))
        t["L1_b" + n] = cols(a["L1_xattn_b" + n], 8)
    t["L1_WO"] = np.ascontiguousarray(a["L1_xattn_WO"].reshape(8, P, P).transpose(1, 0, 2))
    t["L1_bO"] = rows(a["L1_xattn_bO"])
    t["L1_router"] = a["L1_ffn_router_w"]
    t["L1_up_w"] = np.ascontiguousarray(a["L1_ffn_up_w"].transpose(1, 0, 2))
    t["L1_down_w"] = np.ascontiguousarray(a["L1_ffn_down_w"].reshape(8, 4, P, P).transpose(2, 0, 1, 3).reshape(P, 8, 512))
    t["L2_ffn_w_freq_real"], t["L2_ffn_w_freq_imag"] = a["L2_ffn_w_freq_real"], a["L2_ffn_w_freq_imag"]
    t["L2_bias"] = rows(a["L2_ffn_bias"])
    t["L2_saT"] = np.ascontiguousarray(a["L2_xattn_sa_out_w"].T)
    t["L2_sa_v"] = np.ascontiguousarray(a["L2_xattn_qkv_w"][2 * P:])
    t["L2_sa_vb"] = np.ascontiguousarray(np.broadcast_to(a["L2_xattn_qkv_b"][2 * P:, None], (P, P)))
    t["L2_vecs"] = rows(np.stack([a["L2_xattn_" + n] for n in ("sa_out_b", "ln1_g", "ln1_b", "ln2_g", "ln2_b", "lin2_b", "ln3_g", "ln3_b")]))
    t["L2_lin1T"] = np.ascontiguousarray(a["L2_xattn_lin1_w"].T)
    t["L2_lin1b"] = cols(a["L2_xattn_lin1_b"], 4)
    t["L2_lin2T"] = np.ascontiguousarray(a["L2_xattn_lin2_w"].T.reshape(4, P, P).transpose(1, 0, 2))
    for name, heads, ws, bs, wo, bo in (
            ("L2", 8, np.split(a["L2_xattn_in_proj_w"], 3), np.split(a["L2_xattn_in_proj_b"], 3), a["L2_xattn_mha_out_w"], a["L2_xattn_mha_out_b"]),
            ("L3", 16, [a["L3_xattn_W" + n] for n in "qkv"], [a["L3_xattn_b" + n] for n in "qkv"], a["L3_xattn_Wo"], a["L3_xattn_bo"])):
        by_dim = np.arange(P).reshape(heads, P // heads).T.reshape(P)
        t[name + "_wq"], t[name + "_wk"] = (np.ascontiguousarray(m.T[:, by_dim]) for m in ws[:2])
        t[name + "_bq"], t[name + "_bk"] = (np.ascontiguousarray(v[by_dim][:, None]) for v in bs[:2])
        t[name + "_wv"], t[name + "_bv"] = np.ascontiguousarray(ws[2].T), rows(bs[2])
        t[name + "_wo"], t[name + "_bo"] = np.ascontiguousarray(wo.T), rows(bo)
    t["stack_fill"] = np.stack([np.concatenate([np.zeros((3, 4096)), np.ones((3, 4096))]), np.concatenate([np.ones((3, 4096)), np.zeros((3, 4096))])]).astype(bf16)
    t["L3_centroids"] = a["L3_ffn_centroids"]
    t["L3_g"] = np.stack([a["L3_ffn_g_shared"], a["L3_ffn_g_routed"]], 1)
    both = lambda n: np.concatenate([a[f"L3_ffn_{n}_r"], a[f"L3_ffn_{n}_s"]])
    t["L3_W1"] = np.ascontiguousarray(both("W1").transpose(1, 0, 2))
    t["L3_W2"] = np.ascontiguousarray(both("W2").reshape(10, 4, P, P).transpose(2, 0, 1, 3).reshape(P, 10, 512))
    t["L3_b1"] = cols(both("b1").reshape(40, P), 40)
    t["L3_b2"] = both("b2")
    return t


def program(nc, dram, out, only=None):
    with ExitStack() as ctx:
        k = Kit(nc, ctx, dram, out)
        stage_setup(k)
        for name, stages in LAYERS:
            made = len(k.sems)
            for stage in stages:
                if only is None or stage in only:
                    stage(k)
            if name == "layer2":
                k.retire_semaphores(made)
            memory = {"layer0": k.layer0, "layer1": k.layer1, "layer2": k.layer2, "rest": k.rest}[name]
            memory.close()
        stage_store(k)


def kernel(**inputs):
    from concourse import bacc
    from concourse.bass_utils import run_bass_kernel_spmd

    arrays = host_layout(inputs)
    nc = bacc.Bacc("TRN2", target_bir_lowering=False, num_devices=1)
    dram = {n: nc.dram_tensor("in_" + n, v.shape, mybir.dt.from_np(v.dtype), kind="ExternalInput").ap() for n, v in arrays.items()}
    out = nc.dram_tensor("out", (B, L, P), F32, kind="ExternalOutput").ap()
    program(nc, dram, out)
    r = run_bass_kernel_spmd(nc, [{"in_" + n: v for n, v in arrays.items()}], core_ids=[0])
    return r.results[0]["out"]
```

```python
from contextlib import ExitStack

import concourse.bass as bass
import numpy as np
from concourse import mybir

F32, BF16, F32R = mybir.dt.float32, mybir.dt.bfloat16, mybir.dt.float32r
I32, U32, U8 = mybir.dt.int32, mybir.dt.uint32, mybir.dt.uint8
ACT, ALU, AX = mybir.ActivationFunctionType, mybir.AluOpType, mybir.AxisListType

P = 128
B, L = 8, 256
T2 = L // P
NT = B * T2
EPS = 1e-5
EPS_RMS = float(np.finfo(np.float32).eps)
ROUND = float(3 << 22)
NEG = -1e30


class Order:

    def __init__(self, k, eng, name, turn=0, turns=1, per=None):
        self.k, self.eng, self.name, self.turns, self.per = k, eng, name, turns, per
        self.count = 0
        self.start = k.ordered[name] + (turn * per if turns > 1 else 0)

    def mark(self, ins):
        self.count += 1
        return ins.then_inc(self.k.order[self.name], 1)

    def settle(self):
        self.eng.wait_ge(self.k.order[self.name], self.start + self.count)

    def settle_apart(self):
        self.settle()
        self.k.carry(self.eng)

    def close(self):
        assert self.turns == 1 or self.count == self.per, (self.name, self.count)
        self.k.ordered[self.name] += self.turns * self.count


class Kit:

    def __init__(self, nc, ctx, dram, out):
        self.nc, self.ctx, self.d, self.out = nc, ctx, dram, out
        self.order = {e: ctx.enter_context(nc.semaphore(f"{e}_order")) for e in ("dve", "act", "pool")}
        self.ordered = dict.fromkeys(self.order, 0)
        self.bank = [self.psum(f"bank{n}") for n in range(8)]
        self.x = self.sb("x_stream", [P, NT, P])
        self.sems = []
        self.tick, self.ticks = self.sb("tick", [1, 256]), 0
        self.stats, self.rstd, self.normed = self.sem("norm_stats"), self.sem("norm_rstd"), 0
        self.all_xn, self.all_ps, self.all_ev, self.alls = self.sem("all_xn"), self.sem("all_ps"), self.sem("all_ev"), 0
        self.norms_split = 0
        self.rest, self.layer2, self.layer1, self.layer0 = ExitStack(), ExitStack(), ExitStack(), ExitStack()
        self.w = {}

    def sb(self, name, shape, dt=F32, ctx=None):
        return (ctx or self.ctx).enter_context(self.nc.sbuf_tensor(name, shape, dt))

    def norms(self, count):
        self.normed += count
        return self.stats, self.rstd, self.normed - count

    def carry(self, eng):
        self.ticks += 1
        own = self.tick[:, self.ticks - 1:self.ticks]
        if eng is self.nc.gpsimd:
            eng.tensor_tensor(own, self.w["eps"][0:1, 0:1], self.w["eps"][0:1, 0:1], ALU.add)
        else:
            eng.memset(own, 0.0)

    def psum(self, name):
        return self.ctx.enter_context(self.nc.psum_tensor(name, [P, 512], F32))

    def sem(self, name):
        found = self.nc.alloc_semaphore(name=name)
        self.sems.append(found)
        return found

    def retire_semaphores(self, since):
        with self.nc.Block() as block:
            @block.gpsimd
            def _(pool):
                for s in self.sems[since:]:
                    pool.sem_clear(s)
        for s in self.sems[since:]:
            self.nc.release_semaphore(s)
        del self.sems[since:]


def flat(ap):
    return ap.rearrange("p a b -> p (a b)")


def stage_setup(k):
    nc = k.nc
    loaded = k.sem("setup_loaded")
    first = ["dft", "idft", "head_block", "iota8", "rolled_base", "not_first",
             "q0_wq", "q0_wk", "q0_wv", "q0_wo", "spread_rows", "fourier_cos", "fourier_sin", "fourier_nsin",
             "L2_ffn_w_freq_real", "L2_ffn_w_freq_imag", "L2_saT", "L2_sa_v", "L2_sa_vb"]
    kept = ["ident", "ident_bf", "L2_vecs"]
    later = ["L2_bias", "L2_lin1T", "L2_lin1b", "L2_lin2T",
             "L2_wq", "L2_wk", "L2_wv", "L2_wo", "L2_bq", "L2_bk", "L2_bv", "L2_bo",
             "L3_wq", "L3_wk", "L3_wv", "L3_wo", "L3_bq", "L3_bk", "L3_bv", "L3_bo",
             "L3_centroids", "L3_g", "L3_b1", "L3_b2", "prefix"]
    second = ["L1_WQ", "L1_WK", "L1_WV", "L1_WO", "L1_bQ", "L1_bK", "L1_bV", "L1_bO", "L1_router",
              "causal", "iota_k", "head_pick"]
    w = k.w
    k.later = later + second
    for n in kept + later:
        w[n] = k.sb("w_" + n, list(k.d[n].shape), k.d[n].dtype)
    n_small = 16 * (1 + len(kept + first))
    w["fourier"] = k.sb("fourier", [P, P])
    w["minus_half"] = k.sb("minus_half", [P, NT])
    w["eps"], w["eps_rms"] = k.sb("eps", [P, NT]), k.sb("eps_rms", [P, NT])
    w["sa"] = k.sb("sa", [P, P])
    w["sa_bias"] = k.sb("sa_bias", [P, P])
    w["mask_bytes"] = k.sb("mask_bytes", [P, B * L], U8)
    w["lens"], w["lens_int"] = k.sb("lens", [P, B]), k.sb("lens_int", [P, B], I32)
    for n in second:
        w[n] = k.sb("w_" + n, list(k.d[n].shape), k.d[n].dtype, k.layer1)
    for n in ("up_w", "down_w"):
        w[n] = k.sb(n, [P, 8, 512], F32, k.layer1)
    for n in first:
        w[n] = k.sb("w_" + n, list(k.d[n].shape), k.d[n].dtype, k.layer0)
    for n in ("gate", "up", "down"):
        w["tern_" + n] = k.sb("tern_" + n, [P, 512], BF16, k.layer0)
        w["scale_" + n] = k.sb("scale_" + n, [P, 1], F32, k.layer0)
    with ExitStack() as local:
        raw = k.sb("raw_ternary", [P, 3, 512], ctx=local)
        ratio = k.sb("ternary_ratio", [P, 3, 512], ctx=local)
        rowsum = k.sb("ternary_rowsum", [P, 3], ctx=local)
        inv = k.sb("ternary_inv", [P, 3], ctx=local)
        ones = k.sb("ones128", [P, P], ctx=local)
        spec = k.sb("fourier_ab", [P, 2, P], ctx=local)
        k.later_loaded, k.big_loaded, raw_loaded = k.sem("later_loaded"), k.sem("ffn1_loaded"), k.sem("raw_loaded")
        summed, spectra, mixed = k.sem("setup_summed"), k.sem("setup_spectra"), k.sem("setup_mixed")
        prepared = k.sem("setup_prepared")
        with nc.Block() as block:
            @block.sync
            def _(sp):
                sp.dma_start(raw[:], k.d["ternary"]).then_inc(raw_loaded, 16)
                sp.dma_start(k.x[:], k.d["x"].rearrange("b (t p) d -> p (b t) d", p=P)).then_inc(loaded, 16)
                for n in kept + first:
                    sp.dma_start(w[n][:], k.d[n]).then_inc(loaded, 16)

            @block.vector
            def _(v):
                order = Order(k, v, "dve")
                nc.vector.memset(ones[:], 1.0)
                nc.vector.memset(w["eps"][:], EPS)
                nc.vector.memset(w["eps_rms"][:], EPS_RMS)
                nc.vector.memset(w["minus_half"][:], -0.5).then_inc(prepared, 1)
                v.wait_ge(raw_loaded, 16)
                order.mark(nc.vector.tensor_reduce(rowsum[:], raw[:], AX.X, ALU.add, apply_absolute_value=True))
                order.settle()
                nc.vector.tensor_scalar(rowsum[:], rowsum[:], 1.0 / (512 * P), None, ALU.mult).then_inc(prepared, 1)
                v.wait_ge(summed, 1)
                order.mark(nc.vector.tensor_scalar(rowsum[:], k.bank[0][:, 0:3], EPS, None, ALU.max))
                order.settle()
                order.mark(nc.vector.reciprocal(inv[:], rowsum[:]))
                order.settle()
                for j, n in enumerate(("gate", "up", "down")):
                    order.mark(nc.vector.tensor_scalar(ratio[:, j, :], raw[:, j, :], inv[:, j:j + 1], ROUND, ALU.mult, ALU.add))
                    order.settle()
                    order.mark(nc.vector.tensor_scalar(ratio[:, j, :], ratio[:, j, :], -ROUND, 1.0, ALU.add, ALU.min))
                    order.settle()
                    nc.vector.tensor_scalar(w["tern_" + n][:], ratio[:, j, :], -1.0, None, ALU.max)
                    order.mark(nc.vector.tensor_copy(w["scale_" + n][:], rowsum[:, j:j + 1]))
                v.wait_ge(loaded, n_small)
                v.wait_ge(spectra, 1)
                nc.vector.tensor_copy(flat(spec[:]), k.bank[1][:, 0:2 * P]).then_inc(prepared, 1)
                v.wait_ge(mixed, 1)
                nc.vector.tensor_scalar(w["fourier"][:], k.bank[2][:, 0:P], 1.0 / P, None, ALU.mult)
                nc.vector.tensor_tensor(w["sa"][:], k.bank[3][:, 0:P], w["ident"][:], ALU.add)
                order.mark(nc.vector.tensor_tensor(w["sa_bias"][:], k.bank[3][:, P:2 * P], w["L2_vecs"][:, 0, :], ALU.add))
                order.settle()
                order.close()

            @block.tensor
            def _(pe):
                mm = nc.tensor.matmul
                pe.wait_ge(prepared, 2)
                mm(k.bank[0][:, 0:3], ones[:], rowsum[:], start=True, stop=True).then_inc(summed, 1)
                pe.wait_ge(loaded, n_small)
                wr, wi = w["L2_ffn_w_freq_real"], w["L2_ffn_w_freq_imag"]
                c, s, ns = w["fourier_cos"], w["fourier_sin"], w["fourier_nsin"]
                mm(k.bank[1][:, 0:P], wr[:], c[:], start=True, stop=False)
                mm(k.bank[1][:, 0:P], wi[:], s[:], start=False, stop=True)
                mm(k.bank[1][:, P:2 * P], wi[:], c[:], start=True, stop=False)
                mm(k.bank[1][:, P:2 * P], wr[:], ns[:], start=False, stop=True).then_inc(spectra, 1)
                mm(k.bank[3][:, 0:P], w["L2_sa_v"][:], w["L2_saT"][:], start=True, stop=True)
                mm(k.bank[3][:, P:2 * P], w["L2_sa_vb"][:], w["L2_saT"][:], start=True, stop=True)
                pe.wait_ge(prepared, 3)
                mm(k.bank[2][:, 0:P], spec[:, 0, :], c[:], start=True, stop=False)
                mm(k.bank[2][:, 0:P], spec[:, 1, :], ns[:], start=False, stop=True).then_inc(mixed, 1)


def load_later(k, sp):
    w = k.w
    sp.dma_start(w["mask_bytes"][:], k.d["mask_bytes"].partition_broadcast(P)).then_inc(k.later_loaded, 16)
    sp.dma_start(w["lens_int"][:], k.d["lens"].partition_broadcast(P)).then_inc(k.later_loaded, 16)
    for n in k.later:
        sp.dma_start(w[n][:], k.d[n]).then_inc(k.later_loaded, 16)
    for n in ("up_w", "down_w"):
        sp.dma_start(w[n][:], k.d["L1_" + n]).then_inc(k.big_loaded, 16)


def stage_later_is_here(k):
    count = 16 * (2 + len(k.later))
    with k.nc.Block() as block:
        @block.vector
        def _(v):
            v.wait_ge(k.later_loaded, count)
            order = Order(k, v, "dve")
            order.mark(k.nc.vector.tensor_copy(k.w["lens"][:], k.w["lens_int"][:]))
            order.settle()
            order.close()

        @block.scalar
        def _(act):
            act.wait_ge(k.later_loaded, count)

        @block.gpsimd
        def _(pool):
            pool.wait_ge(k.later_loaded, count)

        @block.tensor
        def _(pe):
            pe.wait_ge(k.later_loaded, count)

        @block.sync
        def _(sp):
            sp.wait_ge(k.later_loaded, count)


def ln_stats(k, order, src, six, two, last):
    nc, tiles = k.nc, src.shape[1]
    for t in range(tiles):
        ins = nc.vector.bn_stats(six[:, t, :], src[:, t, :])
    order.mark(ins)
    order.settle_apart()
    for t in range(tiles):
        ins = nc.vector.bn_aggr(two[:, t, :], six[:, t, :])
    return last(ins)


def rstd_on_pool(k, order, var, rstd, n, eps=EPS):
    nc = k.nc
    order.mark(nc.gpsimd.tensor_tensor(rstd, var, k.w["eps"][:, 0:n] if eps == EPS else k.w["eps_rms"][:, 0:n], ALU.add))
    order.settle()
    return nc.gpsimd.tensor_tensor(rstd, rstd, k.w["minus_half"][:, 0:n], ALU.pow)


def stage_autocorrelation(k):
    nc, w, S = k.nc, k.w, 4
    TURNS = B // S
    TOP = int(np.floor(np.log(L)))
    with ExitStack() as local:
        sb = lambda n, s, d=F32: [k.sb(f"ac_{n}{j}", s, d, local) for j in range(S)]
        ctx, ctxT = sb("ctx", [P, T2, P]), sb("ctxT", [P, L])
        six, two, rstd = sb("six", [P, T2, 6]), sb("two", [P, T2, 2]), sb("rstd", [P, T2])
        xn, xnT, qk = sb("xn", [P, T2, P]), sb("xnT", [P, L]), sb("qk", [P, T2, 2 * P])
        freq, prod, cross = sb("freq", [P, 2, 2 * P]), sb("prod", [P, 2, P]), sb("cross", [P, 2, P])
        spec = sb("spec", [P, 2, P])
        top, neg, at = sb("top", [P, 8]), sb("neg", [P, 1]), sb("at", [P, 8], U32)
        e5, den, shift, shift_i = sb("e5", [P, 8]), sb("den", [P, 1]), sb("shift", [P, 8]), sb("shift_i", [P, 8], I32)
        hit, roll, mix = sb("hit", [P, 8, TOP]), sb("roll", [P, 8]), sb("mix", [P, P])
        ctx_wo, val_wo, spread = sb("ctx_wo", [P, L]), sb("val_wo", [P, L]), sb("spread", [P, 4, P])
        sem = lambda n: k.sem("ac_" + n)
        ctx_in = [sem(f"ctx_in{j}") for j in range(S)]
        stats, rs, n0 = k.norms(B)
        xn_r, tr, evac = sem("xn"), sem("pe"), sem("evac")
        prod_r, spec_r, mix_r, done, topped, exped = sem("prod"), sem("spec"), sem("mix"), sem("done"), sem("topped"), sem("exped")
        PE, EV = 8, 6

        with nc.Block() as block:
            @block.sync
            def _(sp):
                with sp.Fori(0, TURNS) as i:
                    for s in range(S):
                        n = i * S + s
                        sp.wait_ge(done, n + 1)
                        sp.dma_start(ctx[s][:], k.d["ctx"][bass.ds(n, 1)].rearrange("b (t p) d -> p (b t) d", p=P)).then_inc(ctx_in[s], 16)
                        sp.dma_start(ctxT[s][:], k.d["ctxT"][bass.ds(n, 1)].rearrange("b d l -> (b d) l")).then_inc(ctx_in[s], 16)
                load_later(k, sp)

            @block.gpsimd
            def _(pool):
                with pool.Fori(0, TURNS) as i:
                    order = Order(k, pool, "pool", i, TURNS, S)
                    for s in range(S):
                        pool.wait_ge(stats, n0 + i * S + s + 1)
                        rstd_on_pool(k, order, two[s][:, :, 1], rstd[s][:], T2).then_inc(rs, 1)
                    for s in range(S):
                        pool.wait_ge(evac, i * S * EV + 2 * S + s + 1)
                        nc.gpsimd.tensor_tensor(cross[s][:, 0, :], freq[s][:, 0, 0:P], freq[s][:, 1, P:2 * P], ALU.mult)
                        nc.gpsimd.tensor_tensor(cross[s][:, 1, :], freq[s][:, 1, 0:P], freq[s][:, 0, P:2 * P], ALU.mult).then_inc(prod_r, 1)
                    order.close()

            @block.vector
            def _(v):
                v.sem_inc(done, S)
                with v.Fori(0, TURNS) as i:
                    order = Order(k, v, "dve", i, TURNS, 11 * S)
                    for s in range(S):
                        ln_stats(k, order, k.x[:, bass.ds((i * S + s) * T2, T2), :], six[s], two[s], lambda ins: ins.then_inc(stats, 1))
                    for s in range(S):
                        v.wait_ge(rs, n0 + i * S + s + 1)
                        for t in range(T2):
                            ins = nc.vector.tensor_scalar(xn[s][:, t, :], k.x[:, bass.ds((i * S + s) * T2 + t, 1), :].rearrange("p a b -> p (a b)"),
                                                          two[s][:, t, 0:1], rstd[s][:, t:t + 1], ALU.subtract, ALU.mult)
                        ins.then_inc(xn_r, 1)
                    for s in range(S):
                        v.wait_ge(evac, i * S * EV + 2 * S + s + 1)
                        order.mark(nc.vector.tensor_tensor(prod[s][:], freq[s][:, :, 0:P], freq[s][:, :, P:2 * P], ALU.mult))
                    for s in range(S):
                        order.settle()
                        nc.vector.scalar_tensor_tensor(spec[s][:, 0, :], prod[s][:, 1, :], w["not_first"][:, 0:1], prod[s][:, 0, :], ALU.mult, ALU.add)
                        v.wait_ge(prod_r, i * S + s + 1)
                        order.mark(nc.vector.tensor_tensor(spec[s][:, 1, :], cross[s][:, 0, :], cross[s][:, 1, :], ALU.subtract))
                    order.settle()
                    for s in range(S):
                        nc.vector.tensor_copy(spec[s][0:1, 1, :], prod[s][0:1, 1, :]).then_inc(spec_r, 1)
                    for s in range(S):
                        v.wait_ge(tr, i * S * PE + 5 * S + s + 1)
                        corr = k.bank[2 * s][:, 0:L]
                        k.carry(v)
                        order.mark(nc.vector.max(top[s][:], corr))
                        order.settle_apart()
                        order.mark(nc.vector.max_index(at[s][:], top[s][:], corr))
                        nc.vector.tensor_scalar(neg[s][:], top[s][:, 0:1], -1.0, None, ALU.mult).then_inc(topped, 1)
                    for s in range(S):
                        order.settle()
                        order.mark(nc.vector.tensor_scalar(shift_i[s][:], at[s][:], -1.0, w["rolled_base"][:, 0:1], ALU.mult, ALU.add))
                    order.settle()
                    for s in range(S):
                        order.mark(nc.vector.tensor_single_scalar(shift_i[s][:], shift_i[s][:], 7, ALU.bitwise_and))
                    order.settle()
                    for s in range(S):
                        order.mark(nc.vector.tensor_copy(shift[s][:], shift_i[s][:]))
                    order.settle()
                    for s in range(S):
                        order.mark(nc.vector.tensor_tensor(
                            hit[s][:], shift[s][:, 0:TOP].unsqueeze(1).to_broadcast([P, 8, TOP]),
                            w["iota8"][:].unsqueeze(2).to_broadcast([P, 8, TOP]), ALU.is_equal))
                    order.settle()
                    for s in range(S):
                        v.wait_ge(exped, i * S + s + 1)
                        nc.vector.reciprocal(den[s][:], den[s][:])
                        order.mark(nc.vector.tensor_tensor(hit[s][:], hit[s][:], e5[s][:, 0:TOP].unsqueeze(1).to_broadcast([P, 8, TOP]), ALU.mult))
                    order.settle()
                    for s in range(S):
                        order.mark(nc.vector.tensor_reduce(roll[s][:], hit[s][:], AX.X, ALU.add))
                    order.settle()
                    for s in range(S):
                        nc.vector.scalar_tensor_tensor(
                            mix[s][:].rearrange("p (g m) -> p g m", m=8), w["head_block"][:].rearrange("p (g m) -> p g m", m=8), den[s][:, 0:1],
                            roll[s][:].unsqueeze(1).to_broadcast([P, 16, 8]), ALU.mult, ALU.mult).then_inc(mix_r, 1)
                    for s in range(S):
                        v.wait_ge(tr, i * S * PE + 7 * S + s + 1)
                        xs = k.x[:, bass.ds((i * S + s) * T2, T2), :]
                        nc.vector.tensor_tensor(xs, xs, k.bank[2 * s][:, L:2 * L].rearrange("p (t d) -> p t d", t=T2), ALU.add).then_inc(done, 1)
                    order.close()

            @block.scalar
            def _(act):
                with act.Fori(0, TURNS) as i:
                    for step, (src, dst) in enumerate((
                            (lambda s: k.bank[2 * s][:, 0:L], lambda s: xnT[s][:]),
                            (lambda s: k.bank[2 * s + 1][:], lambda s: flat(qk[s][:])),
                            (lambda s: k.bank[2 * s][:], lambda s: flat(freq[s][:])),
                            (lambda s: k.bank[2 * s + 1][:, 0:L], lambda s: ctx_wo[s][:]),
                            (lambda s: k.bank[2 * s + 1][:, L:2 * L], lambda s: val_wo[s][:]))):
                        for s in range(S):
                            act.wait_ge(tr, i * S * PE + step * S + s + 1)
                            nc.scalar.copy(dst(s), src(s)).then_inc(evac, 1)
                    for s in range(S):
                        act.wait_ge(topped, i * S + s + 1)
                        nc.scalar.activation(e5[s][:, 0:TOP], top[s][:, 0:TOP], ACT.Exp, bias=neg[s][:, 0:1], accum_out=den[s][:, 0:1]).then_inc(exped, 1)
                    for s in range(S):
                        act.wait_ge(tr, i * S * PE + 6 * S + s + 1)
                        nc.scalar.copy(flat(spread[s][:]), k.bank[2 * s + 1][:]).then_inc(evac, 1)

            @block.tensor
            def _(pe):
                mm = nc.tensor.matmul
                with pe.Fori(0, TURNS) as i:
                    for s in range(S):
                        a = k.bank[2 * s]
                        pe.wait_ge(xn_r, i * S + s + 1)
                        for t in range(T2):
                            ins = nc.tensor.transpose(a[:, t * P:(t + 1) * P], xn[s][:, t, :], w["ident"][:])
                        ins.then_inc(tr, 1)
                    for s in range(S):
                        b = k.bank[2 * s + 1]
                        pe.wait_ge(evac, i * S * EV + s + 1)
                        pe.wait_ge(ctx_in[s], i * 32 + 32)
                        for t in range(T2):
                            mm(b[:, t * L:t * L + P], xnT[s][:, t * P:(t + 1) * P], w["q0_wq"][:], start=True, stop=True)
                            ins = mm(b[:, t * L + P:(t + 1) * L], ctxT[s][:, t * P:(t + 1) * P], w["q0_wk"][:], start=True, stop=True)
                        ins.then_inc(tr, 1)
                    for s in range(S):
                        a = k.bank[2 * s]
                        pe.wait_ge(evac, i * S * EV + S + s + 1)
                        for f in range(2):
                            for t in range(T2):
                                ins = mm(a[:, f * L:(f + 1) * L], w["dft"][:, t, f * P:(f + 1) * P], qk[s][:, t, :], start=(t == 0), stop=(t == T2 - 1))
                        ins.then_inc(tr, 1)
                    for s in range(S):
                        b = k.bank[2 * s + 1]
                        pe.wait_ge(evac, i * S * EV + S + s + 1)
                        for t in range(T2):
                            ins = mm(b[:, t * P:(t + 1) * P], ctx[s][:, t, :], w["q0_wo"][:], start=True, stop=True)
                        ins.then_inc(tr, 1)
                    for s in range(S):
                        pe.wait_ge(evac, i * S * EV + 3 * S + s + 1)
                        mm(k.bank[2 * s + 1][:, L:2 * L], w["q0_wv"][:], ctx_wo[s][:], start=True, stop=True).then_inc(tr, 1)
                    for s in range(S):
                        a = k.bank[2 * s]
                        pe.wait_ge(spec_r, i * S + s + 1)
                        mm(a[:, 0:L], spec[s][:, 0, :], w["idft"][:, 0, :], start=True, stop=False)
                        mm(a[:, 0:L], spec[s][:, 1, :], w["idft"][:, 1, :], start=False, stop=True).then_inc(tr, 1)
                    for s in range(S):
                        pe.wait_ge(mix_r, i * S + s + 1)
                        pe.wait_ge(evac, i * S * EV + 4 * S + s + 1)
                        mm(k.bank[2 * s + 1][:], mix[s][:], w["spread_rows"][:], start=True, stop=True).then_inc(tr, 1)
                    for s in range(S):
                        pe.wait_ge(evac, i * S * EV + 5 * S + s + 1)
                        for t in range(T2):
                            for half in range(2):
                                ins = mm(k.bank[2 * s][:, L + t * P:L + (t + 1) * P], spread[s][:, 2 * t + half, :], val_wo[s][:, half * P:(half + 1) * P],
                                         start=(half == 0), stop=(half == 1))
                        ins.then_inc(tr, 1)




def stage_ternary_ffn(k):
    nc, w, S = k.nc, k.w, 4
    TURNS, HID = NT // S, 512
    tt, ts = nc.vector.tensor_tensor, nc.vector.tensor_scalar
    with ExitStack() as local:
        one = lambda n, s, d=F32: k.sb(f"tf_{n}", s, d, local)
        sb = lambda n, s, d=F32: [k.sb(f"tf_{n}{j}", s, d, local) for j in range(S)]
        six, two, rstd, xn = one("six", [P, NT, 6]), one("two", [P, NT, 2]), one("rstd", [P, NT]), one("xn", [P, NT, P])
        step, inv, gate_scale, up_scale = (one(n, [P, NT]) for n in ("step", "inv", "gate_scale", "up_scale"))
        xq, xqT = one("xq", [P, NT, P], BF16), one("xqT", [P, S, P], BF16)
        h_max, h_step, h_inv, out_scale = (one(n, [P, S]) for n in ("h_max", "h_step", "h_inv", "out_scale"))
        g, h, hr = sb("g", [P, HID]), sb("h", [P, HID]), sb("hr", [P, HID])
        hq, hqT = sb("hq", [P, HID], BF16), sb("hqT", [P, 4, P], BF16)
        sem = lambda n: k.sem("tf_" + n)
        stats, rs, n0 = k.norms(2)
        halves = [slice(j * NT // 2, (j + 1) * NT // 2) for j in range(2)]
        xq_r, xT_ps, xT_r, up_ps, act_r, h_inv_r, hr_r, hq_r, hT_ps, hT_r, dn_ps, done = (sem(n) for n in (
            "xq", "xT_ps", "xT", "up_ps", "silu", "h_inv", "h_scaled", "hq", "hT_ps", "hT", "down_ps", "done"))
        with nc.Block() as block:
            @block.gpsimd
            def _(pool):
                order = Order(k, pool, "pool")
                for j, half in enumerate(halves):
                    pool.wait_ge(stats, n0 + j + 1)
                    rstd_on_pool(k, order, two[:, half, 1], rstd[:, half], NT // 2).then_inc(rs, 1)
                order.close()

            @block.vector
            def _(v):
                order = Order(k, v, "dve")
                for half in halves:
                    ln_stats(k, order, k.x[:, half, :], six[:, half, :], two[:, half, :], lambda ins: ins.then_inc(stats, 1))
                for t in range(NT):
                    if t % (NT // 2) == 0:
                        v.wait_ge(rs, n0 + t // (NT // 2) + 1)
                    ins = ts(xn[:, t, :], k.x[:, t, :], two[:, t, 0:1], rstd[:, t:t + 1], ALU.subtract, ALU.mult)
                order.mark(ins)
                order.settle()
                order.mark(nc.vector.tensor_reduce(step[:], xn[:], AX.X, ALU.max, apply_absolute_value=True))
                order.settle()
                order.mark(ts(step[:], step[:], EPS, 1.0 / 127, ALU.max, ALU.mult))
                order.settle()
                order.mark(nc.vector.reciprocal(inv[:], step[:]))
                order.settle()
                ts(gate_scale[:], step[:], w["scale_gate"][:, 0:1], None, ALU.mult)
                ts(up_scale[:], step[:], w["scale_up"][:, 0:1], None, ALU.mult)
                for t in range(NT):
                    ins = ts(xn[:, t, :], xn[:, t, :], inv[:, t:t + 1], ROUND, ALU.mult, ALU.add)
                order.mark(ins)
                order.settle()
                for j in range(TURNS):
                    ts(xq[:, j * S:(j + 1) * S, :], xn[:, j * S:(j + 1) * S, :], -ROUND, 127.0, ALU.add, ALU.min).then_inc(xq_r, 1)
                v.sem_inc(done, S)
                order.close()
                with v.Fori(0, TURNS) as i:
                    order = Order(k, v, "dve", i, TURNS, 4)
                    for s in range(S):
                        v.wait_ge(act_r, i * S + s + 1)
                        ins = nc.vector.scalar_tensor_tensor(h[s][:], k.bank[2 * s + 1][:], up_scale[:, bass.ds(i * S + s, 1)], g[s][:], ALU.mult, ALU.mult)
                    order.mark(ins)
                    order.settle()
                    for s in range(S):
                        ins = nc.vector.tensor_reduce(h_max[:, s:s + 1], h[s][:], AX.X, ALU.max, apply_absolute_value=True)
                    order.mark(ins)
                    order.settle()
                    order.mark(ts(h_step[:], h_max[:], EPS, 1.0 / 127, ALU.max, ALU.mult))
                    order.settle()
                    nc.vector.reciprocal(h_inv[:], h_step[:]).then_inc(h_inv_r, 1)
                    order.mark(ts(out_scale[:], h_step[:], w["scale_down"][:, 0:1], None, ALU.mult))
                    for s in range(S):
                        v.wait_ge(hr_r, i * S + s + 1)
                        ts(hq[s][:], hr[s][:], -ROUND, 127.0, ALU.add, ALU.min).then_inc(hq_r, 1)
                    order.settle()
                    for s in range(S):
                        v.wait_ge(dn_ps, i * S + s + 1)
                        xs = flat(k.x[:, bass.ds(i * S + s, 1), :])
                        nc.vector.scalar_tensor_tensor(xs, k.bank[2 * s + 1][:, 0:P], out_scale[:, s:s + 1], xs, ALU.mult, ALU.add).then_inc(done, 1)
                    order.close()

            @block.scalar
            def _(act):
                with act.Fori(0, TURNS) as i:
                    act.wait_ge(xT_ps, i + 1)
                    nc.scalar.copy(flat(xqT[:]), k.bank[0][:].bitcast(BF16)[:, 0:S * P]).then_inc(xT_r, 1)
                    for s in range(S):
                        act.wait_ge(up_ps, i * S + s + 1)
                        nc.scalar.activation(g[s][:], k.bank[2 * s][:], ACT.Silu, scale=gate_scale[:, bass.ds(i * S + s, 1)]).then_inc(act_r, 1)
                    act.wait_ge(h_inv_r, i + 1)
                    for s in range(S):
                        nc.scalar.activation(hr[s][:], h[s][:], ACT.Copy, scale=h_inv[:, s:s + 1], bias=ROUND).then_inc(hr_r, 1)
                    for s in range(S):
                        act.wait_ge(hT_ps, i * S + s + 1)
                        nc.scalar.copy(flat(hqT[s][:]), k.bank[2 * s][:].bitcast(BF16)[:, 0:HID]).then_inc(hT_r, 1)

            @block.tensor
            def _(pe):
                mm = nc.tensor.matmul
                with pe.Fori(0, TURNS) as i:
                    pe.wait_ge(xq_r, i + 1)
                    for s in range(S):
                        ins = nc.tensor.transpose(k.bank[0][:].bitcast(BF16)[:, s * P:(s + 1) * P], flat(xq[:, bass.ds(i * S + s, 1), :]), w["ident_bf"][:])
                    ins.then_inc(xT_ps, 1)
                    pe.wait_ge(xT_r, i + 1)
                    for s in range(S):
                        pe.wait_ge(done, i * S + s + 1)
                        mm(k.bank[2 * s][:], xqT[:, s, :], w["tern_gate"][:], start=True, stop=True)
                        mm(k.bank[2 * s + 1][:], xqT[:, s, :], w["tern_up"][:], start=True, stop=True).then_inc(up_ps, 1)
                    for s in range(S):
                        pe.wait_ge(hq_r, i * S + s + 1)
                        for c in range(4):
                            ins = nc.tensor.transpose(k.bank[2 * s][:].bitcast(BF16)[:, c * P:(c + 1) * P], hq[s][:, c * P:(c + 1) * P], w["ident_bf"][:])
                        ins.then_inc(hT_ps, 1)
                    for s in range(S):
                        pe.wait_ge(hT_r, i * S + s + 1)
                        for c in range(4):
                            ins = mm(k.bank[2 * s + 1][:, 0:P], hqT[s][:, c, :], w["tern_down"][:, c * P:(c + 1) * P], start=(c == 0), stop=(c == 3))
                        ins.then_inc(dn_ps, 1)


def stage_fourier(k):
    nc, w, S = k.nc, k.w, 4
    TURNS = B // S
    with ExitStack() as local:
        sb = lambda n, s, d=F32: [k.sb(f"fo_{n}{j}", s, d, local) for j in range(S)]
        six, two, rstd, xn, xnT = sb("six", [P, T2, 6]), sb("two", [P, T2, 2]), sb("rstd", [P, T2]), sb("xn", [P, T2, P]), sb("xnT", [P, L])
        sem = lambda n: k.sem("fo_" + n)
        stats, rs, n0 = k.norms(B)
        xn_r, pe_r, ev, done = (sem(n) for n in ("xn", "pe", "evac", "done"))
        with nc.Block() as block:
            @block.gpsimd
            def _(pool):
                with pool.Fori(0, TURNS) as i:
                    order = Order(k, pool, "pool", i, TURNS, S)
                    for s in range(S):
                        pool.wait_ge(stats, n0 + i * S + s + 1)
                        rstd_on_pool(k, order, two[s][:, :, 1], rstd[s][:], T2).then_inc(rs, 1)
                    order.close()

            @block.vector
            def _(v):
                with v.Fori(0, TURNS) as i:
                    order = Order(k, v, "dve", i, TURNS, 2 * S)
                    for s in range(S):
                        ln_stats(k, order, k.x[:, bass.ds((i * S + s) * T2, T2), :], six[s], two[s], lambda ins: ins.then_inc(stats, 1))
                    for s in range(S):
                        v.wait_ge(rs, n0 + i * S + s + 1)
                        for t in range(T2):
                            ins = nc.vector.tensor_scalar(xn[s][:, t, :], flat(k.x[:, bass.ds((i * S + s) * T2 + t, 1), :]),
                                                          two[s][:, t, 0:1], rstd[s][:, t:t + 1], ALU.subtract, ALU.mult)
                        ins.then_inc(xn_r, 1)
                    for s in range(S):
                        xs = k.x[:, bass.ds((i * S + s) * T2, T2), :]
                        v.wait_ge(xn_r, i * S + s + 1)
                        order.mark(nc.vector.tensor_tensor(xs, xs, w["L2_bias"][:].unsqueeze(1).to_broadcast([P, T2, P]), ALU.add))
                        order.settle()
                        v.wait_ge(pe_r, i * S * 2 + S + s + 1)
                        nc.vector.tensor_tensor(xs, xs, k.bank[2 * s + 1][:, 0:L].rearrange("p (t d) -> p t d", t=T2), ALU.add).then_inc(done, 1)
                    order.close()

            @block.scalar
            def _(act):
                with act.Fori(0, TURNS) as i:
                    for s in range(S):
                        act.wait_ge(pe_r, i * S * 2 + s + 1)
                        nc.scalar.copy(xnT[s][:], k.bank[2 * s][:, 0:L]).then_inc(ev, 1)

            @block.tensor
            def _(pe):
                with pe.Fori(0, TURNS) as i:
                    for s in range(S):
                        pe.wait_ge(xn_r, i * S + s + 1)
                        for t in range(T2):
                            ins = nc.tensor.transpose(k.bank[2 * s][:, t * P:(t + 1) * P], xn[s][:, t, :], w["ident"][:])
                        ins.then_inc(pe_r, 1)
                    for s in range(S):
                        pe.wait_ge(ev, i * S + s + 1)
                        for t in range(T2):
                            ins = nc.tensor.matmul(k.bank[2 * s + 1][:, t * P:(t + 1) * P], xnT[s][:, t * P:(t + 1) * P], w["fourier"][:], start=True, stop=True)
                        ins.then_inc(pe_r, 1)


def norm_and_transpose(k, xnT, src, norm=True, context=None):
    nc, w, T = k.nc, k.w, 4
    with ExitStack() as local:
        if norm:
            six, two, rstd = (k.sb(f"nt{k.normed}_{n}", s, F32, local) for n, s in (("six", [P, NT, 6]), ("two", [P, NT, 2]), ("rstd", [P, NT])))
            xn = k.sb(f"nt{k.normed}_xn", [P, NT, P], F32, local)
            stats, rs, n0 = k.norms(2)
            halves = [slice(j * NT // 2, (j + 1) * NT // 2) for j in range(2)]
        else:
            xn = src
        with nc.Block() as block:
            @block.sync
            def _(sp):
                if context is not None:
                    ctxT, ctx_in = context
                    sp.dma_start(ctxT[:], k.d["ctxT"].rearrange("b d l -> d b l")).then_inc(ctx_in, 16)

            @block.gpsimd
            def _(pool):
                if norm:
                    order = Order(k, pool, "pool")
                    for j, half in enumerate(halves):
                        pool.wait_ge(stats, n0 + j + 1)
                        rstd_on_pool(k, order, two[:, half, 1], rstd[:, half], NT // 2).then_inc(rs, 1)
                    order.close()

            @block.vector
            def _(v):
                if norm:
                    order = Order(k, v, "dve")
                    for half in halves:
                        ln_stats(k, order, src[:, half, :], six[:, half, :], two[:, half, :], lambda ins: ins.then_inc(stats, 1))
                    order.close()
                    for t in range(NT):
                        if t % (NT // 2) == 0:
                            v.wait_ge(rs, n0 + t // (NT // 2) + 1)
                        ins = nc.vector.tensor_scalar(xn[:, t, :], src[:, t, :], two[:, t, 0:1], rstd[:, t:t + 1], ALU.subtract, ALU.mult)
                        if t % T == T - 1:
                            ins.then_inc(k.all_xn, 1)

            @block.scalar
            def _(act):
                for j in range(NT // T):
                    act.wait_ge(k.all_ps, k.alls + j + 1)
                    nc.scalar.copy(flat(xnT[:, j * T:(j + 1) * T, :]), k.bank[j][:]).then_inc(k.all_ev, 1)

            @block.tensor
            def _(pe):
                for j in range(NT // T):
                    if norm:
                        pe.wait_ge(k.all_xn, k.norms_split + j + 1)
                    for t in range(T):
                        ins = nc.tensor.transpose(k.bank[j][:, t * P:(t + 1) * P], xn[:, j * T + t, :], w["ident"][:])
                    ins.then_inc(k.all_ps, 1)
        k.alls += NT // T
        k.norms_split += NT // T if norm else 0


def stage_causal_attention(k):
    nc, w, S = k.nc, k.w, 2
    TURNS, H, D = B // S, 16, 64
    PAIRS, SCALE = H // 2, 64 ** -0.5
    NS, NR, NB, NP = 3, 5, 2, 3
    TSK, OSK = 3, 5
    with ExitStack() as local:
        sb = lambda n, s, d=F32, c=S: [k.sb(f"ca_{n}{j}", s, d, local) for j in range(c)]
        xnT = k.sb("ca_xnT", [P, NT, P], ctx=local)
        norm_and_transpose(k, xnT, k.x)
        ctxT = sb("ctxT", [P, L])
        q, kk, val, heads = sb("q", [P, H, L]), sb("k", [P, PAIRS, L]), sb("v", [P, T2, H * D]), sb("heads", [P, PAIRS, L])
        bar, ln1, z, zc = sb("bar", [P, 3 * P]), sb("len", [P, 1]), sb("z", [P, 1]), sb("zc", [P, 1])
        nz = sb("nz", [P, 1])
        sm, mx, nmx, den = sb("sm", [P, 3 * P], c=NR), sb("mx", [P, 2], c=NR), sb("nmx", [P, 2], c=NR), sb("den", [P, 2], c=NR)
        rden, prob = sb("rden", [P, 2], c=NR), sb("prob", [P, 3 * P], c=NR)
        pT = sb("pT", [P, 4 * P], c=NP * S)
        sem = lambda n: k.sem("ca_" + n)
        ctx_in = [sem(f"ctx_in{j}") for j in range(S)]
        ctx_used, proj, pev, vev = (sem(n) for n in ("ctx_used", "proj", "qk", "v"))
        bar_r, s_ps, s_sm, ex, rd, nrm, t_ps, t_ev, o_ps, o_ev, y_ps, done = (
            sem(n) for n in ("bar", "scores", "masked", "exp", "rden", "norm", "pT_ps", "pT", "o_ps", "heads", "y_ps", "done"))
        v_ps, kev = sem("v_ps"), sem("kev")
        HS = S * H
        NPROJ = 2 * PAIRS

        with nc.Block() as block:
            @block.sync
            def _(sp):
                with sp.Fori(0, TURNS) as i:
                    for s in range(S):
                        n = i * S + s
                        sp.wait_ge(ctx_used, n + 1)
                        sp.dma_start(ctxT[s][:], k.d["ctxT"][bass.ds(n, 1)].rearrange("b d l -> (b d) l")).then_inc(ctx_in[s], 16)

            @block.gpsimd
            def _(pool):
                with pool.Fori(0, TURNS) as i:
                    for g in range(HS):
                        s, m = g // H, g % NR
                        pool.wait_ge(rd, i * HS + g + 1)
                        k.carry(pool)
                        nc.gpsimd.tensor_scalar(prob[m][:, 0:P], prob[m][:, 0:P], rden[m][:, 0:1], zc[s][:, 0:1], ALU.mult, ALU.add)
                        nc.gpsimd.tensor_scalar(prob[m][:, P:3 * P], prob[m][:, P:3 * P], rden[m][:, 1:2], zc[s][:, 0:1], ALU.mult, ALU.add).then_inc(nrm, 1)

            def head_sum(v, order, i, g):
                s, m = g // H, g % NR
                v.wait_ge(ex, i * HS + g + 1)
                order.mark(nc.vector.reciprocal(rden[m][:], den[m][:]))
                order.settle()
                nc.vector.tensor_scalar(rden[m][:], rden[m][:], nz[s][:, 0:1], None, ALU.mult).then_inc(rd, 1)

            @block.vector
            def _(v):
                v.sem_inc(ctx_used, S)
                v.sem_inc(done, S)
                with v.Fori(0, TURNS) as i:
                    order = Order(k, v, "dve", i, TURNS, 4 * S + 2 * HS)
                    for s in range(S):
                        order.mark(nc.vector.tensor_copy(ln1[s][:], w["lens"][:, bass.ds(i * S + s, 1)]))
                    order.settle()
                    for s in range(S):
                        nc.vector.tensor_scalar(z[s][:], ln1[s][:], 0.0, None, ALU.is_le)
                        order.mark(nc.vector.tensor_scalar(bar[s][:], w["iota_k"][:], ln1[s][:, 0:1], NEG, ALU.is_ge, ALU.mult))
                    order.settle()
                    for s in range(S):
                        nc.vector.tensor_scalar(nz[s][:], z[s][:], -1.0, 1.0, ALU.mult, ALU.add)
                        nc.vector.tensor_scalar(zc[s][:], z[s][:], 1.0 / L, None, ALU.mult)
                        order.mark(nc.vector.tensor_tensor(bar[s][:], bar[s][:], w["causal"][:], ALU.add))
                    order.settle()
                    for s in range(S):
                        for r in range(NP):
                            ins = nc.vector.tensor_scalar(pT[s * NP + r][:, 0:P], w["ident"][:], 0.0, zc[s][:, 0:1], ALU.mult, ALU.add)
                        ins.then_inc(bar_r, 1)
                    for s in range(S):
                        for p in range(PAIRS):
                            v.wait_ge(proj, i * S * NPROJ + s * NPROJ + 2 * p + 1)
                            for o in range(2):
                                ins = nc.vector.tensor_scalar(q[s][:, 2 * p + o, :], k.bank[2 * (p % 2)][:, 0:L], w["L1_bQ"][:, p:p + 1], w["head_pick"][:, o:o + 1], ALU.add, ALU.mult)
                            ins.then_inc(pev, 1)
                    for g in range(HS):
                        s, m = g // H, g % NR
                        v.wait_ge(s_ps, i * HS + g + 1)
                        if g >= NR:
                            v.wait_ge(ex, i * HS + g - NR + 1)
                        k.carry(v)
                        for a, b, j in ((0, P, 0), (P, 3 * P, 1)):
                            ins = nc.vector.tensor_tensor_reduce(out=sm[m][:, a:b], in0=k.bank[2 + g % NS][:, a:b], in1=bar[s][:, a:b], scale=1.0, scalar=2 * NEG,
                                                                 op0=ALU.add, op1=ALU.max, accum_out=mx[m][:, j:j + 1])
                        order.mark(ins)
                        order.settle()
                        nc.vector.tensor_scalar(nmx[m][:], mx[m][:], -SCALE, None, ALU.mult).then_inc(s_sm, 1)
                        if g >= 1:
                            head_sum(v, order, i, g - 1)
                    head_sum(v, order, i, HS - 1)
                    for s in range(S):
                        xs = k.x[:, bass.ds((i * S + s) * T2, T2), :]
                        order.mark(nc.vector.tensor_tensor(xs, xs, w["L1_bO"][:].unsqueeze(1).to_broadcast([P, T2, P]), ALU.add))
                        order.settle()
                        v.wait_ge(y_ps, i * S + s + 1)
                        nc.vector.tensor_tensor(xs, xs, k.bank[s][:, 0:L].rearrange("p (t d) -> p t d", t=T2), ALU.add).then_inc(done, 1)
                    order.close()

            def head_out(act, i, pr):
                act.wait_ge(o_ps, i * HS + 2 * pr + 2)
                nc.scalar.activation(heads[pr // PAIRS][:, pr % PAIRS, :], k.bank[(7, 1)[pr % 2]][:, 0:L], ACT.Identity,
                                     bias=w["L1_bV"][:, pr % PAIRS:pr % PAIRS + 1]).then_inc(o_ev, 1)

            @block.scalar
            def _(act):
                with act.Fori(0, TURNS) as i:
                    for s in range(S):
                        for t in range(T2):
                            for c in range(2):
                                j = (s * T2 + t) * 2 + c
                                act.wait_ge(v_ps, i * S * 4 + j + 1)
                                nc.scalar.copy(val[s][:, t, c * 512:(c + 1) * 512], k.bank[5 + j % 2][:]).then_inc(vev, 1)
                    for s in range(S):
                        for p in range(PAIRS):
                            act.wait_ge(proj, i * S * NPROJ + s * NPROJ + 2 * p + 2)
                            nc.scalar.activation(kk[s][:, p, :], k.bank[2 * (p % 2) + 1][:, 0:L], ACT.Identity, bias=w["L1_bK"][:, p:p + 1]).then_inc(kev, 1)
                        act.sem_inc(ctx_used, 1)
                    for g in range(HS + TSK - 1):
                        if g < HS:
                            m = g % NR
                            act.wait_ge(s_sm, i * HS + g + 1)
                            if g >= NR:
                                act.wait_ge(t_ps, i * HS + g - NR + 1)
                            nc.scalar.activation(prob[m][:, 0:P], sm[m][:, 0:P], ACT.Exp, bias=nmx[m][:, 0:1], scale=SCALE, accum_out=den[m][:, 0:1])
                            nc.scalar.activation(prob[m][:, P:3 * P], sm[m][:, P:3 * P], ACT.Exp, bias=nmx[m][:, 1:2], scale=SCALE, accum_out=den[m][:, 1:2]).then_inc(ex, 1)
                        h = g - TSK + 1
                        if h >= 0:
                            r = h // H * NP + h % NP
                            act.wait_ge(t_ps, i * HS + h + 1)
                            if h >= NP:
                                act.wait_ge(o_ps, i * HS + h - NP + 1)
                            nc.scalar.copy(pT[r][:, P:4 * P], k.bank[5 + h % NB][:, 0:3 * P]).then_inc(t_ev, 1)
                            if h >= 4 and h % 2 == 0:
                                head_out(act, i, (h - 4) // 2)
                    head_out(act, i, HS // 2 - 2)
                    head_out(act, i, HS // 2 - 1)

            @block.tensor
            def _(pe):
                mm = nc.tensor.matmul
                with pe.Fori(0, TURNS) as i:
                    for s in range(S):
                        pe.wait_ge(ctx_in[s], i * 16 + 16)
                        for t in range(T2):
                            for c in range(2):
                                j = (s * T2 + t) * 2 + c
                                if j >= 2:
                                    pe.wait_ge(vev, i * S * 4 + j - 1)
                                mm(k.bank[5 + j % 2][:], ctxT[s][:, t * P:(t + 1) * P], w["L1_WV"][:, c * 512:(c + 1) * 512], start=True, stop=True).then_inc(v_ps, 1)
                    for s in range(S):
                        for p in range(PAIRS):
                            a, done_q = s * PAIRS + p, i * S * PAIRS + s * PAIRS + p
                            if a == 0:
                                pe.wait_ge(done, (i + 1) * S)
                            if a >= 2:
                                pe.wait_ge(pev, done_q - 1)
                                pe.wait_ge(kev, done_q - 1)
                            mm(k.bank[2 * (p % 2)][:, 0:L], w["L1_WQ"][:, p * P:(p + 1) * P], flat(xnT[:, bass.ds((i * S + s) * T2, T2), :]), start=True, stop=True).then_inc(proj, 1)
                            mm(k.bank[2 * (p % 2) + 1][:, 0:L], w["L1_WK"][:, p * P:(p + 1) * P], ctxT[s][:], start=True, stop=True).then_inc(proj, 1)
                    pe.wait_ge(vev, (i + 1) * S * 4)
                    pe.wait_ge(pev, (i + 1) * S * PAIRS)
                    pe.wait_ge(kev, (i + 1) * S * PAIRS)
                    for g in range(HS + OSK):
                        if g < HS:
                            s, h, bank = g // H, g % H, k.bank[2 + g % NS]
                            if g >= NS:
                                pe.wait_ge(s_sm, i * HS + g - NS + 1)
                            mm(bank[:, 0:P], q[s][:, h, 0:P], kk[s][:, h // 2, 0:P], start=True, stop=True)
                            mm(bank[:, P:3 * P], q[s][:, h, P:2 * P], kk[s][:, h // 2, :], start=True, stop=True).then_inc(s_ps, 1)
                        if TSK <= g < HS + TSK:
                            u = g - TSK
                            pe.wait_ge(nrm, i * HS + u + 1)
                            if u >= NB:
                                pe.wait_ge(t_ev, i * HS + u - NB + 1)
                            for c in range(3):
                                ins = nc.tensor.transpose(k.bank[5 + u % NB][:, c * P:(c + 1) * P], prob[u % NR][:, c * P:(c + 1) * P], w["ident"][:])
                            ins.then_inc(t_ps, 1)
                        if g >= OSK:
                            u = g - OSK
                            s, h, pr = u // H, u % H, u // 2
                            pe.wait_ge(t_ev, i * HS + u + 1)
                            if h == 0:
                                pe.wait_ge(bar_r, i * S + s + 1)
                            if h % 2 == 0 and pr >= 2:
                                pe.wait_ge(o_ev, i * PAIRS * S + pr - 1)
                            o = k.bank[(7, 1)[pr % 2]][(h % 2) * D:(h % 2 + 1) * D, 0:L]
                            r = pT[s * NP + u % NP]
                            mm(o, val[s][:, 0, h * D:(h + 1) * D], r[:, P:3 * P], start=True, stop=False)
                            mm(o.rearrange("p (a b) -> p a b", a=2), val[s][:, 1, h * D:(h + 1) * D], r[:].rearrange("p (a b) -> p a b", b=P)[:, 0:4:3, :],
                               start=False, stop=True).then_inc(o_ps, 1)
                    for s in range(S):
                        pe.wait_ge(o_ev, i * PAIRS * S + (s + 1) * PAIRS)
                        for t in range(T2):
                            for p in range(PAIRS):
                                ins = mm(k.bank[s][:, t * P:(t + 1) * P], heads[s][:, p, t * P:(t + 1) * P], w["L1_WO"][:, p, :], start=(p == 0), stop=(p == PAIRS - 1))
                        ins.then_inc(y_ps, 1)


def stage_experts(k, tag, loaded, first, second, act_fn, shared, top, bias):
    nc, w, T = k.nc, k.w, 4
    TURNS, N, RE = NT // T, T * P, 8
    E = RE + shared
    UPS, DOWNS, XTS = (2, 3, 6), (4, 5), (0, 7)
    NU, ND = len(UPS), len(DOWNS)
    KINDS = 2 if bias else 1
    with ExitStack() as local:
        sb = lambda n, s, d=F32, c=None: (k.sb(f"{tag}_{n}", s, d, local) if c is None else [k.sb(f"{tag}_{n}{j}", s, d, local) for j in range(c)])
        six, two, rstd, sq, r2 = sb("six", [P, NT, 6]), sb("two", [P, NT, 2]), sb("rstd", [P, NT]), sb("sq", [P, NT]), sb("r2", [P, NT])
        back, both, xn, xT = sb("back", [P, NT]), sb("both", [P, NT]), sb("xn", [P, NT, P]), sb("xT", [P, TURNS, N])
        x_in = sb("x_in", [P, N], c=2) if bias else None
        x_high, x_low = sb("x_high", [P, TURNS, N], F32R, c=KINDS), sb("x_low", [P, TURNS, N], F32R, c=KINDS)
        first_high, first_low = sb("first_high", [P, E, 512], F32R), sb("first_low", [P, E, 512], F32R)
        h = sb("h", [P, 4, N], c=2)
        logit, mx, val = sb("logit", [P, NT, RE]), sb("mx", [P, NT]), sb("val", [P, NT, RE])
        above, tie, rank = sb("above", [P, NT, RE * RE]), sb("tie", [P, NT, RE * RE]), sb("rank", [P, NT, RE])
        den, gate, gateT = sb("den", [P, NT]), sb("gate", [P, NT, E]), sb("gateT", [E, N])
        gate_now = sb("gate_now", [P, T, E])
        sem = lambda n: k.sem(f"{tag}_" + n)
        stats, rs, n0 = k.norms(2)
        halves_of = [slice(j * NT // 2, (j + 1) * NT // 2) for j in range(2)]
        xn_r, xT_ps, xT_r, halves, w_high, w_low = (sem(n) for n in ("xn", "xT_ps", "xT", "x_halves", "w_high", "w_low"))
        logit_ps, soft, gate_r, now_r, gT_ps, gT_r = (sem(n) for n in ("logit_ps", "soft", "gate", "gate_now", "gateT_ps", "gateT"))
        up_ps, act_r, dn_ps, done = sem("up_ps"), sem("hidden"), sem("down_ps"), sem("done")
        as_f32 = lambda ap: ap.bitcast(F32)
        with nc.Block() as block:
            @block.gpsimd
            def _(pool):
                order = Order(k, pool, "pool")
                for j, t in enumerate(halves_of):
                    pool.wait_ge(stats, n0 + j + 1)
                    ins = rstd_on_pool(k, order, two[:, t, 1], rstd[:, t], NT // 2)
                    if bias:
                        for factor in (two[:, t, 1], sq[:, t]):
                            order.mark(ins)
                            order.settle()
                            ins = nc.gpsimd.tensor_tensor(sq[:, t], factor, rstd[:, t], ALU.mult)
                        order.mark(ins)
                        order.settle()
                        order.mark(rstd_on_pool(k, order, sq[:, t], r2[:, t], NT // 2, EPS_RMS))
                        order.settle()
                        ins = nc.gpsimd.tensor_tensor(both[:, t], rstd[:, t], r2[:, t], ALU.mult)
                    ins.then_inc(rs, 1)
                order.close()
                with pool.Fori(0, E) as e:
                    pool.wait_ge(w_high, e + 1)
                    of = lambda x: flat(x[:, bass.ds(e, 1), :])
                    nc.gpsimd.tensor_tensor(of(first_low), of(first), as_f32(of(first_high)), ALU.subtract).then_inc(w_low, 1)

            def gates(v, order):
                tt, ts = nc.vector.tensor_tensor, nc.vector.tensor_scalar
                v.wait_ge(logit_ps, TURNS)
                if bias:
                    v.wait_ge(soft, 1)
                    order.mark(ts(val[:], val[:], 1.0, None, ALU.add))
                    order.settle()
                    order.mark(nc.vector.reciprocal(val[:], val[:]))
                    order.settle()
                else:
                    lg = k.bank[1][:, 0:NT * RE].rearrange("p (t e) -> p t e", t=NT)
                    order.mark(nc.vector.tensor_reduce(mx[:], lg, AX.X, ALU.max))
                    order.settle()
                    tt(logit[:], lg, mx[:].unsqueeze(2).to_broadcast([P, NT, RE]), ALU.subtract).then_inc(gate_r, 1)
                    v.wait_ge(soft, 1)
                mine = val[:].unsqueeze(3).to_broadcast([P, NT, RE, RE])
                other = val[:].unsqueeze(2).to_broadcast([P, NT, RE, RE])
                grid = lambda x: x[:].rearrange("p t (e j) -> p t e j", e=RE)
                tt(grid(above), other, mine, ALU.is_gt)
                order.mark(tt(grid(tie), other, mine, ALU.is_equal))
                order.settle()
                order.mark(tt(tie[:], tie[:], w["prefix"][:].rearrange("p a b -> p (a b)").unsqueeze(1).to_broadcast([P, NT, RE * RE]), ALU.mult))
                order.settle()
                order.mark(tt(above[:], above[:], tie[:], ALU.add))
                order.settle()
                order.mark(nc.vector.tensor_reduce(rank[:], grid(above), AX.X, ALU.add))
                order.settle()
                order.mark(ts(rank[:], rank[:], float(top), None, ALU.is_lt))
                order.settle()
                order.mark(tt(rank[:], rank[:], val[:], ALU.mult))
                order.settle()
                order.mark(nc.vector.tensor_reduce(den[:], val[:] if bias else rank[:], AX.X, ALU.add))
                order.settle()
                order.mark(nc.vector.reciprocal(den[:], den[:]))
                order.settle()
                tt(gate[:, :, 0:RE], rank[:], den[:].unsqueeze(2).to_broadcast([P, NT, RE]), ALU.mult).then_inc(gate_r, 1)
                v.wait_ge(gate_r, 2)

            @block.vector
            def _(v):
                tt, ts = nc.vector.tensor_tensor, nc.vector.tensor_scalar
                first_order = Order(k, v, "dve")
                for half in halves_of:
                    ln_stats(k, first_order, k.x[:, half, :], six[:, half, :], two[:, half, :], lambda ins: ins.then_inc(stats, 1))
                if bias:
                    nc.vector.memset(gate[:], 1.0)
                for t in range(NT):
                    if t % (NT // 2) == 0:
                        v.wait_ge(rs, n0 + t // (NT // 2) + 1)
                    ins = ts(xn[:, t, :], k.x[:, t, :], two[:, t, 0:1], (both if bias else rstd)[:, t:t + 1], ALU.subtract, ALU.mult)
                    if t % T == T - 1:
                        ins.then_inc(xn_r, 1)
                if bias:
                    first_order.mark(nc.vector.reciprocal(back[:], r2[:]))
                    first_order.settle()
                    ts(back[:], back[:], -1.0, None, ALU.mult).then_inc(gate_r, 1)
                first_order.close()
                order = Order(k, v, "dve")
                for j in range(TURNS):
                    v.wait_ge(xT_r, j + 1)
                    if bias:
                        for kind in range(KINDS):
                            ins = ts(x_in[kind][:], xT[:, j, :], w["L3_g"][:, kind:kind + 1], None, ALU.mult)
                        order.mark(ins)
                        order.settle()
                    src = [x[:] for x in x_in] if bias else [xT[:, j, :]]
                    for kind in range(KINDS):
                        ins = nc.vector.tensor_copy(x_high[kind][:, j, :], src[kind])
                    order.mark(ins)
                    order.settle()
                    for kind in range(KINDS):
                        ins = order.mark(tt(x_low[kind][:, j, :], src[kind], as_f32(x_high[kind][:, j, :]), ALU.subtract))
                    order.settle()
                    v.sem_inc(halves, 1)
                order.close()
                v.sem_inc(done, ND)
                v.sem_inc(gT_r, 1)
                last_order = Order(k, v, "dve")
                if bias:
                    for t in range(NT):
                        ins = ts(xn[:, t, :], k.x[:, t, :], two[:, t, 0:1], rstd[:, t:t + 1], ALU.subtract, ALU.mult)
                    last_order.mark(ins)
                    last_order.settle()
                    last_order.mark(tt(k.x[:], k.x[:], xn[:], ALU.add))
                gates(v, last_order)
                last_order.close()
                with v.Fori(0, TURNS) as i:
                    nc.vector.tensor_copy(gate_now[:], gate[:, bass.ds(i * T, T), :]).then_inc(now_r, 1)
                    v.wait_ge(now_r, i + 1)
                    for e in range(E):
                        if bias and e == E - 2:
                            v.wait_ge(gT_ps, i + 1)
                            nc.vector.tensor_copy(gateT[:], k.bank[1][0:E, 0:N]).then_inc(gT_r, 1)
                        v.wait_ge(dn_ps, i * E + e + 1)
                        for t in range(T):
                            xt = flat(k.x[:, bass.ds(i * T + t, 1), :])
                            ins = nc.vector.scalar_tensor_tensor(xt, k.bank[DOWNS[e % ND]][:, t * P:(t + 1) * P], gate_now[:, t, e:e + 1], xt, ALU.mult, ALU.add)
                        ins.then_inc(done, 1)
                        v.wait_ge(done, i * E + e + 1 + ND)

            @block.scalar
            def _(act):
                act.wait_ge(loaded, 32)
                with act.Fori(0, E) as e:
                    nc.scalar.copy(flat(first_high[:, bass.ds(e, 1), :]), flat(first[:, bass.ds(e, 1), :])).then_inc(w_high, 1)
                for j in range(TURNS):
                    act.wait_ge(xT_ps, j + 1)
                    nc.scalar.copy(xT[:, j, :], k.bank[XTS[j % 2]][:]).then_inc(xT_r, 1)
                if bias:
                    act.wait_ge(gate_r, 1)
                    act.wait_ge(logit_ps, TURNS)
                    for t in range(NT):
                        ins = nc.scalar.activation(val[:, t, :], k.bank[1][:, t * RE:(t + 1) * RE], ACT.Exp, scale=back[:, t:t + 1])
                    ins.then_inc(soft, 1)
                else:
                    act.wait_ge(gate_r, 1)
                    nc.scalar.activation(val[:], logit[:], ACT.Exp).then_inc(soft, 1)
                with act.Fori(0, TURNS) as i:
                    for e in range(E):
                        for c in range(4):
                            u = e * 4 + c
                            act.wait_ge(up_ps, i * E * 4 + u + 1)
                            if c == 0 and e >= 2:
                                act.wait_ge(dn_ps, i * E + e - 1)
                            nc.scalar.activation(h[e % 2][:, c, :], k.bank[UPS[u % NU]][:], act_fn, bias=w["L3_b1"][:, u:u + 1] if bias else 0.0).then_inc(act_r, 1)

            def logits(pe, j):
                pe.wait_ge(xT_r, j + 1)
                for t in range(T):
                    at = (j * T + t) * RE
                    ins = nc.tensor.matmul(k.bank[1][:, at:at + RE], xT[:, j, t * P:(t + 1) * P], w["L3_centroids" if bias else "L1_router"][:], start=True, stop=True)
                ins.then_inc(logit_ps, 1)

            def down(pe, i, e):
                pe.wait_ge(done, i * E + e + 1)
                pe.wait_ge(act_r, i * E * 4 + e * 4 + 4)
                gated = bias and e == E - 1
                if gated:
                    pe.wait_ge(gT_r, i + 2)
                for t in range(T):
                    o = k.bank[DOWNS[e % ND]][:, t * P:(t + 1) * P]
                    for c in range(4):
                        ins = nc.tensor.matmul(o, h[e % 2][:, c, t * P:(t + 1) * P], second[:, e, c * P:(c + 1) * P], start=(c == 0), stop=(c == 3 and not gated))
                    if gated:
                        ins = nc.tensor.matmul(o, gateT[:, t * P:(t + 1) * P], w["L3_b2"][:], start=False, stop=True)
                ins.then_inc(dn_ps, 1)

            @block.tensor
            def _(pe):
                for j in range(TURNS):
                    pe.wait_ge(xn_r, j + 1)
                    if j >= 2:
                        pe.wait_ge(xT_r, j - 1)
                    for t in range(T):
                        ins = nc.tensor.transpose(k.bank[XTS[j % 2]][:, t * P:(t + 1) * P], xn[:, j * T + t, :], w["ident"][:])
                    ins.then_inc(xT_ps, 1)
                    if j >= 1:
                        logits(pe, j - 1)
                logits(pe, TURNS - 1)
                pe.wait_ge(loaded, 32)
                with pe.Fori(0, TURNS) as i:
                    pe.wait_ge(halves, i + 1)
                    for e in range(E):
                        pe.wait_ge(w_low, e + 1)
                        kind = 0 if e >= RE else KINDS - 1
                        turn = lambda x: flat(x[kind][:, bass.ds(i, 1), :])
                        for c in range(4):
                            u = e * 4 + c
                            if u >= NU:
                                pe.wait_ge(act_r, i * E * 4 + u - NU + 1)
                            hidden = k.bank[UPS[u % NU]][:]
                            high, low = (x[:, e, c * P:(c + 1) * P] for x in (first_high, first_low))
                            nc.tensor.matmul(hidden, high, turn(x_high), start=True, stop=False)
                            nc.tensor.matmul(hidden, high, turn(x_low), start=False, stop=False)
                            nc.tensor.matmul(hidden, low, turn(x_high), start=False, stop=True).then_inc(up_ps, 1)
                        if bias and e == E - 2:
                            pe.wait_ge(now_r, i + 1)
                            pe.wait_ge(gT_r, i + 1)
                            for t in range(T):
                                ins = nc.tensor.transpose(k.bank[1][0:E, t * P:(t + 1) * P], gate_now[:, t, :], w["ident"][:])
                            ins.then_inc(gT_ps, 1)
                        if e >= 1:
                            down(pe, i, e - 1)
                    down(pe, i, E - 1)


def stage_load_last(k):
    k.layer1.close()
    for n in ("L3_W1", "L3_W2"):
        k.w[n] = k.sb("w_" + n, [P, 10, 512])
    k.last_loaded = k.sem("last_loaded")
    with k.nc.Block() as block:
        @block.sync
        def _(sp):
            sp.wait_ge(k.big_loaded, 32)
            for n in ("L3_W1", "L3_W2"):
                sp.dma_start(k.w[n][:], k.d[n]).then_inc(k.last_loaded, 16)


def stage_experts_gelu(k):
    stage_experts(k, "e1", k.big_loaded, k.w["up_w"], k.w["down_w"], ACT.Gelu_apprx_tanh, 0, 4, False)


def stage_experts_shared(k):
    stage_experts(k, "e3", k.last_loaded, k.w["L3_W1"], k.w["L3_W2"], ACT.Gelu, 2, 2, True)


def gain(engine, order, t, factor, offset, dst):
    row = lambda x: x.unsqueeze(1).to_broadcast([P, t.shape[1], P])
    order.mark(engine.tensor_tensor(t, t, row(factor), ALU.mult))
    order.settle()
    return engine.tensor_tensor(dst, t, row(offset), ALU.add)


def normalise(nc, dst, src, two, rstd, tiles):
    for t in tiles:
        ins = nc.vector.tensor_scalar(dst[:, t, :], src[:, t, :], two[:, t, 0:1], rstd[:, t:t + 1], ALU.subtract, ALU.mult)
    return ins


def stage_self_attention(k):
    nc, w, T = k.nc, k.w, 4
    k.y = k.sb("y_stream", [P, NT, P], F32, k.layer2)
    groups = [slice(j * T, (j + 1) * T) for j in range(NT // T)]
    with ExitStack() as local:
        sb = lambda n, s: k.sb("sa_" + n, s, F32, local)
        xnT = sb("xnT", [P, NT, P])
        norm_and_transpose(k, xnT, k.x)
        t, six, two, rstd = sb("t", [P, NT, P]), sb("six", [P, NT, 6]), sb("two", [P, NT, 2]), sb("rstd", [P, NT])
        stats, rs, n0 = k.norms(NT // T)
        pe_r, t_r = k.sem("sa_pe"), k.sem("sa_t")
        with nc.Block() as block:
            @block.gpsimd
            def _(pool):
                order = Order(k, pool, "pool")
                for j, g in enumerate(groups):
                    pool.wait_ge(stats, n0 + j + 1)
                    rstd_on_pool(k, order, two[:, g, 1], rstd[:, g], T).then_inc(rs, 1)
                for j in (0, 1):
                    pool.wait_ge(t_r, j + 1)
                    order.mark(gain(nc.gpsimd, order, t[:, groups[j], :], w["L2_vecs"][:, 1, :], w["L2_vecs"][:, 2, :], k.y[:, groups[j], :]))
                order.close()

            @block.vector
            def _(v):
                order = Order(k, v, "dve")
                for j, g in enumerate(groups):
                    v.wait_ge(pe_r, j + 1)
                    order.mark(nc.vector.tensor_tensor(t[:, g, :], k.bank[j][:].rearrange("p (t d) -> p t d", t=T), w["sa_bias"][:].unsqueeze(1).to_broadcast([P, T, P]), ALU.add))
                    order.settle()
                    ln_stats(k, order, t[:, g, :], six[:, g, :], two[:, g, :], lambda ins: ins.then_inc(stats, 1))
                for j, g in enumerate(groups):
                    v.wait_ge(rs, n0 + j + 1)
                    ins = normalise(nc, t, t, two, rstd, range(g.start, g.stop))
                    order.mark(ins) if j >= 2 else ins.then_inc(t_r, 1)
                order.settle()
                for j in (2, 3):
                    order.mark(gain(nc.vector, order, t[:, groups[j], :], w["L2_vecs"][:, 1, :], w["L2_vecs"][:, 2, :], k.y[:, groups[j], :]))
                order.close()

            @block.tensor
            def _(pe):
                for t in range(NT):
                    ins = nc.tensor.matmul(k.bank[t // T][:, t % T * P:(t % T + 1) * P], xnT[:, t, :], w["sa"][:], start=True, stop=True)
                    if t % T == T - 1:
                        ins.then_inc(pe_r, 1)


def stage_relu_ffn(k):
    nc, w, T = k.nc, k.w, 4
    GROUPS, N = NT // T, T * P
    groups = [slice(j * T, (j + 1) * T) for j in range(GROUPS)]
    BT, BH, BO = (0, 1), (2, 3, 4), (5, 6)
    vec = lambda n: w["L2_vecs"][:, n, :]
    with ExitStack() as local:
        sb = lambda n, s, c=None: k.sb("rf_" + n, s, F32, local) if c is None else [k.sb(f"rf_{n}{j}", s, F32, local) for j in range(c)]
        t, y2, out = sb("t", [P, NT, P]), sb("y2", [P, NT, P]), sb("out", [P, NT, P])
        six, two, rstd = sb("six", [P, NT, 6]), sb("two", [P, NT, 2]), sb("rstd", [P, NT])
        yT, h = sb("yT", [P, N], 2), sb("h", [P, 4, N], 2)
        stats, rs, n0 = k.norms(1 + GROUPS)
        normed, y_even, y_odd, t_r, yT_ps, yT_r, h_ps, h_r, o_ps, out_r, joined, again = (k.sem("rf_" + n) for n in (
            "normed", "y2_even", "y2_odd", "t", "yT_ps", "yT", "h_ps", "h", "out_ps", "out", "joined", "renormed"))
        with nc.Block() as block:
            @block.gpsimd
            def _(pool):
                order = Order(k, pool, "pool")
                pool.wait_ge(stats, n0 + 1)
                rstd_on_pool(k, order, two[:, :, 1], rstd[:], NT).then_inc(rs, 1)
                for j in (1, 3):
                    pool.wait_ge(normed, j // 2 + 1)
                    gain(nc.gpsimd, order, t[:, groups[j], :], vec(3), vec(4), y2[:, groups[j], :]).then_inc(y_odd, 1)
                for j, g in enumerate(groups):
                    pool.wait_ge(y_even, 2)
                    pool.wait_ge(y_odd, 2)
                    nc.gpsimd.tensor_tensor(t[:, g, :], y2[:, g, :], vec(5).unsqueeze(1).to_broadcast([P, T, P]), ALU.add).then_inc(t_r, 1)
                for j, g in enumerate(groups):
                    pool.wait_ge(stats, n0 + j + 2)
                    rstd_on_pool(k, order, two[:, g, 1], rstd[:, g], T).then_inc(rs, 1)
                    pool.wait_ge(again, j + 1)
                    order.mark(gain(nc.gpsimd, order, out[:, g, :], vec(6), vec(7), t[:, g, :]))
                    order.settle()
                    nc.gpsimd.tensor_tensor(k.x[:, g, :], k.x[:, g, :], t[:, g, :], ALU.add).then_inc(joined, 1)
                order.close()

            @block.vector
            def _(v):
                order = Order(k, v, "dve")
                ln_stats(k, order, k.y, six, two, lambda ins: ins.then_inc(stats, 1))
                v.wait_ge(rs, n0 + 1)
                for j, g in enumerate(groups):
                    ins = normalise(nc, t, k.y, two, rstd, range(g.start, g.stop))
                    if j % 2 == 1:
                        ins.then_inc(normed, 1)
                    else:
                        order.mark(ins)
                        order.settle()
                        gain(nc.vector, order, t[:, g, :], vec(3), vec(4), y2[:, g, :]).then_inc(y_even, 1)
                for j, g in enumerate(groups):
                    v.wait_ge(t_r, j + 1)
                    v.wait_ge(o_ps, j + 1)
                    order.mark(nc.vector.tensor_tensor(t[:, g, :], t[:, g, :], k.bank[BO[j % 2]][:].rearrange("p (t d) -> p t d", t=T), ALU.add))
                    order.settle()
                    v.sem_inc(out_r, 1)
                    ln_stats(k, order, t[:, g, :], six[:, g, :], two[:, g, :], lambda ins: ins.then_inc(stats, 1))
                    v.wait_ge(rs, n0 + j + 2)
                    normalise(nc, out, t, two, rstd, range(g.start, g.stop)).then_inc(again, 1)
                order.close()

            @block.scalar
            def _(act):
                for j in range(GROUPS):
                    act.wait_ge(yT_ps, j + 1)
                    nc.scalar.copy(yT[j % 2][:], k.bank[BT[j % 2]][:]).then_inc(yT_r, 1)
                    for c in range(4):
                        act.wait_ge(h_ps, j * 4 + c + 1)
                        if j >= 2 and c == 0:
                            act.wait_ge(o_ps, j - 1)
                        nc.scalar.activation(h[j % 2][:, c, :], k.bank[BH[(j * 4 + c) % 3]][:], ACT.Relu, bias=w["L2_lin1b"][:, c:c + 1]).then_inc(h_r, 1)

            @block.tensor
            def _(pe):
                mm = nc.tensor.matmul

                def turned(j):
                    pe.wait_ge((y_even, y_odd)[j % 2], j // 2 + 1)
                    if j >= 2:
                        pe.wait_ge(yT_r, j - 1)
                    for s in range(T):
                        ins = nc.tensor.transpose(k.bank[BT[j % 2]][:, s * P:(s + 1) * P], y2[:, j * T + s, :], w["ident"][:])
                    ins.then_inc(yT_ps, 1)

                turned(0)
                for j in range(GROUPS):
                    if j + 1 < GROUPS:
                        turned(j + 1)
                    pe.wait_ge(yT_r, j + 1)
                    for c in range(4):
                        u = j * 4 + c
                        if u >= 3:
                            pe.wait_ge(h_r, u - 2)
                        mm(k.bank[BH[u % 3]][:], w["L2_lin1T"][:, c * P:(c + 1) * P], yT[j % 2][:], start=True, stop=True).then_inc(h_ps, 1)
                    pe.wait_ge(h_r, j * 4 + 4)
                    if j >= 2:
                        pe.wait_ge(out_r, j - 1)
                    for s in range(T):
                        for c in range(4):
                            ins = mm(k.bank[BO[j % 2]][:, s * P:(s + 1) * P], h[j % 2][:, c, s * P:(s + 1) * P], w["L2_lin2T"][:, c, :], start=(c == 0), stop=(c == 3))
                    ins.then_inc(o_ps, 1)


def bf16_parts(value):
    parts, rest = [], np.float32(value)
    for _ in range(3):
        bits = np.array(rest, np.float32).view(np.uint32)
        part = ((bits + np.uint32(0x7FFF) + ((bits >> np.uint32(16)) & np.uint32(1))) & np.uint32(0xFFFF0000)).view(np.float32)
        parts.append(float(part))
        rest = np.float32(rest - part)
    return parts


def stage_cross_attention(k, tag, H, stream, norm, masked):
    nc, w = k.nc, k.w
    D, S = P // H, 4
    R, HL, HB, G = 6 * D, H * L, H // 2, H // 4
    ROWS = R + (6 if masked else 3)
    SLOTS = (0, 0, 0, 1, 1, 2), (0, 1, 2, 0, 1, 0)
    LATE = 1 if H > 8 else 0
    PAD = 96 if ROWS > 96 else 0
    SCALE = float(D) ** -0.5
    stack = nc.dram_tensor(f"{tag}_stack", [B, 2, ROWS * HL], BF16).ap()
    maxima = nc.dram_tensor(f"{tag}_maxima", [B, 2, 6 * HB * P], BF16).ap()
    NB = 3 if 6 * HB <= 32 else P // (2 * HB)
    RING = 3
    NP = 8
    BS, BE, BV, B_MAX, B_OUT = (2, 3), (5, 6), (7, 0), 1, 4
    STEP = H // 4
    tt, ts, cp = nc.vector.tensor_tensor, nc.vector.tensor_scalar, nc.vector.tensor_copy
    with ExitStack() as local:
        sb = lambda n, s, d=F32, c=RING, at=local: [k.sb(f"{tag}_{n}{j}", s, d, at) for j in range(c)]
        all_v, val = k.sb(f"{tag}_all_v", [P, NT, P], F32, local), sb("val", [P, T2, H, 32])
        qs, ks = sb("qs", [P, HL], BF16), sb("ks", [P, HL], BF16)
        sem = lambda n: k.sem(f"{tag}_" + n)
        each = lambda n, c: [sem(f"{n}{j}") for j in range(c)]

        stacked, rows_clear = each("stacked", RING), sem("rows_cleared")

        def load(sp, b):
            for side, dst in ((0, qs), (1, ks)):
                sp.dma_start(dst[b % RING][0:ROWS, :], stack[b:b + 1, side, :].rearrange("b (r c) -> (b r) c", c=HL)).then_inc(stacked[b % RING], 16)

        with ExitStack() as early:
            xnT = k.sb(f"{tag}_xnT", [P, NT, P], ctx=early)
            ctxT, ctx_in = k.sb(f"{tag}_ctxT", [P, B, L], ctx=early), sem("ctx_in")
            norm_and_transpose(k, xnT, stream, norm, (ctxT, ctx_in))
            one = lambda n, s, d=F32: k.sb(f"{tag}_{n}", s, d, early) if masked else None
            mask, mrow, mfloat, mpart = one("mask", [P, B * L]), one("mrow", [B, L], U8), one("mfloat", [B, L]), one("mpart", [B, 3, L], BF16)
            qk, rest = sb("qk", [P, 2 * L], F32, S, early), sb("rest", [P, 2 * L], F32, S, early)
            parts = k.sb(f"{tag}_parts", [P, B, 3, 2 * L], BF16, early)
            part = lambda b, j: parts[:, bass.ds(b, 1), j, :].rearrange("p b c -> p (b c)")
            wrote = sem("wrote")
            part_r = each("part", 3)
            fill, const_r, qk_ps, v_ps, v_r, qk_r, rest_r = (sem(n) for n in ("fill", "const", "qk_ps", "v_ps", "v", "qk", "rest"))
            with nc.Block() as block:
                @block.sync
                def _(sp):
                    sp.dma_start(stack[:, 0, R * HL:ROWS * HL].rearrange("b (r c) -> b r c", c=HL), k.d["stack_fill"][0:1, 0:ROWS - R, 0:HL].to_broadcast([B, ROWS - R, HL])).then_inc(fill, 16)
                    sp.dma_start(stack[:, 1, R * HL:(R + 3) * HL].rearrange("b (r c) -> b r c", c=HL), k.d["stack_fill"][1:2, 0:3, 0:HL].to_broadcast([B, 3, HL])).then_inc(fill, 16)
                    if masked:
                        sp.dma_start(mrow[:], k.d["mask_rows"]).then_inc(fill, 16)
                    with sp.Fori(0, B // S) as i:
                        turn = bass.ds(i * S, S)
                        for n in range(3):
                            sp.wait_ge(part_r[n], (i + 1) * S)
                            for side, of_slot in enumerate(SLOTS):
                                for j in range(6):
                                    if of_slot[j] == n:
                                        sp.dma_start(stack[turn, side, j * P * L:(j + 1) * P * L].rearrange("b (p t) -> p b t", t=L),
                                                     parts[:, turn, n, side * L:(side + 1) * L]).then_inc(wrote, 16)
                    if masked:
                        sp.wait_ge(const_r, 1)
                        for j in range(3):
                            sp.dma_start(stack[:, 1, (R + 3 + j) * HL:(R + 4 + j) * HL].rearrange("b (h t) -> b h t", h=H), mpart[:, j, :].unsqueeze(1).to_broadcast([B, H, L])).then_inc(fill, 16)
                    sp.wait_ge(fill, 16 * (6 if masked else 2))
                    sp.wait_ge(wrote, B // S * 16 * 12)
                    sp.wait_ge(rows_clear, 1)
                    for b in range(RING):
                        load(sp, b)

                @block.gpsimd
                def _(pool):
                    for x in qs + ks:
                        ins = nc.gpsimd.memset(x[PAD:P, :], 0.0)
                    ins.then_inc(rows_clear, 1)
                    for n, x in enumerate(val):
                        pool.wait_ge(rows_clear, n + 1)
                        nc.gpsimd.memset(x[:, :, :, 0:1], 1.0)
                        nc.gpsimd.memset(x[:, :, :, 1:32], 0.0).then_inc(rows_clear, 1)

                @block.scalar
                def _(act):
                    with act.Fori(0, B // S) as i:
                        for s in range(S):
                            act.wait_ge(qk_r, i * S + s + 1)
                            nc.scalar.copy(part(i * S + s, 0), qk[s][:]).then_inc(part_r[0], 1)
                        for s in range(S):
                            act.wait_ge(rest_r, i * S + s + 1)
                            nc.scalar.copy(part(i * S + s, 1), rest[s][:]).then_inc(part_r[1], 1)

                @block.vector
                def _(v):
                    order = Order(k, v, "dve")
                    v.sem_inc(v_r, S)
                    if masked:
                        order.mark(cp(mask[:], w["mask_bytes"][:]))
                        v.wait_ge(fill, 48)
                        order.mark(cp(mfloat[:], mrow[:]))
                        order.settle()
                        order.mark(ts(mfloat[:], mfloat[:], -1.0, 1.0, ALU.mult, ALU.add))
                        order.settle()
                        for j, c in enumerate(bf16_parts(-1e4 * np.sqrt(np.float32(D)))):
                            ins = ts(mpart[:, j, :], mfloat[:], c, None, ALU.mult)
                        ins.then_inc(const_r, 1)
                    order.close()
                    tt(stream[:], stream[:], w[f"{tag}_bo"][:].unsqueeze(1).to_broadcast([P, NT, P]), ALU.add)
                    with v.Fori(0, B // S) as i:
                        for s in range(S):
                            v.wait_ge(qk_ps, i * S + s + 1)
                            ts(qk[s][:, 0:L], k.bank[s][:, 0:L], w[f"{tag}_bq"][:, 0:1], None, ALU.add)
                            if masked:
                                nc.vector.scalar_tensor_tensor(qk[s][:, L:2 * L], k.bank[s][:, L:2 * L], w[f"{tag}_bk"][:, 0:1], mask[:, bass.ds((i * S + s) * L, L)], ALU.add, ALU.mult).then_inc(qk_r, 1)
                            else:
                                ts(qk[s][:, L:2 * L], k.bank[s][:, L:2 * L], w[f"{tag}_bk"][:, 0:1], None, ALU.add).then_inc(qk_r, 1)
                        for s in range(S):
                            v.wait_ge(v_ps, i * S + s + 1)
                            ins = tt(all_v[:, bass.ds((i * S + s) * T2, T2), :], k.bank[4 + s][:, 0:L].rearrange("p (t d) -> p t d", t=T2),
                                     w[f"{tag}_bv"][:].unsqueeze(1).to_broadcast([P, T2, P]), ALU.add)
                            ins.then_inc(v_r, 1)
                        for s in range(S):
                            v.wait_ge(part_r[0], i * S + s + 1)
                            tt(rest[s][:], qk[s][:], part(i * S + s, 0), ALU.subtract).then_inc(rest_r, 1)
                        for s in range(S):
                            v.wait_ge(part_r[1], i * S + s + 1)
                            tt(part(i * S + s, 2), rest[s][:], part(i * S + s, 1), ALU.subtract).then_inc(part_r[2], 1)

                @block.tensor
                def _(pe):
                    pe.wait_ge(ctx_in, 16)
                    for i in range(B // S):
                        for s in range(S):
                            b = i * S + s
                            pe.wait_ge(v_r, b + 1)
                            nc.tensor.matmul(k.bank[s][:, 0:L], w[f"{tag}_wq"][:], flat(xnT[:, b * T2:(b + 1) * T2, :]), start=True, stop=True)
                            nc.tensor.matmul(k.bank[s][:, L:2 * L], w[f"{tag}_wk"][:], ctxT[:, b, :], start=True, stop=True).then_inc(qk_ps, 1)
                        for s in range(S):
                            for j in range(T2):
                                ins = nc.tensor.matmul(k.bank[4 + s][:, j * P:(j + 1) * P], ctxT[:, i * S + s, j * P:(j + 1) * P], w[f"{tag}_wv"][:], start=True, stop=True)
                            ins.then_inc(v_ps, 1)

        nmax, nrest, nparts = sb("nmax", [P, 2 * H]), sb("nrest", [P, 2 * HB]), sb("nparts", [P, NB, 2 * HB], BF16)
        nT = [sb(f"nT_{half}", [6 * HB, P], BF16) for half in "ab"]
        prob = sb("prob", [P, 2, L], c=NP)
        out32, rden, o, oT = sb("out32", [P, G, L]), sb("rden", [P, H], c=1)[0], sb("o", [P, T2, P], c=1)[0], sb("oT", [P, L], c=1)[0]
        nwrote = each("nwrote", RING)
        nrow = [each("nrow_a", RING), each("nrow_b", RING)]
        s_ps, mx_r, np_r, nt_ps, nt_r, e_ps, ex_r, pv_ps, o_ev = (sem(n) for n in (
            "s_ps", "max", "nparts", "nT_ps", "nT", "e_ps", "exp", "pv_ps", "out32"))
        out_ps, o_r, oT_r, done, val_r = sem("out_ps"), sem("o"), sem("oT"), sem("done"), sem("val")
        OUT = 4
        slot_steps = [j * STEP + 1 for j in range(OUT)]

        def number(i, c):
            return i * RING + c

        def have(eng, semaphore, value):
            if not isinstance(value, int) or value > 0:
                eng.wait_ge(semaphore, value)

        def new_parts(v, order, b, c, half):
            c, src = c % RING, nmax[c % RING][:, half * 2 * HB:(half + 1) * 2 * HB]
            v.wait_ge(mx_r, b * H + (half + 1) * HB)
            order.mark(cp(nparts[c][:, 0, :], src))
            order.settle()
            order.mark(tt(nrest[c][:], src, nparts[c][:, 0, :], ALU.subtract))
            order.settle()
            order.mark(cp(nparts[c][:, 1, :], nrest[c][:]))
            order.settle()
            tt(nparts[c][:, 2, :], nrest[c][:], nparts[c][:, 1, :], ALU.subtract).then_inc(np_r, 1)

        def maxima_rows(v, b, c, half):
            v.wait_ge(nt_ps, b * 2 + half + 1)
            cp(nT[half][c % RING][:], k.bank[B_MAX][:].bitcast(BF16)[0:6 * HB, 0:P]).then_inc(nt_r, 1)

        def divide(v, order, b, j):
            v.wait_ge(out_ps, b * OUT + j + 1)
            heads = k.bank[B_OUT][:, 0:G * P].rearrange("p (h c) -> p h c", c=32)
            order.mark(nc.vector.reciprocal(rden[:], heads[:, :, 0]))
            order.settle()
            tt(o[:, j, :].rearrange("p (h d) -> p h d", h=H), heads[:, :, 1:1 + D], rden[:].unsqueeze(2).to_broadcast([P, H, D]), ALU.mult).then_inc(o_r, 1)

        def vector_slot(v, order, i, s, e, out):
            for h in range(H):
                if e is not None and h == LATE:
                    maxima_rows(v, number(i, e), e, 1)
                if s is not None:
                    b = number(i, s)
                    v.wait_ge(s_ps, b * H + h + 1)
                    nc.vector.tensor_reduce(nmax[s % RING][:, 2 * h:2 * h + 2], k.bank[BS[h % 2]][:].rearrange("p (t l) -> p t l", t=2), AX.X, ALU.max, negate=True).then_inc(mx_r, 1)
                    if h == HB - 1:
                        new_parts(v, order, b, s, 0)
                    if h == HB + 1:
                        maxima_rows(v, b, s, 0)
                if out is not None:
                    b = number(i, out)
                    if h == slot_steps[0]:
                        divide(v, order, b, 0)
                    if h == slot_steps[1]:
                        v.wait_ge(o_r, b * 2 + 1)
                        divide(v, order, b, 1)
                    if h == slot_steps[3]:
                        v.wait_ge(out_ps, b * OUT + 4)
                        xs = stream[:, bass.ds(b * T2, T2), :]
                        tt(xs, xs, k.bank[B_OUT][:, L:2 * L].rearrange("p (t d) -> p t d", t=T2), ALU.add).then_inc(done, 1)
            if s is not None:
                new_parts(v, order, number(i, s), s, 1)

        def gather(act, b, c, g):
            act.wait_ge(pv_ps, b * G + g + 1)
            nc.scalar.copy(out32[c % RING][:, g, :], k.bank[BV[g % 2]][:, 0:L]).then_inc(o_ev, 1)

        def scalar_slot(act, i, e, out):
            for h in range(H):
                if e is not None:
                    b = number(i, e)
                    act.wait_ge(e_ps, b * H + h + 1)
                    if h % 4 == 0:
                        have(act, pv_ps, b * G + h // 4 + 1 - NP // 4)
                    nc.scalar.activation(flat(prob[h % NP][:]), k.bank[BE[h % 2]][:], ACT.Exp, scale=SCALE).then_inc(ex_r, 1)
                    if h % 4 == 2 and h > 4:
                        gather(act, b, e, h // 4 - 1)
                if out is not None and h == 0:
                    gather(act, number(i, out), out, G - 1)
                if out is not None and h == slot_steps[2]:
                    act.wait_ge(out_ps, number(i, out) * OUT + 3)
                    nc.scalar.copy(oT[:], k.bank[B_OUT][:, 0:L]).then_inc(oT_r, 1)

        def values(pe, b, c, g):
            pe.wait_ge(ex_r, b * H + 4 * g + 4)
            have(pe, o_ev, b * G + g - 1)
            for t in range(T2):
                for h in range(4 * g, 4 * g + 4):
                    r = 32 * (h % 4)
                    ins = nc.tensor.matmul(k.bank[BV[g % 2]][r:r + 32, 0:L], val[c % RING][:, t, h, :], prob[h % NP][:, t, :], start=(t == 0), stop=(t == T2 - 1), tile_position=(0, r))
            ins.then_inc(pv_ps, 1)

        def tensor_slot(pe, i, s, e, out):
            mm = nc.tensor.matmul
            for h in range(H):
                if e is not None and h == LATE:
                    turn_maxima(pe, number(i, e), e, 1)
                if s is not None:
                    b, q, kk = number(i, s), qs[s % RING], ks[s % RING]
                    if h == 0:
                        pe.wait_ge(stacked[s % RING], (i + s // RING) * 32 + 32)
                    have(pe, mx_r, b * H + h + 1 - len(BS))
                    for j in range(2):
                        ins = mm(k.bank[BS[h % 2]][:, j * L:(j + 1) * L], q[:, h * L + j * P:h * L + (j + 1) * P], kk[:, h * L:(h + 1) * L], start=True, stop=True)
                    ins.then_inc(s_ps, 1)
                    if h == HB + 1:
                        turn_maxima(pe, b, s, 0)
                if e is not None:
                    b, q, kk = number(i, e), qs[e % RING], ks[e % RING]
                    if h % HB == 0:
                        pe.wait_ge(nrow[h // HB][e % RING], (i + e // RING) * 16 + 16)
                    have(pe, ex_r, b * H + h + 1 - len(BE))
                    for j in range(2):
                        ins = mm(k.bank[BE[h % 2]][:, j * L:(j + 1) * L], kk[:, h * L + j * P:h * L + (j + 1) * P], q[:, h * L:(h + 1) * L], start=True, stop=True)
                    ins.then_inc(e_ps, 1)
                    if h == 0:
                        pe.wait_ge(val_r, b + 1)
                    if h % 4 == 1 and h > 4:
                        values(pe, b, e, h // 4 - 1)
                if out is not None and h in slot_steps:
                    output_step(pe, number(i, out), out, slot_steps.index(h))
            if e is not None:
                values(pe, number(i, e), e, G - 1)

        def turn_maxima(pe, b, c, half):
            pe.wait_ge(np_r, b * 2 + half + 1)
            have(pe, nt_r, b * 2 + half)
            nc.tensor.transpose(k.bank[B_MAX][:].bitcast(BF16)[0:2 * NB * HB, 0:P], flat(nparts[c % RING][:]), w["ident_bf"][:]).then_inc(nt_ps, 1)

        def output_step(pe, b, c, step):
            bank = k.bank[B_OUT]
            if step < T2:
                if step == 0:
                    pe.wait_ge(o_ev, (b + 1) * G)
                    pe.wait_ge(done, b + 1)
                else:
                    pe.wait_ge(o_r, b * T2 + 1)
                for g in range(G):
                    ins = nc.tensor.transpose(bank[:, g * P:(g + 1) * P], out32[c % RING][:, g, step * P:(step + 1) * P], w["ident"][:])
            elif step == 2:
                pe.wait_ge(o_r, b * T2 + 2)
                for j in range(T2):
                    ins = nc.tensor.transpose(bank[:, j * P:(j + 1) * P], o[:, j, :], w["ident"][:])
            else:
                pe.wait_ge(oT_r, b + 1)
                for j in range(T2):
                    ins = nc.tensor.matmul(bank[:, L + j * P:L + (j + 1) * P], oT[:, j * P:(j + 1) * P], w[f"{tag}_wo"][:], start=True, stop=True)
            ins.then_inc(out_ps, 1)

        def pool_slot(pool, i, c):
            b = number(i, c)
            if c >= 2:
                pool.wait_ge(pv_ps, (b - 2) * G + 1)
            nc.gpsimd.tensor_copy(val[c % RING][:, :, :, 1:1 + D], all_v[:, bass.ds(b * T2, T2), :].rearrange("p t (h d) -> p t h d", h=H)).then_inc(val_r, 1)

        TURNS = (B - 2) // RING

        with nc.Block() as block:
            @block.sync
            def _(sp):
                for b in range(B):
                    ring = b % RING
                    for half in range(2):
                        mx = maxima[b:b + 1, half, :]
                        sp.wait_ge(nt_r, b * 2 + half + 1)
                        sp.dma_start(mx.rearrange("b (c q) -> (b c) q", q=P), nT[half][ring][:]).then_inc(nwrote[ring], 16)
                        sp.wait_ge(nwrote[ring], (b // RING * 2 + half + 1) * 16)
                        sp.dma_start(qs[ring][R:R + 3, half * HB * L:(half + 1) * HB * L], mx.rearrange("b (r c) -> (b r) c", r=3)).then_inc(nrow[half][ring], 16)
                    if 1 <= b and b + 2 < B:
                        sp.wait_ge(e_ps, b * H)
                        load(sp, b + 2)

            @block.gpsimd
            def _(pool):
                pool_slot(pool, 0, 0)
                pool_slot(pool, 0, 1)
                with pool.Fori(0, TURNS) as i:
                    for c in range(2, 2 + RING):
                        pool_slot(pool, i, c)

            @block.vector
            def _(v):
                order = Order(k, v, "dve")
                for c in range(RING):
                    ins = nc.vector.memset(nparts[c][:], 0.0)
                order.mark(ins)
                v.sem_inc(done, 1)
                vector_slot(v, order, 0, 0, None, None)
                vector_slot(v, order, 0, 1, 0, None)
                order.close()
                with v.Fori(0, TURNS) as i:
                    order = Order(k, v, "dve", i, TURNS, 8 * RING)
                    for c in range(2, 2 + RING):
                        vector_slot(v, order, i, c, c - 1, c - 2)
                    order.close()
                order = Order(k, v, "dve")
                vector_slot(v, order, 0, None, B - 1, B - 2)
                vector_slot(v, order, 0, None, None, B - 1)
                order.close()

            @block.scalar
            def _(act):
                scalar_slot(act, 0, 0, None)
                with act.Fori(0, TURNS) as i:
                    for c in range(2, 2 + RING):
                        scalar_slot(act, i, c - 1, c - 2)
                scalar_slot(act, 0, B - 1, B - 2)
                scalar_slot(act, 0, None, B - 1)

            @block.tensor
            def _(pe):
                tensor_slot(pe, 0, 0, None, None)
                tensor_slot(pe, 0, 1, 0, None)
                with pe.Fori(0, TURNS) as i:
                    for c in range(2, 2 + RING):
                        tensor_slot(pe, i, c, c - 1, c - 2)
                tensor_slot(pe, 0, None, B - 1, B - 2)
                tensor_slot(pe, 0, None, None, B - 1)


def stage_attention_8(k):
    stage_cross_attention(k, "L2", 8, k.y, False, False)


def stage_attention_16(k):
    stage_cross_attention(k, "L3", 16, k.x, True, True)


def stage_store(k):
    stored = k.sem("stored")
    with k.nc.Block() as block:
        @block.sync
        def _(sp):
            sp.dma_start(k.out.rearrange("b (t p) d -> p (b t) d", p=P), k.x[:]).then_inc(stored, 16)
            sp.wait_ge(stored, 16)


LAYERS = [("layer0", [stage_autocorrelation, stage_ternary_ffn]),
          ("layer1", [stage_later_is_here, stage_causal_attention, stage_experts_gelu, stage_load_last]),
          ("layer2", [stage_self_attention, stage_attention_8, stage_relu_ffn]),
          ("rest", [stage_fourier, stage_attention_16, stage_experts_shared])]


def host_layout(a):
    bf16 = mybir.dt.np(BF16)

    f = np.float32
    t = {}
    rows = lambda v: np.ascontiguousarray(np.broadcast_to(v, (P,) + v.shape))
    cols = lambda v, n: np.ascontiguousarray(v.reshape(n, P).T)
    t["x"] = a["x"]
    t["ctx"] = a["ctx_1024"]
    t["ctxT"] = np.ascontiguousarray(a["ctx_1024"].transpose(0, 2, 1))
    t["ternary"] = np.ascontiguousarray(np.stack([
        a["L0_ffn_w_gate"].T, a["L0_ffn_w_up"].T,
        a["L0_ffn_w_down"].T.reshape(4, P, P).transpose(1, 0, 2).reshape(P, 512)], 1))
    t["mask_bytes"] = a["mask_BxS2_bf1"].view(np.uint8).reshape(B * L)
    t["mask_rows"] = a["mask_BxS2_bf1"].view(np.uint8)
    t["lens"] = a["_lenS2"]
    t["ident"] = np.eye(P, dtype=f)
    t["ident_bf"] = np.eye(P, dtype=bf16)
    tok, fr = np.arange(L)[:, None], np.arange(P)[None, :]
    cosine, sine = np.cos(2 * np.pi * tok * fr / L), np.sin(2 * np.pi * tok * fr / L)
    nyq = (-1.0) ** np.arange(L)
    second = sine.copy()
    second[:, 0] = nyq
    t["dft"] = np.ascontiguousarray(np.concatenate([cosine, second], 1).reshape(T2, P, L).transpose(1, 0, 2)).astype(f)
    first_i, second_i = 2 * cosine.T / L, -2 * sine.T / L
    first_i[0] = 1.0 / L
    second_i[0] = nyq / L
    t["idft"] = np.ascontiguousarray(np.stack([first_i, second_i], 1)).astype(f)
    ch = np.arange(P)
    t["head_block"] = (ch[:, None] // 8 == ch[None, :] // 8).astype(f)
    out_row = 2 * (ch % 8 * 16 + ch // 8)
    spread = np.zeros((P, T2, 2, P), f)
    for half in range(2):
        spread[ch, (out_row + half) // P, half, (out_row + half) % P] = 1
    t["spread_rows"] = spread.reshape(P, 4 * P)
    t["iota8"] = rows(np.arange(8, dtype=f))
    t["rolled_base"] = (ch % 8 + L).astype(f)[:, None]
    t["not_first"] = (ch > 0).astype(f)[:, None]
    ang = 2 * np.pi * (ch[:, None] * ch[None, :] % P) / P
    t["fourier_cos"], t["fourier_sin"], t["fourier_nsin"] = np.cos(ang).astype(f), np.sin(ang).astype(f), (-np.sin(ang)).astype(f)
    kk = np.concatenate([np.arange(P), np.arange(L)])
    qq = np.concatenate([np.zeros(P), np.full(L, P)])
    t["iota_k"] = rows(kk.astype(f))
    t["causal"] = np.where(kk[None] <= qq[None] + ch[:, None], 0, NEG).astype(f)
    t["head_pick"] = np.stack([ch < 64, ch >= 64], 1).astype(f)
    t["prefix"] = rows((np.arange(8)[None, :] < np.arange(8)[:, None]).astype(f))
    for n in ("wq", "wk", "wv", "wo"):
        t["q0_" + n] = a["L0_xattn_" + n]
    for n in ("Q", "K", "V"):
        t["L1_W" + n] = np.ascontiguousarray(a["L1_xattn_W" + n].transpose(1, 0, 2).reshape(P, 1024))
        t["L1_b" + n] = cols(a["L1_xattn_b" + n], 8)
    t["L1_WO"] = np.ascontiguousarray(a["L1_xattn_WO"].reshape(8, P, P).transpose(1, 0, 2))
    t["L1_bO"] = rows(a["L1_xattn_bO"])
    t["L1_router"] = a["L1_ffn_router_w"]
    t["L1_up_w"] = np.ascontiguousarray(a["L1_ffn_up_w"].transpose(1, 0, 2))
    t["L1_down_w"] = np.ascontiguousarray(a["L1_ffn_down_w"].reshape(8, 4, P, P).transpose(2, 0, 1, 3).reshape(P, 8, 512))
    t["L2_ffn_w_freq_real"], t["L2_ffn_w_freq_imag"] = a["L2_ffn_w_freq_real"], a["L2_ffn_w_freq_imag"]
    t["L2_bias"] = rows(a["L2_ffn_bias"])
    t["L2_saT"] = np.ascontiguousarray(a["L2_xattn_sa_out_w"].T)
    t["L2_sa_v"] = np.ascontiguousarray(a["L2_xattn_qkv_w"][2 * P:])
    t["L2_sa_vb"] = np.ascontiguousarray(np.broadcast_to(a["L2_xattn_qkv_b"][2 * P:, None], (P, P)))
    t["L2_vecs"] = rows(np.stack([a["L2_xattn_" + n] for n in ("sa_out_b", "ln1_g", "ln1_b", "ln2_g", "ln2_b", "lin2_b", "ln3_g", "ln3_b")]))
    t["L2_lin1T"] = np.ascontiguousarray(a["L2_xattn_lin1_w"].T)
    t["L2_lin1b"] = cols(a["L2_xattn_lin1_b"], 4)
    t["L2_lin2T"] = np.ascontiguousarray(a["L2_xattn_lin2_w"].T.reshape(4, P, P).transpose(1, 0, 2))
    for name, heads, ws, bs, wo, bo in (
            ("L2", 8, np.split(a["L2_xattn_in_proj_w"], 3), np.split(a["L2_xattn_in_proj_b"], 3), a["L2_xattn_mha_out_w"], a["L2_xattn_mha_out_b"]),
            ("L3", 16, [a["L3_xattn_W" + n] for n in "qkv"], [a["L3_xattn_b" + n] for n in "qkv"], a["L3_xattn_Wo"], a["L3_xattn_bo"])):
        by_dim = np.arange(P).reshape(heads, P // heads).T.reshape(P)
        t[name + "_wq"], t[name + "_wk"] = (np.ascontiguousarray(m.T[:, by_dim]) for m in ws[:2])
        t[name + "_bq"], t[name + "_bk"] = (np.ascontiguousarray(v[by_dim][:, None]) for v in bs[:2])
        t[name + "_wv"], t[name + "_bv"] = np.ascontiguousarray(ws[2].T), rows(bs[2])
        t[name + "_wo"], t[name + "_bo"] = np.ascontiguousarray(wo.T), rows(bo)
    t["stack_fill"] = np.stack([np.concatenate([np.zeros((3, 4096)), np.ones((3, 4096))]), np.concatenate([np.ones((3, 4096)), np.zeros((3, 4096))])]).astype(bf16)
    t["L3_centroids"] = a["L3_ffn_centroids"]
    t["L3_g"] = np.stack([a["L3_ffn_g_shared"], a["L3_ffn_g_routed"]], 1)
    both = lambda n: np.concatenate([a[f"L3_ffn_{n}_r"], a[f"L3_ffn_{n}_s"]])
    t["L3_W1"] = np.ascontiguousarray(both("W1").transpose(1, 0, 2))
    t["L3_W2"] = np.ascontiguousarray(both("W2").reshape(10, 4, P, P).transpose(2, 0, 1, 3).reshape(P, 10, 512))
    t["L3_b1"] = cols(both("b1").reshape(40, P), 40)
    t["L3_b2"] = both("b2")
    return t


def program(nc, dram, out, only=None):
    with ExitStack() as ctx:
        k = Kit(nc, ctx, dram, out)
        stage_setup(k)
        for name, stages in LAYERS:
            made = len(k.sems)
            for stage in stages:
                if only is None or stage in only or stage is stage_later_is_here:
                    stage(k)
            if name == "layer2":
                k.retire_semaphores(made)
            memory = {"layer0": k.layer0, "layer1": k.layer1, "layer2": k.layer2, "rest": k.rest}[name]
            memory.close()
        stage_store(k)


def kernel(**inputs):
    from concourse import bacc
    from concourse.bass_utils import run_bass_kernel_spmd

    arrays = host_layout(inputs)
    nc = bacc.Bacc("TRN2", target_bir_lowering=False, num_devices=1)
    dram = {n: nc.dram_tensor("in_" + n, v.shape, mybir.dt.from_np(v.dtype), kind="ExternalInput").ap() for n, v in arrays.items()}
    out = nc.dram_tensor("out", (B, L, P), F32, kind="ExternalOutput").ap()
    program(nc, dram, out)
    r = run_bass_kernel_spmd(nc, [{"in_" + n: v for n, v in arrays.items()}], core_ids=[0])
    return r.results[0]["out"]
```
